# Optimizing a Trainium2 kernel written in Bass

```python
import numpy as np
import jax
import jax.numpy as jnp

def _softmax(x, axis=-1):
    return jax.nn.softmax(x, axis=axis)

def _gelu(x):
    return jax.nn.gelu(x, approximate=True)

def _silu(x):
    return jax.nn.silu(x)

def _sigmoid(x):
    return jax.nn.sigmoid(x)

def _layernorm(x, axis=-1, eps=1e-05):
    m = jnp.mean(x, axis=axis, keepdims=True)
    v = jnp.var(x, axis=axis, keepdims=True)
    return (x - m) / jnp.sqrt(v + eps)

def _scatter_add(tgt, idx, src, axis=0):
    return tgt.at[idx].add(src)

def _segment_sum(src, seg, n):
    return jax.ops.segment_sum(src, seg, n)
kernel_name = 'mk_perceiver_d1_seqx_r8_b82730'

def setup_inputs(seed: int=0):
    np.random.seed(seed)
    _w = jnp.asarray

    def _rec_inputs():
        import jax
        import jax.numpy as jnp
        _rk = jax.random.key(seed)
        x = 7.22e-05 + 1 * jax.random.normal(jax.random.fold_in(_rk, 1), (32, 64, 256), jnp.float32)
        _lenS = 64 - jax.random.randint(jax.random.fold_in(_rk, 7), (32,), 0, max(1, 64 // 4) + 1, jnp.int32)
        _lenS2 = 1601 - jax.random.randint(jax.random.fold_in(_rk, 8), (32,), 0, max(1, 1601 // 4) + 1, jnp.int32)
        _ctx_512P = jax.random.normal(jax.random.fold_in(_rk, 11), (32, 16, 64), jnp.float32)
        _ctx_512c = jax.random.dirichlet(jax.random.fold_in(_rk, 511), 0.3 * jnp.ones((16,), jnp.float32), (32, 1601))
        _ctx_512t = jnp.einsum('bsk,bkd->bsd', _ctx_512c, _ctx_512P)
        _ctx_512t = _ctx_512t * jax.lax.rsqrt(jnp.mean(jnp.square(_ctx_512t)) + 1e-12) * 0.953939
        ctx_512 = -0.000514642 + 1.00011 * (_ctx_512t + 0.3 * jax.random.normal(jax.random.fold_in(_rk, 611), (32, 1601, 64), jnp.float32))
        return (x, ctx_512)
    x, ctx_512 = _rec_inputs()

    def _L0_xattn_setup():
        import jax, jax.numpy as jnp
        import numpy as np
        B, S, H, NH, L = (2, 256, 256, 16, 64)
        HD = H // NH
        key = jax.random.key(seed)
        k1, k2, k3, k4, k5 = jax.random.split(key, 5)
        scale = 0.02
        return {'q': jax.random.normal(k1, (B, S, H), dtype=jnp.float32), 'latent_kv': jax.random.normal(k2, (B, S, L), dtype=jnp.float32), 'Wq': jax.random.normal(k3, (H, H), dtype=jnp.float32) * scale, 'Wkv_expand': jax.random.normal(k4, (2 * H, L), dtype=jnp.float32) * scale, 'Wout': jax.random.normal(k5, (H, H), dtype=jnp.float32) * scale}
    _L0_xattn_all = _L0_xattn_setup()
    _L0_xattn_in = {k: v for k, v in _L0_xattn_all.items() if k in ('Wq', 'Wkv_expand', 'Wout')}
    del _L0_xattn_all

    def _L0_attn_setup():
        import jax, jax.numpy as jnp
        import numpy as np
        EPS = 1e-05

        def rmsnorm(x, g):
            var = jnp.mean(x * x, axis=-1, keepdims=True)
            return x * jax.lax.rsqrt(var + EPS) * g

        def activation_quant(x):
            s = 127.0 / jnp.clip(jnp.max(jnp.abs(x), axis=-1, keepdims=True), 1e-05)
            return jnp.clip(jnp.round(x * s), -128.0, 127.0) / s

        def weight_quant(w):
            s = 1.0 / jnp.clip(jnp.mean(jnp.abs(w)), 1e-05)
            return jnp.clip(jnp.round(w * s), -1.0, 1.0) / s

        def bitlinear(x, w, g):
            xn = rmsnorm(x, g)
            xq = xn + jax.lax.stop_gradient(activation_quant(xn) - xn)
            wq = w + jax.lax.stop_gradient(weight_quant(w) - w)
            return jnp.einsum('bsh,oh->bso', xq, wq)
        key = jax.random.key(seed)
        k1, k2, k3, k4, k5 = jax.random.split(key, 5)
        H, I = (256, 1024)
        B, S = (2, 256)
        return {'x': jax.random.normal(k1, (B, S, H), dtype=jnp.float32), 'w_gate': jax.random.normal(k2, (2 * I, H), dtype=jnp.float32) * 0.02, 'g_gate': jax.random.uniform(k3, (H,), dtype=jnp.float32, minval=0.5, maxval=1.5), 'w_down': jax.random.normal(k4, (H, I), dtype=jnp.float32) * 0.02, 'g_down': jax.random.uniform(k5, (I,), dtype=jnp.float32, minval=0.5, maxval=1.5)}
    _L0_attn_all = _L0_attn_setup()
    _L0_attn_in = {k: v for k, v in _L0_attn_all.items() if k in ('w_gate', 'g_gate', 'w_down', 'g_down')}
    del _L0_attn_all

    def _L0_ffn_setup():
        import jax, jax.numpy as jnp
        import numpy as np
        B, S, D = (2, 256, 256)
        MOE_D = 176
        E = 16
        K = 6
        ALPHA = 0.001

        def _moe_forward(x, gate_w, w_gate, w_up, w_down):
            b, s, d = x.shape
            T = b * s
            h = x.reshape(T, d)
            logits = h @ gate_w.T
            scores = jax.nn.softmax(logits.astype(jnp.float32), axis=-1)
            topk_w, topk_idx = jax.lax.top_k(scores, K)
            cw = jnp.zeros((T, E), jnp.float32)
            cw = cw.at[jnp.arange(T)[:, None], topk_idx].add(topk_w)
            y = jnp.zeros((T, d), x.dtype)
            for e in range(E):
                g = h @ w_gate[e].T
                u = h @ w_up[e].T
                out = jax.nn.silu(g) * u @ w_down[e].T
                y = y + cw[:, e:e + 1].astype(x.dtype) * out
            counts = jnp.sum(jax.nn.one_hot(topk_idx.reshape(b, s * K), E, dtype=jnp.float32), axis=1)
            ce = counts * (E / (s * K))
            scores_bse = scores.reshape(b, s, E)
            aux = jnp.mean(jnp.sum(ce * scores_bse.mean(axis=1), axis=1)) * ALPHA
            return (y.reshape(b, s, d), aux)
        key = jax.random.key(seed)
        ks = jax.random.split(key, 5)
        sd = 1.0 / np.sqrt(D)
        sm = 1.0 / np.sqrt(MOE_D)
        return {'x': jax.random.normal(ks[0], (B, S, D), jnp.float32), 'gate_w': jax.random.normal(ks[1], (E, D), jnp.float32) * sd, 'w_gate': jax.random.normal(ks[2], (E, MOE_D, D), jnp.float32) * sd, 'w_up': jax.random.normal(ks[3], (E, MOE_D, D), jnp.float32) * sd, 'w_down': jax.random.normal(ks[4], (E, D, MOE_D), jnp.float32) * sm}
    _L0_ffn_all = _L0_ffn_setup()
    _L0_ffn_in = {k: v for k, v in _L0_ffn_all.items() if k in ('gate_w', 'w_gate', 'w_up', 'w_down')}
    del _L0_ffn_all
    return {'x': x, 'ctx_512': ctx_512, 'L0_xattn_Wq': _L0_xattn_in['Wq'], 'L0_xattn_Wkv_expand': _L0_xattn_in['Wkv_expand'], 'L0_xattn_Wout': _L0_xattn_in['Wout'], 'L0_attn_w_gate': _L0_attn_in['w_gate'], 'L0_attn_g_gate': _L0_attn_in['g_gate'], 'L0_attn_w_down': _L0_attn_in['w_down'], 'L0_attn_g_down': _L0_attn_in['g_down'], 'L0_ffn_gate_w': _L0_ffn_in['gate_w'], 'L0_ffn_w_gate': _L0_ffn_in['w_gate'], 'L0_ffn_w_up': _L0_ffn_in['w_up'], 'L0_ffn_w_down': _L0_ffn_in['w_down']}

def reference(x, ctx_512, L0_xattn_Wq, L0_xattn_Wkv_expand, L0_xattn_Wout, L0_attn_w_gate, L0_attn_g_gate, L0_attn_w_down, L0_attn_g_down, L0_ffn_gate_w, L0_ffn_w_gate, L0_ffn_w_up, L0_ffn_w_down):
    import jax
    import jax.numpy as jnp

    def _L0_xattn_ref(q, latent_kv, Wq, Wkv_expand, Wout):
        import jax, jax.numpy as jnp
        import numpy as np
        B, S, H, NH, L = (2, 256, 256, 16, 64)
        HD = H // NH
        b, sq, _ = q.shape
        sk = latent_kv.shape[1]
        qp = q @ Wq.T
        kv = latent_kv @ Wkv_expand.T
        k, v = jnp.split(kv, 2, axis=-1)
        qh = qp.reshape(b, sq, NH, HD).transpose(0, 2, 1, 3)
        kh = k.reshape(b, sk, NH, HD).transpose(0, 2, 1, 3)
        vh = v.reshape(b, sk, NH, HD).transpose(0, 2, 1, 3)
        inv_sqrt_d = 1.0 / jnp.sqrt(jnp.float32(HD))
        scores = jnp.einsum('bhqd,bhkd->bhqk', qh, kh) * inv_sqrt_d
        causal = jnp.tril(jnp.ones((sq, sk), dtype=bool))
        scores = jnp.where(causal, scores, jnp.finfo(scores.dtype).min)
        attn = jax.nn.softmax(scores, axis=-1)
        out = jnp.einsum('bhqk,bhkd->bhqd', attn, vh)
        out = out.transpose(0, 2, 1, 3).reshape(b, sq, H)
        return out @ Wout.T

    def _L0_attn_ref(x, w_gate, g_gate, w_down, g_down):
        import jax, jax.numpy as jnp
        import numpy as np
        EPS = 1e-05

        def rmsnorm(x, g):
            var = jnp.mean(x * x, axis=-1, keepdims=True)
            return x * jax.lax.rsqrt(var + EPS) * g

        def activation_quant(x):
            s = 127.0 / jnp.clip(jnp.max(jnp.abs(x), axis=-1, keepdims=True), 1e-05)
            return jnp.clip(jnp.round(x * s), -128.0, 127.0) / s

        def weight_quant(w):
            s = 1.0 / jnp.clip(jnp.mean(jnp.abs(w)), 1e-05)
            return jnp.clip(jnp.round(w * s), -1.0, 1.0) / s

        def bitlinear(x, w, g):
            xn = rmsnorm(x, g)
            xq = xn + jax.lax.stop_gradient(activation_quant(xn) - xn)
            wq = w + jax.lax.stop_gradient(weight_quant(w) - w)
            return jnp.einsum('bsh,oh->bso', xq, wq)
        y = bitlinear(x, w_gate, g_gate)
        gate, v = jnp.split(y, 2, axis=-1)
        h = jax.nn.silu(gate) * v
        return bitlinear(h, w_down, g_down)

    def _L0_ffn_ref(x, gate_w, w_gate, w_up, w_down):
        import jax, jax.numpy as jnp
        import numpy as np
        B, S, D = (2, 256, 256)
        MOE_D = 176
        E = 16
        K = 6
        ALPHA = 0.001

        def _moe_forward(x, gate_w, w_gate, w_up, w_down):
            b, s, d = x.shape
            T = b * s
            h = x.reshape(T, d)
            logits = h @ gate_w.T
            scores = jax.nn.softmax(logits.astype(jnp.float32), axis=-1)
            topk_w, topk_idx = jax.lax.top_k(scores, K)
            cw = jnp.zeros((T, E), jnp.float32)
            cw = cw.at[jnp.arange(T)[:, None], topk_idx].add(topk_w)
            y = jnp.zeros((T, d), x.dtype)
            for e in range(E):
                g = h @ w_gate[e].T
                u = h @ w_up[e].T
                out = jax.nn.silu(g) * u @ w_down[e].T
                y = y + cw[:, e:e + 1].astype(x.dtype) * out
            counts = jnp.sum(jax.nn.one_hot(topk_idx.reshape(b, s * K), E, dtype=jnp.float32), axis=1)
            ce = counts * (E / (s * K))
            scores_bse = scores.reshape(b, s, E)
            aux = jnp.mean(jnp.sum(ce * scores_bse.mean(axis=1), axis=1)) * ALPHA
            return (y.reshape(b, s, d), aux)
        y, _aux = _moe_forward(x, gate_w, w_gate, w_up, w_down)
        return y
    x = x + _L0_xattn_ref(_layernorm(x, axis=-1), ctx_512, L0_xattn_Wq, L0_xattn_Wkv_expand, L0_xattn_Wout)
    x = x + _L0_attn_ref(_layernorm(x, axis=-1), L0_attn_w_gate, L0_attn_g_gate, L0_attn_w_down, L0_attn_g_down)
    x = x + _L0_ffn_ref(_layernorm(x, axis=-1), L0_ffn_gate_w, L0_ffn_w_gate, L0_ffn_w_up, L0_ffn_w_down)
    return x

_drawn_inputs = setup_inputs


def setup_inputs(seed=0):
    import zlib

    import numpy as np

    out = dict(_drawn_inputs(seed))
    spreads = {}
    factors = {'L0_xattn_Wq': 32.675}
    for name, (base, spread) in spreads.items():
        noise = np.random.default_rng([zlib.crc32(name.encode()), seed]).standard_normal(out[name].shape)
        drawn = base * np.exp(spread * noise) if base else spread * noise
        out[name] = jnp.asarray(drawn.astype(out[name].dtype))
    for name, factor in factors.items():
        out[name] = (out[name] * factor).astype(out[name].dtype)
    return out
```

```python
from contextlib import ExitStack

import numpy as np

import concourse.bass as bass
from concourse import mybir

P = 128
F32 = mybir.dt.float32
F32R = mybir.dt.float32r
BF16 = mybir.dt.bfloat16
U32 = mybir.dt.uint32
ALU = mybir.AluOpType
ACT = mybir.ActivationFunctionType
AX = mybir.AxisListType

B, S, D = 32, 64, 256
SKV, L = 1601, 64
NH = 16
HD = D // NH
INNER = 1024
E, FE, TOPK = 16, 176, 6
T = B * S
NT = T // P
NP = NT // 2
DC = D // P
EPS = 1e-5
ROUND = 1.5 * 2.0 ** 23
MASKED = -1.0e30

HPC = P // HD
NCH = E * FE // P
GT = 512
NG = T // GT
IC = INNER // P


def seen(n):
    return n + 1


class Bufs:

    def __init__(self, nc, ctx):
        self.nc, self.ctx = nc, ctx

    def sb(self, name, shape, dt=F32):
        return self.ctx.enter_context(self.nc.sbuf_tensor(name, shape, dt))

    def ps(self, name, shape, dt=F32):
        return self.ctx.enter_context(self.nc.psum_tensor(name, shape, dt))

    def sem(self, name):
        return self.ctx.enter_context(self.nc.semaphore(name))


class Hold:

    def __init__(self, eng, sem):
        self.eng, self.sem = eng, sem

    def __call__(self):
        self.eng.nop().then_inc(self.sem, 1)


def credit(eng, *sems):
    for s in sems:
        eng.nop().then_inc(s, 1)


def setup_stage(nc, k, Wq, Wkv, Wout, x, ctx_in):
    with ExitStack() as ctx:
        b = Bufs(nc, ctx)
        wq = b.sb("wq_nat", [P, DC, D])
        wkv = b.sb("wkv_nat", [P, 2 * D // P, L])
        wo = b.sb("wo_nat", [P, DC, D])
        psQ = b.ps("psWq", [P, DC, D])
        psO = b.ps("psWo", [P, DC, D])
        psKV = b.ps("psWkv", [L, 2 * D])
        zeroed = b.sem("zeroed")
        ident_ready = b.sem("ident_ready")
        w_loaded = b.sem("w_loaded")
        wT_ready = b.sem("wT_ready")
        wT_hi_ready = b.sem("wT_hi_ready")

        with nc.Block() as block:
            @block.sync
            def _(sp):
                sp.dma_start(wq[:, :, :], Wq.rearrange("(c p) i -> p c i", p=P)).then_inc(w_loaded, 16)
                sp.dma_start(wo[:, :, :], Wout.rearrange("(c p) i -> p c i", p=P)).then_inc(w_loaded, 16)
                sp.dma_start(wkv[:, :, :], Wkv.rearrange("(c p) i -> p c i", p=P)).then_inc(w_loaded, 16)
                sp.dma_start(k.x[:, :, :], x.rearrange("b s d -> (b s) d").rearrange("(n p) d -> p n d", p=P)
                             ).then_inc(k.x_loaded, 16)
                w_gate, w_down, g_gate, g_down = k.bit_weights
                sp.dma_start(k.wg_nat[:, :, :], w_gate.rearrange("(c p) i -> p c i", p=P)).then_inc(k.bit_loaded, 16)
                sp.dma_start(k.wd_nat[:, :, :], w_down.rearrange("(c p) i -> p c i", p=P)).then_inc(k.bit_loaded, 16)
                sp.dma_start(k.g_in[:, :], g_gate.unsqueeze(0).to_broadcast([P, D])).then_inc(k.bit_loaded, 16)
                sp.dma_start(k.g_hid[:, :], g_down.unsqueeze(0).to_broadcast([P, INNER])).then_inc(k.bit_loaded, 16)

            @block.gpsimd
            def _(pool):
                step = [0]

                def in_turn(ins):
                    ins.then_inc(zeroed, 1)
                    step[0] += 1
                    pool.wait_ge(zeroed, step[0])

                in_turn(nc.gpsimd.memset(k.ident[:, :], 0.0))
                nc.gpsimd.affine_select(out=k.ident[:, :], in_=k.ident[:, :], compare_op=ALU.not_equal, fill=1.0,
                                        base=0, pattern=[[-1, P]], channel_multiplier=1).then_inc(ident_ready, 1)
                pool.wait_ge(ident_ready, 1)
                in_turn(nc.gpsimd.memset(k.causal[:, :, :], 0.0))
                for half in range(2):
                    rows = k.causal[half * S:(half + 1) * S, :, :]
                    in_turn(nc.gpsimd.affine_select(out=rows, in_=rows, compare_op=ALU.is_ge, fill=MASKED, base=0,
                                                    pattern=[[0, HPC], [-1, S]], channel_multiplier=1))
                in_turn(nc.gpsimd.memset(k.headmask[:, :], 1.0))
                in_turn(nc.gpsimd.affine_select(out=k.headmask[:, :], in_=k.headmask[:, :], compare_op=ALU.is_ge,
                                                fill=0.0, base=0, pattern=[[-HD, HPC]], channel_multiplier=1))
                in_turn(nc.gpsimd.affine_select(out=k.headmask[:, :], in_=k.headmask[:, :], compare_op=ALU.is_ge,
                                                fill=0.0, base=HD - 1, pattern=[[HD, HPC]], channel_multiplier=-1))

            @block.scalar
            def _(act):
                ctx_v = ctx_in.rearrange("(n b) s l -> b s n l", b=2)
                for half in range(2):
                    act.dma_start(k.ctx[half * S:(half + 1) * S, :, :], ctx_v[half, 0:S, :, :]).then_inc(k.ctx_loaded, 16)
                act.wait_ge(wT_ready, 1)
                nc.scalar.activation(k.wqT_hi[:, :, :], psQ[:, :, :], ACT.Copy).then_inc(wT_hi_ready, 1)
                act.wait_ge(wT_ready, 2)
                nc.scalar.activation(k.woT_hi[:, :, :], psO[:, :, :], ACT.Copy).then_inc(wT_hi_ready, 1)
                act.wait_ge(wT_ready, 3)
                nc.scalar.activation(k.wkvT_hi[:, :], psKV[:, :], ACT.Copy).then_inc(wT_hi_ready, 1)

            @block.vector
            def _(dve):
                for half in range(2):
                    nc.vector.memset(k.vmask[half * S:(half + 1) * S, :, half, :], 1.0)
                    nc.vector.memset(k.vmask[half * S:(half + 1) * S, :, 1 - half, :], 0.0)
                nc.vector.memset(k.minus_half[:, :], -0.5)
                nc.vector.memset(k.ones[:, :], 1.0)
                dve.wait_ge(ident_ready, 1)
                nc.vector.tensor_copy(k.identb[:, :], k.ident[:, :])
                for n, (lo, ps, hi) in enumerate(((k.wqT_lo[:, :, :], psQ[:, :, :], k.wqT_hi[:, :, :]),
                                                  (k.woT_lo[:, :, :], psO[:, :, :], k.woT_hi[:, :, :]),
                                                  (k.wkvT_lo[:, :], psKV[:, :], k.wkvT_hi[:, :]))):
                    dve.wait_ge(wT_hi_ready, n + 1)
                    nc.vector.tensor_tensor(lo, ps, hi.bitcast(F32), ALU.subtract)

            @block.tensor
            def _(pe):
                pe.wait_ge(ident_ready, 1)
                pe.wait_ge(w_loaded, 48)
                for w, ps in ((wq, psQ), (wo, psO)):
                    for oc in range(DC):
                        for ic in range(DC):
                            last = nc.tensor.transpose(ps[:, ic, oc * P:(oc + 1) * P], w[:, oc, ic * P:(ic + 1) * P],
                                                       k.ident[:, :])
                    last.then_inc(wT_ready, 1)
                for oc in range(2 * D // P):
                    last = nc.tensor.transpose(psKV[:, oc * P:(oc + 1) * P], wkv[:, oc, :], k.ident[:, :])
                last.then_inc(wT_ready, 1)


def attention_stage(nc, k):
    with ExitStack() as ctx:
        b = Bufs(nc, ctx)
        W2 = 2 * P
        stats = b.sb("stats", [P, 2, 6])
        mv = b.sb("mv", [P, 2, 2])
        veps = b.sb("veps", [P, 2])
        rstd = b.sb("rstd", [P, 2])
        h = b.sb("h", [P, 2, D])
        cpair = b.sb("cpair", [P, 2, L])
        hT_hi = b.sb("hT_hi", [P, DC, W2], F32R)
        hT_lo = b.sb("hT_lo", [P, DC, W2], F32R)
        cT_hi = b.sb("cT_hi", [L, 4, 2, S], F32R)
        cT_lo = b.sb("cT_lo", [L, 4, 2, S], F32R)
        q_sb = b.sb("q_sb", [P, DC, W2])
        kbd = b.sb("kbd", [P, DC, HPC, W2])
        vbd = b.sb("vbd", [P, 2, 4, D])
        sub = b.sb("sub", [P, 2, HPC, S])
        mx = b.sb("mx", [P, 2, HPC])
        prob = b.sb("prob", [P, 4, HPC, S])
        rsum = b.sb("rsum", [P, 2, HPC])
        rinv = b.sb("rinv", [P, 2, HPC])
        probn = b.sb("probn", [P, 4, HPC * S])
        pT = b.sb("pT", [P, 2, 4, P])
        oT_hi = b.sb("oT_hi", [P, DC, W2], F32R)
        oT_lo = b.sb("oT_lo", [P, DC, W2], F32R)

        R0 = b.ps("R0", [P, 2, 256])
        R1 = b.ps("R1", [P, 2, 256])
        R2 = b.ps("R2", [P, 2, 256])
        psS = [b.ps(f"psS{u}", [P, 512]) for u in range(2)]
        psT = [b.ps(f"psT{u}", [P, 4, P]) for u in range(2)]
        psO = b.ps("psO", [P, DC, W2])

        s_stats, s_mv, s_veps, s_rstd, s_h = (b.sem(n) for n in ("a_stats", "a_mv", "a_veps", "a_rstd", "a_h"))
        s_hT, s_cT, s_hThi, s_cThi, s_hTlo, s_cTlo = (b.sem(n) for n in (
            "a_hT", "a_cT", "a_hThi", "a_cThi", "a_hTlo", "a_cTlo"))
        s_ctxpair = b.sem("a_ctxpair")
        s_q, s_k, s_v01, s_v23 = (b.sem(n) for n in ("a_q", "a_k", "a_v01", "a_v23"))
        s_qsb, s_kbd, s_vbd01, s_vbd23 = (b.sem(n) for n in ("a_qsb", "a_kbd", "a_vbd01", "a_vbd23"))
        s_score, s_mx, s_sub, s_prob, s_rsum, s_rinv, s_probn = (b.sem(n) for n in (
            "a_score", "a_mx", "a_sub", "a_prob", "a_rsum", "a_rinv", "a_probn"))
        s_pT, s_pTsb, s_pv = (b.sem(n) for n in ("a_pT", "a_pTsb", "a_pv"))
        s_oThi, s_oTlo, s_out, s_x1 = (b.sem(n) for n in ("a_oThi", "a_oTlo", "a_out", "a_x1"))

        def pair_of(t3, i):
            return t3[:, bass.ds(2 * i, 2), :] if not isinstance(i, int) else t3[:, 2 * i:2 * i + 2, :]

        def tile_of(t3, n):
            return t3[:, bass.ds(n, 1), :] if not isinstance(n, int) else t3[:, n:n + 1, :]

        with nc.Block() as block:
            @block.vector
            def _(dve):
                credit(dve, s_stats, s_mv, s_h, s_hTlo, s_cTlo, s_vbd01, s_vbd23, s_mx, s_sub, s_rsum, s_rinv,
                       s_probn, s_oTlo, s_x1)

                hold = Hold(dve, b.sem("a_held_dve"))

                def layernorm(i):
                    for t in range(2):
                        row = tile_of(k.x, 2 * i + t)
                        nc.vector.bn_stats(stats[:, t, :], row).then_inc(s_stats, 1)
                    dve.wait_ge(s_stats, seen(2 * i + 2))
                    hold()
                    for t in range(2):
                        nc.vector.bn_aggr(mv[:, t, :], stats[:, t, :]).then_inc(s_mv, 1)
                    dve.wait_ge(s_mv, seen(2 * i + 2))
                    dve.wait_ge(s_rstd, seen(i + 1))
                    dve.wait_ge(s_hT, seen(i))
                    for t in range(2):
                        nc.vector.tensor_scalar(h[:, t:t + 1, :], tile_of(k.x, 2 * i + t), mv[:, t, 0:1],
                                                rstd[:, t:t + 1], ALU.subtract, ALU.mult).then_inc(s_h, 1)

                def low_parts(i):
                    dve.wait_ge(s_hThi, seen(i + 1))
                    dve.wait_ge(s_k, seen(i))
                    nc.vector.tensor_tensor(hT_lo[:, :, :], R0[:, :, :], hT_hi[:, :, :].bitcast(F32),
                                            ALU.subtract).then_inc(s_hTlo, 1)
                    dve.wait_ge(s_cThi, seen(i + 1))
                    dve.wait_ge(s_v23, seen(i))
                    cps = R1[0:L, 0, :].rearrange("p (b s) -> p b s", b=4)
                    for dup in range(2):
                        last = nc.vector.tensor_tensor(cT_lo[:, :, dup, :], cps, cT_hi[:, :, dup, :].bitcast(F32),
                                                       ALU.subtract)
                    last.then_inc(s_cTlo, 1)

                def values(i, ring):
                    for half, (ps, ready, done) in enumerate(((R1, s_v01, s_vbd01), (R2, s_v23, s_vbd23))):
                        dve.wait_ge(ready, seen(i + 1))
                        if half == 0:
                            dve.wait_ge(s_pv, seen(4 * i - 4) if not isinstance(i, int) or i > 0 else 1)
                        vm = k.vmask[:, :, :, :].rearrange("p a b c -> p (a b c)")
                        for bb in range(2):
                            last = nc.vector.tensor_tensor(vbd[:, ring, 2 * half + bb, :], ps[:, bb, :], vm, ALU.mult)
                        last.then_inc(done, 1)

                def softmax(i, u):
                    n = 4 * i + u
                    r = u % 2
                    dve.wait_ge(s_score, seen(n + 1))
                    sc = psS[r][:, :].rearrange("p (h s) -> p h s", h=HPC)
                    nc.vector.tensor_reduce(mx[:, r, :], sc, AX.X, ALU.max).then_inc(s_mx, 1)
                    dve.wait_ge(s_mx, seen(n + 1))
                    if u >= 2:
                        dve.wait_ge(s_prob, seen(n - 1))
                    nc.vector.tensor_tensor(sub[:, r, :, :], sc, mx[:, r, :].unsqueeze(2).to_broadcast([P, HPC, S]),
                                            ALU.subtract).then_inc(s_sub, 1)

                def normalise(i, u):
                    n = 4 * i + u
                    r = u % 2
                    dve.wait_ge(s_prob, seen(n + 1))
                    nc.vector.tensor_reduce(rsum[:, r, :], prob[:, u, :, :], AX.X, ALU.add).then_inc(s_rsum, 1)
                    dve.wait_ge(s_rsum, seen(n + 1))
                    nc.vector.reciprocal(rinv[:, r, :], rsum[:, r, :]).then_inc(s_rinv, 1)
                    dve.wait_ge(s_rinv, seen(n + 1))
                    dve.wait_ge(s_pT, seen(4 * i - 3 + u) if not isinstance(i, int) or i > 0 else 1)
                    nc.vector.tensor_tensor(probn[:, u, :].rearrange("p (h s) -> p h s", h=HPC), prob[:, u, :, :],
                                            rinv[:, r, :].unsqueeze(2).to_broadcast([P, HPC, S]),
                                            ALU.mult).then_inc(s_probn, 1)

                def out_low(j):
                    dve.wait_ge(s_oThi, seen(j + 1))
                    dve.wait_ge(s_out, seen(j))
                    nc.vector.tensor_tensor(oT_lo[:, :, :], psO[:, :, :], oT_hi[:, :, :].bitcast(F32),
                                            ALU.subtract).then_inc(s_oTlo, 1)

                def residual(j):
                    dve.wait_ge(s_out, seen(j + 1))
                    nc.vector.tensor_tensor(pair_of(k.x, j), R0[:, :, :], pair_of(k.x, j), ALU.add).then_inc(s_x1, 1)

                def front(i, ring, back, more=True):
                    low_parts(i)
                    values(i, ring)
                    softmax(i, 0)
                    softmax(i, 1)
                    normalise(i, 0)
                    if back:
                        out_low(i - 1)
                    softmax(i, 2)
                    normalise(i, 1)
                    if back:
                        residual(i - 1)
                    if more:
                        layernorm(i + 1)
                    softmax(i, 3)
                    normalise(i, 2)
                    normalise(i, 3)

                dve.wait_ge(k.x_loaded, 16)
                layernorm(0)
                front(0, 0, False)
                with dve.Fori(0, NP // 2 - 1) as g:
                    front(2 * g + 1, 1, True)
                    front(2 * g + 2, 0, True)
                front(NP - 1, 1, True, more=False)
                out_low(NP - 1)
                residual(NP - 1)

            @block.gpsimd
            def _(pool):
                credit(pool, s_veps, s_rstd, s_ctxpair)
                pool.wait_ge(k.ctx_loaded, 32)

                hold = Hold(pool, b.sem("a_held_pool"))

                def inv_std(i):
                    pool.wait_ge(s_cT, seen(i))
                    hold()
                    nc.gpsimd.tensor_copy(cpair[:, :, :], pair_of(k.ctx, i)).then_inc(s_ctxpair, 1)
                    pool.wait_ge(s_mv, seen(2 * i + 2))
                    pool.wait_ge(s_h, seen(2 * i))
                    hold()
                    nc.gpsimd.tensor_scalar(veps[:, :], mv[:, :, 1], EPS, None, ALU.add).then_inc(s_veps, 1)
                    pool.wait_ge(s_veps, seen(i + 1))
                    nc.gpsimd.tensor_tensor(rstd[:, :], veps[:, :], k.minus_half[:, 0:2], ALU.pow).then_inc(s_rstd, 1)

                inv_std(0)
                with pool.Fori(1, NP) as i:
                    inv_std(i)

            @block.scalar
            def _(act):
                nc.scalar.preload_act_table(ACT.Exp)
                credit(act, s_hThi, s_cThi, s_qsb, s_kbd, s_prob, s_pTsb, s_oThi)

                def high_parts(i):
                    act.wait_ge(s_hT, seen(i + 1))
                    act.wait_ge(s_q, seen(i))
                    nc.scalar.activation(hT_hi[:, :, :], R0[:, :, :], ACT.Copy).then_inc(s_hThi, 1)
                    act.wait_ge(s_cT, seen(i + 1))
                    act.wait_ge(s_v23, seen(i))
                    cps = R1[0:L, 0, :].rearrange("p (b s) -> p b s", b=4)
                    for dup in range(2):
                        last = nc.scalar.activation(cT_hi[:, :, dup, :], cps, ACT.Copy)
                    last.then_inc(s_cThi, 1)

                def queries_keys(i):
                    act.wait_ge(s_q, seen(i + 1))
                    act.wait_ge(s_score, seen(4 * i))
                    nc.scalar.activation(q_sb[:, :, :], R2[:, :, :], ACT.Copy).then_inc(s_qsb, 1)
                    act.wait_ge(s_k, seen(i + 1))
                    for hh in range(HPC):
                        last = nc.scalar.activation(kbd[:, :, hh, :], R0[:, :, :], ACT.Copy,
                                                    scale=k.headmask[:, hh:hh + 1])
                    last.then_inc(s_kbd, 1)

                def exps(i, u):
                    n = 4 * i + u
                    act.wait_ge(s_sub, seen(n + 1))
                    act.wait_ge(s_probn, seen(4 * i - 3 + u) if not isinstance(i, int) or i > 0 else 1)
                    nc.scalar.activation(prob[:, u, :, :], sub[:, u % 2, :, :], ACT.Exp,
                                         scale=float(HD) ** -0.5).then_inc(s_prob, 1)

                def probs_out(j, u):
                    n = 4 * j + u
                    act.wait_ge(s_pT, seen(n + 1))
                    if isinstance(n, int) and n < 2:
                        act.wait_ge(s_pv, 1)
                    else:
                        act.wait_ge(s_pv, seen(n - 1))
                    nc.scalar.activation(pT[:, u % 2, :, :], psT[u % 2][:, :, :], ACT.Copy).then_inc(s_pTsb, 1)

                def out_high(j):
                    act.wait_ge(s_pv, seen(4 * j + 4))
                    act.wait_ge(s_out, seen(j))
                    nc.scalar.activation(oT_hi[:, :, :], psO[:, :, :], ACT.Copy).then_inc(s_oThi, 1)

                def turn(i, back):
                    high_parts(i)
                    if back:
                        probs_out(i - 1, 0)
                    queries_keys(i)
                    if back:
                        probs_out(i - 1, 1)
                        probs_out(i - 1, 2)
                    exps(i, 0)
                    exps(i, 1)
                    if back:
                        probs_out(i - 1, 3)
                        out_high(i - 1)
                    exps(i, 2)
                    exps(i, 3)

                turn(0, False)
                with act.Fori(1, NP) as i:
                    turn(i, True)
                for u in range(4):
                    probs_out(NP - 1, u)
                out_high(NP - 1)

            @block.tensor
            def _(pe):
                credit(pe, s_hT, s_cT, s_q, s_k, s_v01, s_v23, s_score, s_pT, s_pv, s_out)

                hold = Hold(pe, b.sem("a_held_pe"))

                def three(out, pairs_hi_lo):
                    n = len(pairs_hi_lo)
                    for c, (lh, ll, rh, rl) in enumerate(pairs_hi_lo):
                        nc.tensor.matmul(out, ll, rh, start=(c == 0), stop=False)
                        nc.tensor.matmul(out, lh, rl, start=False, stop=False)
                        last = nc.tensor.matmul(out, lh, rh, start=False, stop=(c == n - 1))
                    return last

                def transposes(i):
                    pe.wait_ge(s_x1, seen(i - 1) if not isinstance(i, int) or i > 0 else 1)
                    for t in range(2):
                        pe.wait_ge(s_h, seen(2 * i + t + 1))
                        for c in range(DC):
                            last = nc.tensor.transpose(R0[:, c, t * P:(t + 1) * P], h[:, t, c * P:(c + 1) * P],
                                                       k.ident[:, :])
                    last.then_inc(s_hT, 1)
                    pe.wait_ge(s_vbd01, seen(i))
                    pe.wait_ge(s_ctxpair, seen(i + 1))
                    hold()
                    for t in range(2):
                        last = nc.tensor.transpose(R1[0:L, 0, t * P:(t + 1) * P], cpair[:, t, :], k.ident[:, :])
                    last.then_inc(s_cT, 1)

                def queries_keys(i):
                    pe.wait_ge(s_hTlo, seen(i + 1))
                    pe.wait_ge(s_vbd23, seen(i))
                    for m in range(DC):
                        cols = slice(m * P, (m + 1) * P)
                        last = three(R2[:, m, :], [(k.wqT_hi[:, c, cols], k.wqT_lo[:, c, cols], hT_hi[:, c, :],
                                                    hT_lo[:, c, :]) for c in range(DC)])
                    last.then_inc(s_q, 1)
                    pe.wait_ge(s_cTlo, seen(i + 1))
                    for m in range(DC):
                        cols = slice(m * P, (m + 1) * P)
                        last = three(R0[:, m, :].rearrange("p (b s) -> p b s", b=4),
                                     [(k.wkvT_hi[:, cols], k.wkvT_lo[:, cols], cT_hi[:, :, 0, :], cT_lo[:, :, 0, :])])
                    last.then_inc(s_k, 1)

                def values(i, half):
                    ps, ready = ((R1, s_v01), (R2, s_v23))[half]
                    if half == 1:
                        pe.wait_ge(s_qsb, seen(i + 1))
                    for bb in range(2):
                        bt = 2 * half + bb
                        hi = cT_hi[:, bt, :, :].rearrange("p a s -> p (a s)")
                        lo = cT_lo[:, bt, :, :].rearrange("p a s -> p (a s)")
                        last = three(ps[:, bb, :], [(hi, lo, k.wkvT_hi[:, D:2 * D], k.wkvT_lo[:, D:2 * D])])
                    last.then_inc(ready, 1)

                def scores(i, u):
                    n = 4 * i + u
                    t, m = u // 2, u % 2
                    if u == 0:
                        pe.wait_ge(s_qsb, seen(i + 1))
                        pe.wait_ge(s_kbd, seen(i + 1))
                    pe.wait_ge(s_sub, seen(n - 1) if not (isinstance(n, int) and n < 2) else 1)
                    nc.tensor.matmul(psS[m][:, :], k.identb[:, :], k.causal[:, :, :].rearrange("p h s -> p (h s)"),
                                     start=True, stop=True, skip_group_check=True)
                    for bb in range(2):
                        tok = slice(t * P + bb * S, t * P + (bb + 1) * S)
                        last = nc.tensor.matmul(psS[m][bb * S:(bb + 1) * S, :].rearrange("p (h s) -> p h s", h=HPC),
                                                q_sb[:, m, tok], kbd[:, m, :, tok], start=False, stop=True,
                                                skip_group_check=True)
                    last.then_inc(s_score, 1)

                def probs_transposed(j, u):
                    n = 4 * j + u
                    pe.wait_ge(s_probn, seen(n + 1))
                    pe.wait_ge(s_pTsb, seen(n - 1) if not (isinstance(n, int) and n < 2) else 1)
                    for hp in range(4):
                        last = nc.tensor.transpose(psT[u % 2][:, hp, :], probn[:, u, hp * P:(hp + 1) * P],
                                                   k.ident[:, :])
                    last.then_inc(s_pT, 1)

                def attend(j, u, ring):
                    n = 4 * j + u
                    t, m = u // 2, u % 2
                    pe.wait_ge(s_pTsb, seen(n + 1))
                    if u == 0:
                        pe.wait_ge(s_oTlo, seen(j))
                        pe.wait_ge(s_vbd23, seen(j + 1))
                    for hp in range(4):
                        for bb in range(2):
                            tok = slice(t * P + bb * S, t * P + (bb + 1) * S)
                            head = (m * 4 + hp) * 2 * HD
                            last = nc.tensor.matmul(psO[32 * hp:32 * hp + 32, m, tok],
                                                    vbd[:, ring, 2 * t + bb, head:head + 2 * HD],
                                                    pT[:, u % 2, hp, bb * S:(bb + 1) * S], start=True, stop=True)
                    last.then_inc(s_pv, 1)

                def project(j):
                    pe.wait_ge(s_oTlo, seen(j + 1))
                    for t in range(2):
                        tok = slice(t * P, (t + 1) * P)
                        last = three(R0[:, t, :], [(oT_hi[:, c, tok], oT_lo[:, c, tok], k.woT_hi[:, c, :],
                                                    k.woT_lo[:, c, :]) for c in range(DC)])
                    last.then_inc(s_out, 1)

                def turn(i, ring, back):
                    transposes(i)
                    if back:
                        probs_transposed(i - 1, 0)
                    queries_keys(i)
                    if back:
                        attend(i - 1, 0, 1 - ring)
                        probs_transposed(i - 1, 1)
                    values(i, 0)
                    values(i, 1)
                    if back:
                        probs_transposed(i - 1, 2)
                        attend(i - 1, 1, 1 - ring)
                    scores(i, 0)
                    scores(i, 1)
                    if back:
                        attend(i - 1, 2, 1 - ring)
                        probs_transposed(i - 1, 3)
                        attend(i - 1, 3, 1 - ring)
                    scores(i, 2)
                    if back:
                        project(i - 1)
                    scores(i, 3)

                turn(0, 0, False)
                with pe.Fori(0, NP // 2 - 1) as g:
                    turn(2 * g + 1, 1, True)
                    turn(2 * g + 2, 0, True)
                turn(NP - 1, 1, True)
                for u in range(4):
                    probs_transposed(NP - 1, u)
                    attend(NP - 1, u, 1)
                project(NP - 1)


class Steps:

    def __init__(self, eng, sem, per_turn):
        self.eng, self.sem, self.per_turn = eng, sem, per_turn

    def begin(self, turn):
        self.base, self.k = turn * self.per_turn, 0

    def done(self, ins):
        ins.then_inc(self.sem, 1)
        self.k += 1

    def wait_last(self):
        self.eng.wait_ge(self.sem, seen(self.base + self.k))

    def end(self):
        assert self.k == self.per_turn, (self.k, self.per_turn)


def at(t3, n, count=1):
    return t3[:, n:n + count, :] if isinstance(n, int) else t3[:, bass.ds(n, count), :]


def quantise_stage(nc, k):
    with ExitStack() as ctx:
        b = Bufs(nc, ctx)
        asum = b.sb("asum", [P, 2])
        wrec = b.sb("wrec", [P, 2])
        stats = b.sb("q_stats", [P, NT, 6])
        tmp = b.sb("q_tmp", [P, 4, NT])
        wgq = b.sb("wgq", [P, 2 * INNER // P, D], BF16)
        wdq = b.sb("wdq", [P, DC, INNER], BF16)
        psSum = b.ps("psSum", [P, 2])
        psW = [b.ps(f"psW{n}", [P, 1024], BF16) for n in range(6)]
        s_abs, s_sum, s_mean, s_rec, s_scaled, s_clip, s_quant, s_wT, s_stats, s_mv, s_pool = (b.sem(n) for n in (
            "q_abs", "q_sum", "q_mean", "q_rec", "q_scaled", "q_clip", "q_quant", "q_wT", "q_statd", "q_mv", "q_pool"))
        w2 = (k.wg_nat[:, :, :].rearrange("p c i -> p (c i)"), k.wd_nat[:, :, :].rearrange("p c i -> p (c i)"))
        q2 = (wgq[:, :, :].rearrange("p c i -> p (c i)"), wdq[:, :, :].rearrange("p c i -> p (c i)"))

        with nc.Block() as block:
            @block.vector
            def _(dve):
                dve.wait_ge(k.bit_loaded, 64)
                for j in range(2):
                    nc.vector.tensor_reduce(asum[:, j:j + 1], w2[j], AX.X, ALU.add,
                                            apply_absolute_value=True).then_inc(s_abs, 1)
                for n in range(NT):
                    nc.vector.bn_stats(stats[:, n, :], k.x[:, n, :]).then_inc(s_stats, 1)
                dve.wait_ge(s_sum, 1)
                for j, count in enumerate((2 * INNER * D, D * INNER)):
                    nc.vector.tensor_scalar(k.wmean[:, j:j + 1], psSum[:, j:j + 1], 1.0 / count, 1e-5, ALU.mult,
                                            ALU.max).then_inc(s_mean, 1)
                dve.wait_ge(s_mean, 2)
                nc.vector.reciprocal(wrec[:, :], k.wmean[:, :]).then_inc(s_rec, 1)
                dve.wait_ge(s_stats, NT)
                for n in range(NT):
                    nc.vector.bn_aggr(k.mv[:, n, :], stats[:, n, :]).then_inc(s_mv, 1)
                for j in range(2):
                    dve.wait_ge(s_scaled, j + 1)
                    nc.vector.tensor_scalar(w2[j], w2[j], 1.0, -1.0, ALU.min, ALU.max).then_inc(s_clip, 1)
                    dve.wait_ge(s_clip, j + 1)
                    nc.vector.tensor_scalar(q2[j], w2[j], ROUND, -ROUND, ALU.add, ALU.add).then_inc(s_quant, 1)
                for n in range(4, 6):
                    dve.wait_ge(s_wT, n + 1)
                    nc.vector.tensor_copy(k.wdT[:, 4 * (n - 4):4 * (n - 3), :],
                                          psW[n][:, :].rearrange("p (c d) -> p c d", c=4))

            @block.gpsimd
            def _(pool):
                step = [0]

                def in_turn(ins):
                    ins.then_inc(s_pool, 1)
                    step[0] += 1
                    pool.wait_ge(s_pool, step[0])

                pool.wait_ge(s_mv, NT)
                var, mh = k.mv[:, :, 1], k.minus_half[:, 0:NT]
                a, r, v2, r2 = (tmp[:, n, :] for n in range(4))
                in_turn(nc.gpsimd.tensor_scalar(a, var, EPS, None, ALU.add))
                in_turn(nc.gpsimd.tensor_tensor(r, a, mh, ALU.pow))
                in_turn(nc.gpsimd.tensor_tensor(v2, r, r, ALU.mult))
                in_turn(nc.gpsimd.tensor_tensor(a, v2, var, ALU.mult))
                in_turn(nc.gpsimd.tensor_scalar(v2, a, EPS, None, ALU.add))
                in_turn(nc.gpsimd.tensor_tensor(r2, v2, mh, ALU.pow))
                in_turn(nc.gpsimd.tensor_tensor(k.norm[:, :], r, r2, ALU.mult))

            @block.scalar
            def _(act):
                for j in range(2):
                    act.wait_ge(s_rec, 1)
                    nc.scalar.activation(w2[j], w2[j], ACT.Copy, scale=wrec[:, j:j + 1]).then_inc(s_scaled, 1)
                for n in range(4):
                    act.wait_ge(s_wT, n + 1)
                    nc.scalar.activation(k.wgT[:, :, n * 512:(n + 1) * 512],
                                         psW[n][:, :].rearrange("p (c o) -> p c o", c=DC), ACT.Copy)

            @block.tensor
            def _(pe):
                pe.wait_ge(s_abs, 2)
                nc.tensor.matmul(psSum[:, :], k.ones[:, :], asum[:, :], start=True, stop=True).then_inc(s_sum, 1)
                pe.wait_ge(s_quant, 1)
                for n in range(4):
                    for c in range(4):
                        for ic in range(DC):
                            last = nc.tensor.transpose(psW[n][:, ic * 512 + c * P:ic * 512 + (c + 1) * P],
                                                       wgq[:, 4 * n + c, ic * P:(ic + 1) * P], k.identb[:, :])
                    last.then_inc(s_wT, 1)
                pe.wait_ge(s_quant, 2)
                for n in range(2):
                    for c in range(4):
                        for dc in range(DC):
                            last = nc.tensor.transpose(psW[4 + n][:, c * D + dc * P:c * D + (dc + 1) * P],
                                                       wdq[:, dc, (4 * n + c) * P:(4 * n + c + 1) * P], k.identb[:, :])
                    last.then_inc(s_wT, 1)


def bitlinear_stage(nc, k):
    with ExitStack() as ctx:
        b = Bufs(nc, ctx)
        xn = b.sb("xn", [P, 1, D])
        xg = b.sb("xg", [P, D])
        xr = b.sb("xr", [P, D])
        q = b.sb("q_in", [P, D], BF16)
        small = b.sb("small_in", [P, 4])
        dq = b.sb("dq", [P, 2])
        qT = b.sb("qT", [P, 2, DC, P], BF16)
        gate = b.sb("gate", [P, 2, INNER])
        hid = b.sb("hid", [P, 2, INNER])
        hsq = b.sb("hsq", [P, INNER])
        ssq = b.sb("ssq", [P, 2])
        rms = b.sb("rms", [P, 2, 2])
        hg = b.sb("hg", [P, INNER])
        hr = b.sb("hr", [P, INNER])
        hq = b.sb("hq", [P, 2, INNER], BF16)
        hsmall = b.sb("small_h", [P, 4])
        dqh = b.sb("dqh", [P, 2])
        hqT = b.sb("hqT", [P, 2, IC, P], BF16)
        psUp = b.ps("psUp", [P, 2 * INNER])
        psQ = b.ps("psQ", [P, DC, P], BF16)
        psH = b.ps("psH", [P, IC, P], BF16)
        psD = b.ps("psD", [P, D])
        s_in, s_q, s_qT, s_qTsb, s_gate, s_v, s_silu, s_hid, s_ssq, s_pool, s_hq, s_hqT, s_hqTsb, s_down, s_x2, \
            s_act = (b.sem(n) for n in ("b_in", "b_q", "b_qT", "b_qTsb", "b_gate", "b_v", "b_silu", "b_hid", "b_ssq",
                                        "b_pool", "b_hq", "b_hqT", "b_hqTsb", "b_down", "b_x2", "b_act"))
        s_hstep, s_held = b.sem("b_hstep"), b.sem("b_held")

        with nc.Block() as block:
            @block.vector
            def _(dve):
                credit(dve, s_in, s_q, s_hid, s_hq, s_x2, s_hstep)
                ins = Steps(dve, s_in, 8)
                hs = Steps(dve, s_hstep, 7)

                def quantise_input(n, par):
                    ins.begin(n)
                    dve.wait_ge(s_q, seen(n))
                    ins.done(nc.vector.tensor_scalar(xn[:, :, :], at(k.x, n), at(k.mv, n)[:, 0, 0:1],
                                                     k.norm1(n), ALU.subtract, ALU.mult))
                    ins.wait_last()
                    ins.done(nc.vector.tensor_tensor(xg[:, :], xn[:, 0, :], k.g_in[:, :], ALU.mult))
                    ins.wait_last()
                    ins.done(nc.vector.tensor_reduce(small[:, 0:1], xg[:, :], AX.X, ALU.max,
                                                     apply_absolute_value=True))
                    ins.wait_last()
                    ins.done(nc.vector.tensor_scalar(small[:, 1:2], small[:, 0:1], 1e-5, None, ALU.max))
                    ins.wait_last()
                    ins.done(nc.vector.reciprocal(small[:, 2:3], small[:, 1:2]))
                    ins.done(nc.vector.tensor_scalar(dq[:, par:par + 1], small[:, 1:2], k.wmean[:, 0:1], 1.0 / 127.0,
                                                     ALU.mult, ALU.mult))
                    ins.wait_last()
                    ins.done(nc.vector.tensor_scalar(small[:, 3:4], small[:, 2:3], 127.0, None, ALU.mult))
                    ins.wait_last()
                    ins.done(nc.vector.tensor_scalar(xr[:, :], xg[:, :], small[:, 3:4], ROUND, ALU.mult, ALU.add))
                    ins.wait_last()
                    dve.wait_ge(s_qT, seen(n))
                    nc.vector.tensor_scalar(q[:, :], xr[:, :], -ROUND, 127.0, ALU.add, ALU.min).then_inc(s_q, 1)
                    ins.end()

                def hidden(n, par):
                    hs.begin(n)
                    dve.wait_ge(s_silu, seen(n + 1))
                    dve.wait_ge(s_v, seen(n + 1))
                    dve.wait_ge(s_ssq, seen(n - 1) if not isinstance(n, int) or n > 0 else 1)
                    nc.vector.scalar_tensor_tensor(out=hid[:, par, :], in0=psUp[:, INNER:2 * INNER],
                                                   scalar=dq[:, par:par + 1], in1=gate[:, par, :], op0=ALU.mult,
                                                   op1=ALU.mult).then_inc(s_hid, 1)
                    dve.wait_ge(s_hid, seen(n + 1))
                    hs.done(nc.vector.tensor_tensor(hg[:, :], hid[:, par, :], k.g_hid[:, :], ALU.mult))
                    hs.wait_last()
                    hs.done(nc.vector.tensor_reduce(hsmall[:, 0:1], hg[:, :], AX.X, ALU.max,
                                                    apply_absolute_value=True))

                def quantise_hidden(n, par):
                    rs = rms[:, par, 1:2]
                    hs.wait_last()
                    dve.wait_ge(s_pool, seen(2 * n + 2))
                    hs.done(nc.vector.tensor_scalar(hsmall[:, 1:2], hsmall[:, 0:1], rs, 1e-5, ALU.mult, ALU.max))
                    hs.wait_last()
                    hs.done(nc.vector.reciprocal(hsmall[:, 2:3], hsmall[:, 1:2]))
                    hs.done(nc.vector.tensor_scalar(dqh[:, par:par + 1], hsmall[:, 1:2], k.wmean[:, 1:2], 1.0 / 127.0,
                                                    ALU.mult, ALU.mult))
                    hs.wait_last()
                    hs.done(nc.vector.tensor_scalar(hsmall[:, 3:4], hsmall[:, 2:3], rs, 127.0, ALU.mult, ALU.mult))
                    hs.wait_last()
                    hs.done(nc.vector.tensor_scalar(hr[:, :], hg[:, :], hsmall[:, 3:4], ROUND, ALU.mult, ALU.add))
                    hs.wait_last()
                    dve.wait_ge(s_hqT, seen(n - 1) if not isinstance(n, int) or n > 0 else 1)
                    nc.vector.tensor_scalar(hq[:, par, :], hr[:, :], -ROUND, 127.0, ALU.add, ALU.min).then_inc(s_hq, 1)
                    hs.end()

                def residual(n, par):
                    dve.wait_ge(s_down, seen(n + 1))
                    nc.vector.scalar_tensor_tensor(out=at(k.x, n)[:, 0, :], in0=psD[:, :], scalar=dqh[:, par:par + 1],
                                                   in1=at(k.x, n)[:, 0, :], op0=ALU.mult, op1=ALU.add
                                                   ).then_inc(s_x2, 1)

                def turn(n, par, before=True, after=True):
                    hidden(n, par)
                    if after:
                        quantise_input(n + 1, 1 - par)
                    if before:
                        residual(n - 1, 1 - par)
                    quantise_hidden(n, par)

                quantise_input(0, 0)
                turn(0, 0, before=False)
                with dve.Fori(0, NT // 2 - 1) as g:
                    turn(2 * g + 1, 1)
                    turn(2 * g + 2, 0)
                turn(NT - 1, 1, after=False)
                residual(NT - 1, 1)

            @block.gpsimd
            def _(pool):
                credit(pool, s_pool)
                hold = Hold(pool, s_held)

                def inv_rms(n, par):
                    pool.wait_ge(s_ssq, seen(n + 1))
                    pool.wait_ge(s_hq, seen(n - 1) if not isinstance(n, int) or n > 0 else 1)
                    hold()
                    nc.gpsimd.tensor_scalar(rms[:, par, 0:1], ssq[:, par:par + 1], 1.0 / INNER, EPS, ALU.mult,
                                            ALU.add).then_inc(s_pool, 1)
                    pool.wait_ge(s_pool, seen(2 * n + 1))
                    nc.gpsimd.tensor_tensor(rms[:, par, 1:2], rms[:, par, 0:1], k.minus_half[:, 0:1],
                                            ALU.pow).then_inc(s_pool, 1)

                inv_rms(0, 0)
                with pool.Fori(0, NT // 2 - 1) as g:
                    inv_rms(2 * g + 1, 1)
                    inv_rms(2 * g + 2, 0)
                inv_rms(NT - 1, 1)

            @block.scalar
            def _(act):
                nc.scalar.preload_act_table(ACT.Silu)
                credit(act, s_qTsb, s_silu, s_ssq, s_hqTsb)

                def q_out(n, par):
                    act.wait_ge(s_qT, seen(n + 1))
                    act.wait_ge(s_v, seen(n - 1) if not isinstance(n, int) or n > 0 else 1)
                    nc.scalar.activation(qT[:, par, :, :], psQ[:, :, :], ACT.Copy).then_inc(s_qTsb, 1)

                def silu(n, par):
                    act.wait_ge(s_gate, seen(n + 1))
                    act.wait_ge(s_hid, seen(n - 1) if not isinstance(n, int) or n > 0 else 1)
                    nc.scalar.activation(gate[:, par, :], psUp[:, 0:INNER], ACT.Silu,
                                         scale=dq[:, par:par + 1]).then_inc(s_silu, 1)

                def squares(n, par):
                    act.wait_ge(s_hid, seen(n + 1))
                    act.wait_ge(s_pool, seen(2 * n - 2) if not isinstance(n, int) or n > 0 else 1)
                    nc.scalar.activation(hsq[:, :], hid[:, par, :], ACT.Square,
                                         accum_out=ssq[:, par:par + 1]).then_inc(s_ssq, 1)

                def hq_out(n, par):
                    act.wait_ge(s_hqT, seen(n + 1))
                    act.wait_ge(s_down, seen(n - 1) if not isinstance(n, int) or n > 0 else 1)
                    nc.scalar.activation(hqT[:, par, :, :], psH[:, :, :], ACT.Copy).then_inc(s_hqTsb, 1)

                def turn(n, par, before=True, after=True):
                    silu(n, par)
                    if before:
                        hq_out(n - 1, 1 - par)
                    squares(n, par)
                    if after:
                        q_out(n + 1, 1 - par)

                q_out(0, 0)
                turn(0, 0, before=False)
                with act.Fori(0, NT // 2 - 1) as g:
                    turn(2 * g + 1, 1)
                    turn(2 * g + 2, 0)
                turn(NT - 1, 1, after=False)
                hq_out(NT - 1, 1)

            @block.tensor
            def _(pe):
                credit(pe, s_qT, s_gate, s_v, s_hqT, s_down)

                def q_transposed(n, par):
                    pe.wait_ge(s_q, seen(n + 1))
                    pe.wait_ge(s_qTsb, seen(n))
                    for c in range(DC):
                        last = nc.tensor.transpose(psQ[:, c, :], q[:, c * P:(c + 1) * P], k.identb[:, :])
                    last.then_inc(s_qT, 1)

                def up(n, par):
                    pe.wait_ge(s_qTsb, seen(n + 1))
                    for half, (free, ready) in enumerate(((s_silu, s_gate), (s_hid, s_v))):
                        pe.wait_ge(free, seen(n))
                        for o in range(2 * half, 2 * half + 2):
                            for c in range(DC):
                                last = nc.tensor.matmul(psUp[:, o * 512:(o + 1) * 512], qT[:, par, c, :],
                                                        k.wgT[:, c, o * 512:(o + 1) * 512], start=(c == 0),
                                                        stop=(c == DC - 1))
                        last.then_inc(ready, 1)

                def h_transposed(n, par):
                    pe.wait_ge(s_hq, seen(n + 1))
                    pe.wait_ge(s_hqTsb, seen(n))
                    for c in range(IC):
                        last = nc.tensor.transpose(psH[:, c, :], hq[:, par, c * P:(c + 1) * P], k.identb[:, :])
                    last.then_inc(s_hqT, 1)

                def down(n, par):
                    pe.wait_ge(s_hqTsb, seen(n + 1))
                    pe.wait_ge(s_x2, seen(n))
                    for c in range(IC):
                        last = nc.tensor.matmul(psD[:, :], hqT[:, par, c, :], k.wdT[:, c, :], start=(c == 0),
                                                stop=(c == IC - 1))
                    last.then_inc(s_down, 1)

                def turn(n, par, before=True, after=True):
                    up(n, par)
                    if before:
                        h_transposed(n - 1, 1 - par)
                    if after:
                        q_transposed(n + 1, 1 - par)
                    if before:
                        down(n - 1, 1 - par)

                q_transposed(0, 0)
                turn(0, 0, before=False)
                with pe.Fori(0, NT // 2 - 1) as g:
                    turn(2 * g + 1, 1)
                    turn(2 * g + 2, 0)
                turn(NT - 1, 1, after=False)
                h_transposed(NT - 1, 1)
                down(NT - 1, 1)


def route_stage(nc, k, gate_w):
    with ExitStack() as ctx:
        b = Bufs(nc, ctx)
        stats = b.sb("r_stats", [P, NT, 6])
        mv = b.sb("r_mv", [P, NT, 2])
        veps = b.sb("r_veps", [P, NT])
        rstd = b.sb("r_rstd", [P, NT])
        h = b.sb("r_h", [P, 2, D])
        gw = b.sb("gw", [E, D])
        gwT_hi, gwT_lo = (b.sb(f"gwT_{p}", [P, DC, E], F32R) for p in ("hi", "lo"))
        lgT = b.sb("lgT", [E, 2 * P])
        logit = b.sb("logit", [P, NT, E])
        mx = b.sb("r_mx", [P, NT])
        ex = b.sb("r_ex", [P, NT, E])
        rsum = b.sb("r_sum", [P, NT])
        rinv = b.sb("r_inv", [P, NT])
        score = b.sb("score", [P, NT, E])
        top = b.sb("top", [P, NT, 8])
        topi = b.sb("topi", [P, NT, 8], U32)
        topf = b.sb("topf", [P, NT, 8])
        iota_i = b.sb("iota_i", [P, E], mybir.dt.int32)
        iota_f = b.sb("iota_f", [P, E])
        eq = b.sb("eq", [P, NT, E, TOPK])
        chosen = b.sb("chosen", [P, NT, E])
        cw = b.sb("cw", [P, NT, E])
        cws = b.sb("cws", [P, NT, 2 * E])
        sel_a = b.sb("sel_a", [2 * E, NCH * P])
        sel_b = b.sb("sel_b", [2 * E, NCH * P])
        psH = b.ps("r_psH", [P, DC, 2 * P])
        psG = b.ps("r_psG", [E, 2 * P])
        psL = b.ps("r_psL", [P, 2, E])
        psW = b.ps("r_psW", [P, DC, E])
        psC = b.ps("r_psC", [2 * E, T])
        (s_gwl, s_gwT, s_gwhi, s_gwlo, s_stats, s_mv, s_pool, s_rstd, s_h, s_hT, s_hi, s_lo, s_lgT, s_lgTsb, s_lg,
         s_lgsb, s_ex, s_step, s_cws, s_cwT, s_iota, s_sel) = (b.sem("r_" + n) for n in (
             "gwl", "gwT", "gwhi", "gwlo", "statd", "mvd", "pool", "rstdd", "hd", "hT", "hi", "lo", "lgTd", "lgTsb", "lg",
             "lgsb", "exd", "step", "cwsd", "cwT", "iota", "sel"))

        with nc.Block() as block:
            @block.sync
            def _(sp):
                sp.dma_start(gw[:, :], gate_w).then_inc(s_gwl, 16)
                sp.dma_start(k.x2_dram, k.x[:, :, :]).then_inc(k.x2_spilled, 16)
                sp.wait_ge(k.x2_spilled, 16)

            @block.gpsimd
            def _(pool):
                pool.wait_ge(s_mv, NT)
                nc.gpsimd.tensor_scalar(veps[:, :], mv[:, :, 1], EPS, None, ALU.add).then_inc(s_pool, 1)
                pool.wait_ge(s_pool, 1)
                nc.gpsimd.tensor_tensor(rstd[:, :], veps[:, :], k.minus_half[:, :], ALU.pow).then_inc(s_rstd, 1)
                pool.wait_ge(s_rstd, 1)
                nc.gpsimd.iota(iota_i[:, :], pattern=[[1, E]], base=0, channel_multiplier=0).then_inc(s_iota, 1)
                pool.wait_ge(s_iota, 1)
                n = 1
                for buf, first in ((sel_a, 0), (sel_b, E)):
                    for ins in (lambda: nc.gpsimd.memset(buf[:, :], 1.0),
                                lambda: nc.gpsimd.affine_select(out=buf[:, :], in_=buf[:, :], compare_op=ALU.is_ge,
                                                                fill=0.0, base=FE * first, pattern=[[1, NCH * P]],
                                                                channel_multiplier=-FE),
                                lambda: nc.gpsimd.affine_select(out=buf[:, :], in_=buf[:, :], compare_op=ALU.is_ge,
                                                                fill=0.0, base=FE - 1 - FE * first,
                                                                pattern=[[-1, NCH * P]], channel_multiplier=FE)):
                        ins().then_inc(s_sel, 1)
                        pool.wait_ge(s_sel, n)
                        n += 1

            @block.scalar
            def _(act):
                nc.scalar.preload_act_table(ACT.Exp)
                act.wait_ge(s_gwT, 1)
                nc.scalar.activation(gwT_hi[:, :, :], psW[:, :, :], ACT.Copy).then_inc(s_gwhi, 1)
                with act.Fori(0, NP) as i:
                    act.wait_ge(s_hT, i + 1)
                    nc.scalar.activation(k.h_hi[:, :, bass.ds(i * 256, 256)], psH[:, :, :], ACT.Copy).then_inc(s_hi, 1)
                    act.wait_ge(s_lgT, i + 1)
                    nc.scalar.activation(lgT[:, :], psG[:, :], ACT.Copy).then_inc(s_lgTsb, 1)
                act.wait_ge(s_step, 2)
                nc.scalar.activation(ex[:, :, :], logit[:, :, :], ACT.Exp).then_inc(s_ex, 1)
                act.wait_ge(s_cwT, 1)
                nc.scalar.activation(k.cwT[:, :], psC[:, :], ACT.Copy)

            @block.vector
            def _(dve):
                credit(dve, s_lo, s_lgsb)
                for n in range(NT):
                    nc.vector.bn_stats(stats[:, n, :], k.x[:, n, :]).then_inc(s_stats, 1)
                dve.wait_ge(s_stats, NT)
                for n in range(NT):
                    nc.vector.bn_aggr(mv[:, n, :], stats[:, n, :]).then_inc(s_mv, 1)
                dve.wait_ge(s_gwhi, 1)
                nc.vector.tensor_tensor(gwT_lo[:, :, :], psW[:, :, :], gwT_hi[:, :, :].bitcast(F32),
                                        ALU.subtract).then_inc(s_gwlo, 1)
                dve.wait_ge(s_mv, NT)
                dve.wait_ge(s_rstd, 1)
                with dve.Fori(0, NP) as i:
                    for t in range(2):
                        n = 2 * i + t
                        nc.vector.tensor_scalar(h[:, t:t + 1, :], at(k.x, n), at(mv, n)[:, 0, 0:1],
                                                rstd[:, bass.ds(n, 1)], ALU.subtract, ALU.mult).then_inc(s_h, 1)
                    dve.wait_ge(s_hi, i + 1)
                    nc.vector.tensor_tensor(k.h_lo[:, :, bass.ds(i * 256, 256)], psH[:, :, :],
                                            k.h_hi[:, :, bass.ds(i * 256, 256)].bitcast(F32),
                                            ALU.subtract).then_inc(s_lo, 1)
                    dve.wait_ge(s_lg, i + 1)
                    nc.vector.tensor_copy(logit[:, bass.ds(2 * i, 2), :], psL[:, :, :]).then_inc(s_lgsb, 1)
                step = [0]

                def in_turn(ins):
                    ins.then_inc(s_step, 1)
                    step[0] += 1
                    dve.wait_ge(s_step, step[0])

                def over_experts(t2):
                    return t2[:, :].unsqueeze(2).to_broadcast([P, NT, E])

                dve.wait_ge(s_lgsb, seen(NP))
                in_turn(nc.vector.tensor_reduce(mx[:, :], logit[:, :, :], AX.X, ALU.max))
                in_turn(nc.vector.tensor_tensor(logit[:, :, :], logit[:, :, :], over_experts(mx), ALU.subtract))
                dve.wait_ge(s_ex, 1)
                in_turn(nc.vector.tensor_reduce(rsum[:, :], ex[:, :, :], AX.X, ALU.add))
                in_turn(nc.vector.reciprocal(rinv[:, :], rsum[:, :]))
                in_turn(nc.vector.tensor_tensor(score[:, :, :], ex[:, :, :], over_experts(rinv), ALU.mult))
                for n in range(NT):
                    last = nc.vector.max(top[:, n, :], score[:, n, :])
                in_turn(last)
                for n in range(NT):
                    last = nc.vector.max_index(topi[:, n, :], top[:, n, :], score[:, n, :])
                in_turn(last)
                in_turn(nc.vector.tensor_copy(topf[:, :, :], topi[:, :, :]))
                dve.wait_ge(s_iota, 1)
                in_turn(nc.vector.tensor_copy(iota_f[:, :], iota_i[:, :]))
                in_turn(nc.vector.tensor_tensor(eq[:, :, :, :],
                                                topf[:, :, 0:TOPK].unsqueeze(2).to_broadcast([P, NT, E, TOPK]),
                                                iota_f[:, :].unsqueeze(1).unsqueeze(3).to_broadcast([P, NT, E, TOPK]),
                                                ALU.is_equal))
                in_turn(nc.vector.tensor_reduce(chosen[:, :, :], eq[:, :, :, :], AX.X, ALU.max))
                in_turn(nc.vector.tensor_tensor(cw[:, :, :], score[:, :, :], chosen[:, :, :], ALU.mult))
                in_turn(nc.vector.tensor_copy(cws[:, :, 0:E].bitcast(F32R), cw[:, :, :]))
                nc.vector.tensor_tensor(cws[:, :, E:2 * E], cw[:, :, :], cws[:, :, 0:E], ALU.subtract).then_inc(s_cws, 1)
                dve.wait_ge(s_sel, 6)
                nc.vector.tensor_tensor(k.sel[:, :], sel_a[:, :], sel_b[:, :], ALU.add)

            @block.tensor
            def _(pe):
                hold = Hold(pe, b.sem("r_held"))
                pe.wait_ge(s_gwl, 16)
                for c in range(DC):
                    last = nc.tensor.transpose(psW[:, c, :], gw[:, c * P:(c + 1) * P], k.ident[0:E, 0:E])
                last.then_inc(s_gwT, 1)
                pe.wait_ge(s_gwlo, 1)
                with pe.Fori(0, NP) as i:
                    pe.wait_ge(s_lo, seen(i))
                    pe.wait_ge(s_h, 2 * i + 2)
                    for t in range(2):
                        for c in range(DC):
                            last = nc.tensor.transpose(psH[:, c, t * P:(t + 1) * P], h[:, t, c * P:(c + 1) * P],
                                                       k.ident[:, :])
                    last.then_inc(s_hT, 1)
                    pe.wait_ge(s_lo, seen(i + 1))
                    cols = bass.ds(i * 256, 256)
                    for c in range(DC):
                        nc.tensor.matmul(psG[:, :], gwT_lo[:, c, :], k.h_hi[:, c, cols], start=(c == 0), stop=False)
                        nc.tensor.matmul(psG[:, :], gwT_hi[:, c, :], k.h_lo[:, c, cols], start=False, stop=False)
                        last = nc.tensor.matmul(psG[:, :], gwT_hi[:, c, :], k.h_hi[:, c, cols], start=False,
                                                stop=(c == DC - 1))
                    last.then_inc(s_lgT, 1)
                    pe.wait_ge(s_lgTsb, i + 1)
                    pe.wait_ge(s_lgsb, seen(i))
                    hold()
                    for t in range(2):
                        last = nc.tensor.transpose(psL[:, t, :], lgT[:, t * P:(t + 1) * P], k.ident[0:E, 0:E])
                    last.then_inc(s_lg, 1)
                pe.wait_ge(s_cws, 1)
                for n in range(NT):
                    last = nc.tensor.transpose(psC[:, n * P:(n + 1) * P], cws[:, n, :], k.ident[:, :])
                last.then_inc(s_cwT, 1)


def expert_weights_stage(nc, k, e_gate, e_up, e_down):
    UNITS = NCH // 2
    RING = 6
    BANKS = 8
    with ExitStack() as ctx:
        b = Bufs(nc, ctx)
        stage = b.sb("w_stage", [P, RING, 2, 2 * P])
        ps = [b.ps(f"w_ps{n}", [P, 2, 2 * P]) for n in range(BANKS)]
        s_load = [b.sem(f"w_load{n}") for n in range(RING)]
        s_T, s_hi, s_lo = (b.sem("w_" + n) for n in ("T", "hi", "lo"))
        units = [(m, j) for m in range(3) for j in range(UNITS)]
        srcs = []
        for m, j in units:
            if m < 2:
                rows = (e_gate, e_up)[m].rearrange("e f d -> (e f) d")[2 * P * j:2 * P * (j + 1), :]
                srcs.append([(None, rows.rearrange("(c p) d -> p c d", p=P))])
            else:
                parts, col = [], 2 * P * j
                while col < 2 * P * (j + 1):
                    e, f = divmod(col, FE)
                    n = min(FE - f, 2 * P * (j + 1) - col)
                    parts.append(((col - 2 * P * j, n), e_down[e, :, f:f + n].rearrange("(c p) f -> p c f", p=P)))
                    col += n
                srcs.append(parts)
        landed, count = [], [0] * RING
        for u in range(len(units)):
            count[u % RING] += 16 * len(srcs[u])
            landed.append(count[u % RING])

        def targets(u):
            m, j = units[u]
            if m < 2:
                cols = slice(2 * P * j, 2 * P * (j + 1))
                return (k.wg_hi, k.wu_hi)[m][:, :, cols], (k.wg_lo, k.wu_lo)[m][:, :, cols]
            return k.wd_hi[:, 2 * j:2 * j + 2, :], k.wd_lo[:, 2 * j:2 * j + 2, :]

        with nc.Block() as block:
            @block.sync
            def _(sp):
                for u, parts in enumerate(srcs):
                    if u >= RING:
                        sp.wait_ge(s_T, u - RING + 1)
                    for where, src in parts:
                        dst = stage[:, u % RING, :, :] if where is None else \
                            stage[:, u % RING, :, where[0]:where[0] + where[1]]
                        sp.dma_start(dst, src).then_inc(s_load[u % RING], 16)

            @block.tensor
            def _(pe):
                for u, (m, j) in enumerate(units):
                    pe.wait_ge(s_load[u % RING], landed[u])
                    if u >= BANKS:
                        pe.wait_ge(s_lo, u - BANKS + 1)
                    bank = ps[u % BANKS]
                    for ch in range(2):
                        for c in range(DC):
                            if m < 2:
                                out, src = bank[:, c, ch * P:(ch + 1) * P], stage[:, u % RING, ch, c * P:(c + 1) * P]
                            else:
                                out, src = bank[:, ch, c * P:(c + 1) * P], stage[:, u % RING, c, ch * P:(ch + 1) * P]
                            last = nc.tensor.transpose(out, src, k.ident[:, :])
                    last.then_inc(s_T, 1)

            @block.scalar
            def _(act):
                for u in range(len(units)):
                    act.wait_ge(s_T, u + 1)
                    nc.scalar.activation(targets(u)[0], ps[u % BANKS][:, :, :], ACT.Copy).then_inc(s_hi, 1)

            @block.vector
            def _(dve):
                for u in range(len(units)):
                    hi, lo = targets(u)
                    dve.wait_ge(s_hi, u + 1)
                    nc.vector.tensor_tensor(lo, ps[u % BANKS][:, :, :], hi.bitcast(F32), ALU.subtract).then_inc(s_lo, 1)


def experts_stage(nc, k):
    with ExitStack() as ctx:
        b = Bufs(nc, ctx)
        a = [b.sb(f"act{n}", [P, GT]) for n in range(2)]
        a_hi = [b.sb(f"act_hi{n}", [P, GT], F32R) for n in range(2)]
        a_lo = [b.sb(f"act_lo{n}", [P, GT], F32R) for n in range(2)]
        yT = b.sb("yT", [P, DC, GT])
        res = b.sb("res", [P, GT // P, D])
        psG = [b.ps(f"psG{n}", [P, GT]) for n in range(2)]
        psU = [b.ps(f"psU{n}", [P, GT]) for n in range(2)]
        psC = b.ps("psC", [P, GT])
        psY = b.ps("psY", [P, DC, GT])
        psT = b.ps("psT", [P, 2, D])
        (s_gate, s_up, s_cw, s_silu, s_t, s_a, s_hi, s_lo, s_down, s_ysb, s_T, s_out, s_res) = (
            b.sem("e_" + n) for n in ("gate", "up", "cw", "silu", "t", "a", "hi", "lo", "down", "ysb", "T", "out",
                                      "res"))
        LAST = NCH - 1

        with nc.Block() as block:
            @block.sync
            def _(sp):
                x2_v, out_v, tiles = k.x2_dram, k.out_v, GT // P
                sp.dma_start(res[:, :, :], x2_v[:, 0:tiles, :]).then_inc(s_res, 16)
                with sp.Fori(0, NG - 1) as g:
                    sp.wait_ge(s_out, seen(2 * g + 2))
                    sp.dma_start(out_v[:, bass.ds(tiles * g, tiles), :], res[:, :, :]).then_inc(k.stored, 16)
                    sp.wait_ge(k.stored, 16 * g + 16)
                    sp.dma_start(res[:, :, :], x2_v[:, bass.ds(tiles * g + tiles, tiles), :]).then_inc(s_res, 16)
                sp.wait_ge(s_out, seen(2 * NG))
                sp.dma_start(out_v[:, NT - tiles:NT, :], res[:, :, :]).then_inc(k.stored, 16)
                sp.wait_ge(k.stored, 16 * NG)

            @block.tensor
            def _(pe):
                credit(pe, s_gate)
                hold = Hold(pe, b.sem("e_held"))

                def tokens(t, c, g):
                    return t[:, c, g * GT:(g + 1) * GT] if isinstance(g, int) else t[:, c, bass.ds(g * GT, GT)]

                def front(g, s):
                    n = g * NCH + s
                    rows = slice(s * P, (s + 1) * P)
                    first = isinstance(n, int) and n < 2
                    for w_hi, w_lo, ps, free, ready in ((k.wg_hi, k.wg_lo, psG, s_silu, s_gate),
                                                        (k.wu_hi, k.wu_lo, psU, s_t, s_up)):
                        if not first:
                            pe.wait_ge(free, seen(n - 1))
                        for c in range(DC):
                            hh, hl = tokens(k.h_hi, c, g), tokens(k.h_lo, c, g)
                            nc.tensor.matmul(ps[s % 2][:, :], w_lo[:, c, rows], hh, start=(c == 0), stop=False)
                            nc.tensor.matmul(ps[s % 2][:, :], w_hi[:, c, rows], hl, start=False, stop=False)
                            last = nc.tensor.matmul(ps[s % 2][:, :], w_hi[:, c, rows], hh, start=False,
                                                    stop=(c == DC - 1))
                        last.then_inc(ready, 1)
                    pe.wait_ge(s_a, seen(n))
                    hold()
                    cw = k.cwT[:, g * GT:(g + 1) * GT] if isinstance(g, int) else k.cwT[:, bass.ds(g * GT, GT)]
                    nc.tensor.matmul(psC[:, :], k.sel[:, rows], cw, start=True, stop=True).then_inc(s_cw, 1)

                def back(n, s, g):
                    pe.wait_ge(s_lo, seen(n + 1))
                    if s == 0:
                        pe.wait_ge(s_ysb, seen(g))
                    for m in range(DC):
                        cols = slice(m * P, (m + 1) * P)
                        nc.tensor.matmul(psY[:, m, :], k.wd_lo[:, s, cols], a_hi[s % 2][:, :], start=(s == 0),
                                         stop=False)
                        nc.tensor.matmul(psY[:, m, :], k.wd_hi[:, s, cols], a_lo[s % 2][:, :], start=False, stop=False)
                        last = nc.tensor.matmul(psY[:, m, :], k.wd_hi[:, s, cols], a_hi[s % 2][:, :], start=False,
                                                stop=(s == LAST))
                    last.then_inc(s_down, 1)

                def transposed(g, half):
                    pe.wait_ge(s_ysb, seen(g + 1))
                    pe.wait_ge(s_out, seen(2 * g + half))
                    for t in range(2):
                        for m in range(DC):
                            tok = (2 * half + t) * P
                            last = nc.tensor.transpose(psT[:, t, m * P:(m + 1) * P], yT[:, m, tok:tok + P],
                                                       k.ident[:, :])
                    last.then_inc(s_T, 1)

                def turn(g, before):
                    for s in range(NCH):
                        front(g, s)
                        if s > 0:
                            back(g * NCH + s - 1, s - 1, g)
                        elif before:
                            back(g * NCH - 1, LAST, g)
                        if before and s in (1, 2):
                            transposed(g - 1, s - 1)

                turn(0, False)
                with pe.Fori(1, NG) as g:
                    turn(g, True)
                back(NG * NCH - 1, LAST, NG - 1)
                for half in range(2):
                    transposed(NG - 1, half)

            @block.scalar
            def _(act):
                nc.scalar.preload_act_table(ACT.Silu)
                credit(act, s_silu, s_ysb)

                def silu(n, s):
                    act.wait_ge(s_gate, seen(n + 1))
                    if not (isinstance(n, int) and n < 2):
                        act.wait_ge(s_lo, seen(n - 1))
                    nc.scalar.activation(a[s % 2][:, :], psG[s % 2][:, :], ACT.Silu).then_inc(s_silu, 1)

                def high(n, s):
                    act.wait_ge(s_a, seen(n + 1))
                    if not (isinstance(n, int) and n < 2):
                        act.wait_ge(s_down, n - 1)
                    nc.scalar.activation(a_hi[s % 2][:, :], a[s % 2][:, :], ACT.Copy).then_inc(s_hi, 1)

                def sums_out(g):
                    act.wait_ge(s_down, (g + 1) * NCH)
                    if not isinstance(g, int) or g > 0:
                        act.wait_ge(s_T, 2 * g)
                    nc.scalar.activation(yT[:, :, :], psY[:, :, :], ACT.Copy).then_inc(s_ysb, 1)

                def turn(g, before):
                    for s in range(NCH):
                        n = g * NCH + s
                        silu(n, s)
                        if before and s == 0:
                            sums_out(g - 1)
                        high(n, s)

                turn(0, False)
                with act.Fori(1, NG) as g:
                    turn(g, True)
                sums_out(NG - 1)

            @block.vector
            def _(dve):
                credit(dve, s_t, s_a, s_lo, s_out)

                def middle(n, s):
                    dve.wait_ge(s_silu, seen(n + 1))
                    dve.wait_ge(s_up, n + 1)
                    nc.vector.tensor_tensor(a[s % 2][:, :], psU[s % 2][:, :], a[s % 2][:, :], ALU.mult).then_inc(s_t, 1)
                    dve.wait_ge(s_t, seen(n + 1))
                    dve.wait_ge(s_cw, n + 1)
                    nc.vector.tensor_tensor(a[s % 2][:, :], psC[:, :], a[s % 2][:, :], ALU.mult).then_inc(s_a, 1)
                    dve.wait_ge(s_hi, n + 1)
                    nc.vector.tensor_tensor(a_lo[s % 2][:, :], a[s % 2][:, :], a_hi[s % 2][:, :].bitcast(F32),
                                            ALU.subtract).then_inc(s_lo, 1)

                def output(g, half):
                    dve.wait_ge(s_T, 2 * g + half + 1)
                    dve.wait_ge(s_res, 16 * g + 16)
                    rows = res[:, 2 * half:2 * half + 2, :]
                    nc.vector.tensor_tensor(rows, psT[:, :, :], rows, ALU.add).then_inc(s_out, 1)

                def turn(g, before):
                    for s in range(NCH):
                        middle(g * NCH + s, s)
                        if before and s in (1, 2):
                            output(g - 1, s - 1)

                turn(0, False)
                with dve.Fori(1, NG) as g:
                    turn(g, True)
                for half in range(2):
                    output(NG - 1, half)


class Kept:
    pass


def build(nc, x, ctx_in, Wq, Wkv, Wout, w_gate, g_gate, w_down, g_down, gate_w, e_gate, e_up, e_down, out):
    k = Kept()
    with ExitStack() as ctx:
        b = Bufs(nc, ctx)
        k.ident = b.sb("ident", [P, P])
        k.identb = b.sb("identb", [P, P], BF16)
        k.minus_half = b.sb("minus_half", [P, NT])
        k.x_loaded = b.sem("x_loaded")
        k.ctx_loaded = b.sem("ctx_loaded")
        k.bit_loaded = b.sem("bit_loaded")
        k.x2_spilled = b.sem("x2_spilled")
        k.stored = b.sem("stored")
        k.h_hi, k.h_lo = (b.sb(f"h3T_{p}", [P, DC, T], F32R) for p in ("hi", "lo"))
        k.cwT = b.sb("cwT", [2 * E, T], F32R)
        k.sel = b.sb("sel", [2 * E, NCH * P], F32R)
        with ExitStack() as xctx:
            xb = Bufs(nc, xctx)
            k.x = xb.sb("x_tok", [P, NT, D])
            k.ones = xb.sb("ones", [P, P])
            k.wg_nat = xb.sb("wg_nat", [P, 2 * INNER // P, D])
            k.wd_nat = xb.sb("wd_nat", [P, DC, INNER])
            k.g_in = xb.sb("g_in", [P, D])
            k.g_hid = xb.sb("g_hid", [P, INNER])
            k.bit_weights = (w_gate, w_down, g_gate, g_down)
            with ExitStack() as actx:
                a = Bufs(nc, actx)
                k.ctx = a.sb("ctx_tok", [P, NT, L])
                k.causal = a.sb("causal", [P, HPC, S], BF16)
                k.headmask = a.sb("headmask", [P, HPC])
                k.vmask = a.sb("vmask", [P, NH // 2, 2, HD])
                k.wqT_hi, k.wqT_lo = (a.sb(f"wqT_{p}", [P, DC, D], F32R) for p in ("hi", "lo"))
                k.woT_hi, k.woT_lo = (a.sb(f"woT_{p}", [P, DC, D], F32R) for p in ("hi", "lo"))
                k.wkvT_hi, k.wkvT_lo = (a.sb(f"wkvT_{p}", [L, 2 * D], F32R) for p in ("hi", "lo"))
                setup_stage(nc, k, Wq, Wkv, Wout, x, ctx_in)
                attention_stage(nc, k)
            with ExitStack() as bctx:
                a = Bufs(nc, bctx)
                k.wgT = a.sb("wgT", [P, DC, 2 * INNER], BF16)
                k.wdT = a.sb("wdT", [P, IC, D], BF16)
                k.wmean = a.sb("wmean", [P, 2])
                k.mv = a.sb("mv_all", [P, NT, 2])
                k.norm = a.sb("norm_all", [P, NT])
                k.norm1 = lambda n: k.norm[:, n:n + 1] if isinstance(n, int) else k.norm[:, bass.ds(n, 1)]
                quantise_stage(nc, k)
                bitlinear_stage(nc, k)
            k.out_v = out.rearrange("b s d -> (b s) d").rearrange("(n p) d -> p n d", p=P)
            k.x2_dram = nc.dram_tensor("x2_spill", [P, NT, D], F32, kind="Internal").ap()
            route_stage(nc, k, gate_w)
        with ExitStack() as ectx:
            a = Bufs(nc, ectx)
            k.wg_hi, k.wg_lo, k.wu_hi, k.wu_lo = (a.sb(n, [P, DC, E * FE], F32R) for n in (
                "wg_hi", "wg_lo", "wu_hi", "wu_lo"))
            k.wd_hi, k.wd_lo = (a.sb(n, [P, NCH, D], F32R) for n in ("wd_hi", "wd_lo"))
            expert_weights_stage(nc, k, e_gate, e_up, e_down)
            experts_stage(nc, k)


_INS = ["x", "ctx_512", "L0_xattn_Wq", "L0_xattn_Wkv_expand", "L0_xattn_Wout", "L0_attn_w_gate", "L0_attn_g_gate",
        "L0_attn_w_down", "L0_attn_g_down", "L0_ffn_gate_w", "L0_ffn_w_gate", "L0_ffn_w_up", "L0_ffn_w_down"]


def kernel(**inputs):
    import numpy as _np
    import concourse.bacc as _bacc
    from concourse import mybir as _mybir
    from concourse.bass_utils import run_bass_kernel_spmd as _run

    nc = _bacc.Bacc("TRN2", target_bir_lowering=False, num_devices=1)
    arrays, args = {}, []
    for name in _INS:
        a = _np.ascontiguousarray(inputs[name])
        arrays[f"in_{name}_dram"] = a
        args.append(nc.dram_tensor(f"in_{name}_dram", a.shape, _mybir.dt.from_np(a.dtype), kind="ExternalInput").ap())
    args.append(nc.dram_tensor("out_0_dram", (B, S, D), _mybir.dt.float32, kind="ExternalOutput").ap())
    build(nc, *args)
    r = _run(nc, [arrays], core_ids=[0])
    return r.results[0]["out_0_dram"]
```

```python
from contextlib import ExitStack

import numpy as np

import concourse.bass as bass
from concourse import mybir

P = 128
F32 = mybir.dt.float32
F32R = mybir.dt.float32r
BF16 = mybir.dt.bfloat16
U32 = mybir.dt.uint32
ALU = mybir.AluOpType
ACT = mybir.ActivationFunctionType
AX = mybir.AxisListType

B, S, D = 32, 64, 256
SKV, L = 1601, 64
NH = 16
HD = D // NH
INNER = 1024
E, FE, TOPK = 16, 176, 6
T = B * S
NT = T // P
NP = NT // 2
DC = D // P
EPS = 1e-5
ROUND = 1.5 * 2.0 ** 23
MASKED = -1.0e30

HPC = P // HD
NCH = E * FE // P
GT = 512
NG = T // GT
IC = INNER // P


def seen(n):
    return max(n, 0) + 1 if isinstance(n, int) else n + 1


class Bufs:

    def __init__(self, nc, ctx):
        self.nc, self.ctx = nc, ctx

    def sb(self, name, shape, dt=F32):
        return self.ctx.enter_context(self.nc.sbuf_tensor(name, shape, dt))

    def ps(self, name, shape, dt=F32):
        return self.ctx.enter_context(self.nc.psum_tensor(name, shape, dt))

    def sem(self, name):
        return self.ctx.enter_context(self.nc.semaphore(name))


class Hold:

    def __init__(self, eng, sem):
        self.eng, self.sem = eng, sem

    def __call__(self):
        self.eng.nop().then_inc(self.sem, 1)


def credit(eng, *sems):
    for s in sems:
        eng.nop().then_inc(s, 1)


def setup_stage(nc, k, Wq, Wkv, Wout, x, ctx_in):
    with ExitStack() as ctx:
        b = Bufs(nc, ctx)
        wq = b.sb("wq_nat", [P, DC, D])
        wkv = b.sb("wkv_nat", [P, 2 * D // P, L])
        wo = b.sb("wo_nat", [P, DC, D])
        psQ = b.ps("psWq", [P, DC, D])
        psO = b.ps("psWo", [P, DC, D])
        psKV = b.ps("psWkv", [L, 2 * D])
        zeroed = b.sem("zeroed")
        ident_ready = b.sem("ident_ready")
        w_loaded = b.sem("w_loaded")
        wT_ready = b.sem("wT_ready")
        wT_hi_ready = b.sem("wT_hi_ready")

        with nc.Block() as block:
            @block.sync
            def _(sp):
                x_v = x.rearrange("b s d -> (b s) d").rearrange("(n p) d -> p n d", p=P)
                sp.dma_start(k.x[:, 0:2, :], x_v[:, 0:2, :]).then_inc(k.x_loaded[0], 16)
                sp.dma_start(wq[:, :, :], Wq.rearrange("(c p) i -> p c i", p=P)).then_inc(w_loaded, 16)
                sp.dma_start(wo[:, :, :], Wout.rearrange("(c p) i -> p c i", p=P)).then_inc(w_loaded, 16)
                sp.dma_start(wkv[:, :, :], Wkv.rearrange("(c p) i -> p c i", p=P)).then_inc(w_loaded, 16)
                sp.dma_start(k.x[:, 2:NT, :], x_v[:, 2:NT, :]).then_inc(k.x_loaded[1], 16)
                w_gate, w_down, g_gate, g_down = k.bit_weights
                sp.dma_start(k.wg_nat[:, :, :], w_gate.rearrange("(c p) i -> p c i", p=P)).then_inc(k.bit_loaded, 16)
                sp.dma_start(k.wd_nat[:, :, :], w_down.rearrange("(c p) i -> p c i", p=P)).then_inc(k.bit_loaded, 16)
                sp.dma_start(k.g_in[:, :], g_gate.unsqueeze(0).to_broadcast([P, D])).then_inc(k.bit_loaded, 16)
                sp.dma_start(k.g_hid[:, :], g_down.unsqueeze(0).to_broadcast([P, INNER])).then_inc(k.bit_loaded, 16)

            @block.gpsimd
            def _(pool):
                step = [0]

                def in_turn(ins):
                    ins.then_inc(zeroed, 1)
                    step[0] += 1
                    pool.wait_ge(zeroed, step[0])

                in_turn(nc.gpsimd.memset(k.ident[:, :], 0.0))
                nc.gpsimd.affine_select(out=k.ident[:, :], in_=k.ident[:, :], compare_op=ALU.not_equal, fill=1.0,
                                        base=0, pattern=[[-1, P]], channel_multiplier=1).then_inc(ident_ready, 1)
                pool.wait_ge(ident_ready, 1)
                in_turn(nc.gpsimd.memset(k.causal[:, :, :], 0.0))
                for half in range(2):
                    rows = k.causal[half * S:(half + 1) * S, :, :]
                    in_turn(nc.gpsimd.affine_select(out=rows, in_=rows, compare_op=ALU.is_ge, fill=MASKED, base=0,
                                                    pattern=[[0, HPC], [-1, S]], channel_multiplier=1))
                in_turn(nc.gpsimd.memset(k.headmask[:, :], 1.0))
                in_turn(nc.gpsimd.affine_select(out=k.headmask[:, :], in_=k.headmask[:, :], compare_op=ALU.is_ge,
                                                fill=0.0, base=0, pattern=[[-HD, HPC]], channel_multiplier=1))
                in_turn(nc.gpsimd.affine_select(out=k.headmask[:, :], in_=k.headmask[:, :], compare_op=ALU.is_ge,
                                                fill=0.0, base=HD - 1, pattern=[[HD, HPC]], channel_multiplier=-1))

            @block.scalar
            def _(act):
                ctx_v = ctx_in.rearrange("(n b) s l -> b s n l", b=2)
                nc.scalar.preload_act_table(ACT.Exp)
                for half in range(2):
                    act.dma_start(k.ctx[half * S:(half + 1) * S, :, :], ctx_v[half, 0:S, :, :]).then_inc(k.ctx_loaded, 16)
                act.wait_ge(wT_ready, 1)
                nc.scalar.activation(k.wqT_hi[:, :, :], psQ[:, :, :], ACT.Copy).then_inc(wT_hi_ready, 1)
                act.wait_ge(wT_ready, 2)
                nc.scalar.activation(k.woT_hi[:, :, :], psO[:, :, :], ACT.Copy).then_inc(wT_hi_ready, 1)
                act.wait_ge(wT_ready, 3)
                nc.scalar.activation(k.wkvT_hi[:, :], psKV[:, :], ACT.Copy).then_inc(wT_hi_ready, 1)

            @block.vector
            def _(dve):
                for half in range(2):
                    nc.vector.memset(k.vmask[half * S:(half + 1) * S, :, half, :], 1.0)
                    nc.vector.memset(k.vmask[half * S:(half + 1) * S, :, 1 - half, :], 0.0)
                nc.vector.memset(k.minus_half[:, :], -0.5)
                nc.vector.memset(k.ones[:, :], 1.0)
                dve.wait_ge(ident_ready, 1)
                nc.vector.tensor_copy(k.identb[:, :], k.ident[:, :])
                for n, (lo, ps, hi) in enumerate(((k.wqT_lo[:, :, :], psQ[:, :, :], k.wqT_hi[:, :, :]),
                                                  (k.woT_lo[:, :, :], psO[:, :, :], k.woT_hi[:, :, :]),
                                                  (k.wkvT_lo[:, :], psKV[:, :], k.wkvT_hi[:, :]))):
                    dve.wait_ge(wT_hi_ready, n + 1)
                    nc.vector.tensor_tensor(lo, ps, hi.bitcast(F32), ALU.subtract)

            @block.tensor
            def _(pe):
                pe.wait_ge(ident_ready, 1)
                pe.wait_ge(w_loaded, 48)
                for w, ps in ((wq, psQ), (wo, psO)):
                    for oc in range(DC):
                        for ic in range(DC):
                            last = nc.tensor.transpose(ps[:, ic, oc * P:(oc + 1) * P], w[:, oc, ic * P:(ic + 1) * P],
                                                       k.ident[:, :])
                    last.then_inc(wT_ready, 1)
                for oc in range(2 * D // P):
                    last = nc.tensor.transpose(psKV[:, oc * P:(oc + 1) * P], wkv[:, oc, :], k.ident[:, :])
                last.then_inc(wT_ready, 1)


def at(t3, n, count=1):
    return t3[:, n:n + count, :] if isinstance(n, int) else t3[:, bass.ds(n, count), :]


def attention_stage(nc, k):
    with ExitStack() as ctx:
        b = Bufs(nc, ctx)
        W2 = 2 * P
        stats = b.sb("stats", [P, 2, 6])
        mv = b.sb("mv", [P, 2, 2])
        veps = b.sb("veps", [P, 2])
        rstd = b.sb("rstd", [P, 2])
        h = b.sb("h", [P, 2, D])
        cpair = b.sb("cpair", [P, 2, L])
        hT_hi = b.sb("hT_hi", [P, DC, W2], F32R)
        hT_lo = b.sb("hT_lo", [P, DC, W2], F32R)
        cT_hi = b.sb("cT_hi", [L, 2, 4, 2, S], F32R)
        cT_lo = b.sb("cT_lo", [L, 2, 4, 2, S], F32R)
        q_sb = b.sb("q_sb", [P, 2, DC, W2])
        kbd = b.sb("kbd", [P, 2, DC, HPC, W2])
        vbd = b.sb("vbd", [P, 2, 4, D])
        sub = b.sb("sub", [P, 2, HPC, S])
        mx = b.sb("mx", [P, 2, HPC])
        prob = b.sb("prob", [P, 4, HPC, S])
        rsum = b.sb("rsum", [P, 4, HPC])
        rinv = b.sb("rinv", [P, 4, HPC])
        probn = b.sb("probn", [P, 2, 4, HPC * S])
        pT = b.sb("pT", [P, 2, 4, P])
        oT_hi = b.sb("oT_hi", [P, DC, W2], F32R)
        oT_lo = b.sb("oT_lo", [P, DC, W2], F32R)

        R0 = b.ps("R0", [P, 2, 256])
        R1 = b.ps("R1", [P, 2, 256])
        R2 = b.ps("R2", [P, 2, 256])
        psS = [b.ps(f"psS{u}", [P, 512]) for u in range(2)]
        psT = [b.ps(f"psT{u}", [P, 4, P]) for u in range(2)]
        psO = b.ps("psO", [P, DC, W2])

        s_stats, s_mv, s_veps, s_rstd, s_h = (b.sem(n) for n in ("a_stats", "a_mv", "a_veps", "a_rstd", "a_h"))
        s_hT, s_cT, s_hThi, s_cThi, s_hTlo, s_cTlo = (b.sem(n) for n in (
            "a_hT", "a_cT", "a_hThi", "a_cThi", "a_hTlo", "a_cTlo"))
        s_ctxpair = b.sem("a_ctxpair")
        s_q, s_k, s_v01, s_v23 = (b.sem(n) for n in ("a_q", "a_k", "a_v01", "a_v23"))
        s_qsb, s_kbd, s_vbd01, s_vbd23 = (b.sem(n) for n in ("a_qsb", "a_kbd", "a_vbd01", "a_vbd23"))
        s_score, s_mx, s_sub, s_prob, s_rsum, s_rinv, s_probn = (b.sem(n) for n in (
            "a_score", "a_mx", "a_sub", "a_prob", "a_rsum", "a_rinv", "a_probn"))
        s_pT, s_pTsb, s_pv = (b.sem(n) for n in ("a_pT", "a_pTsb", "a_pv"))
        s_oThi, s_oTlo, s_out, s_x1 = (b.sem(n) for n in ("a_oThi", "a_oTlo", "a_out", "a_x1"))

        def all_turns(eng, turn):
            turn(0, 0, True, False, False)
            turn(1, 1, True, True, False)
            with eng.Fori(0, NP // 2 - 2) as g:
                turn(2 * g + 2, 0, True, True, True)
                turn(2 * g + 3, 1, True, True, True)
            turn(NP - 2, 0, True, True, True)
            turn(NP - 1, 1, True, True, True)
            turn(NP, 0, False, True, True)
            turn(NP + 1, 1, False, False, True)

        asum = b.sb("asum", [P, 2])
        wrec = b.sb("wrec", [P, 2])
        s_asum, s_wsum, s_wmean, s_wrec, s_tern = (b.sem("a_" + n) for n in ("asum", "wsum", "wmean", "wrec", "tern"))

        with nc.Block() as block:
            @block.vector
            def _(dve):
                credit(dve, s_stats, s_mv, s_h, s_hTlo, s_cTlo, s_vbd01, s_vbd23, s_mx, s_sub, s_rsum, s_rinv,
                       s_oTlo, s_x1)
                hold = Hold(dve, b.sem("a_held_dve"))

                def statistics(i):
                    for t in range(2):
                        nc.vector.bn_stats(stats[:, t, :], at(k.x, 2 * i + t)).then_inc(s_stats, 1)
                    dve.wait_ge(s_stats, seen(2 * i + 2))
                    hold()
                    for t in range(2):
                        nc.vector.bn_aggr(mv[:, t, :], stats[:, t, :]).then_inc(s_mv, 1)

                def normalised(i):
                    dve.wait_ge(s_mv, seen(2 * i + 2))
                    dve.wait_ge(s_rstd, seen(i + 1))
                    dve.wait_ge(s_hT, seen(i))
                    for t in range(2):
                        nc.vector.tensor_scalar(h[:, t:t + 1, :], at(k.x, 2 * i + t), mv[:, t, 0:1],
                                                rstd[:, t:t + 1], ALU.subtract, ALU.mult).then_inc(s_h, 1)

                def low_parts(i, par):
                    dve.wait_ge(s_hThi, seen(i + 1))
                    dve.wait_ge(s_q, seen(i))
                    nc.vector.tensor_tensor(hT_lo[:, :, :], R0[:, :, :], hT_hi[:, :, :].bitcast(F32),
                                            ALU.subtract).then_inc(s_hTlo, 1)
                    dve.wait_ge(s_cThi, seen(i + 1))
                    dve.wait_ge(s_v23, seen(i - 1))
                    cps = R1[0:L, 0, :].rearrange("p (b s) -> p b s", b=4)
                    for dup in range(2):
                        last = nc.vector.tensor_tensor(cT_lo[:, par, :, dup, :], cps,
                                                       cT_hi[:, par, :, dup, :].bitcast(F32), ALU.subtract)
                    last.then_inc(s_cTlo, 1)

                def values(j, par, half):
                    ps, ready, done = ((R1, s_v01, s_vbd01), (R2, s_v23, s_vbd23))[half]
                    dve.wait_ge(ready, seen(j + 1))
                    dve.wait_ge(s_pv, seen(4 * j - 4))
                    nc.vector.tensor_tensor(vbd[:, par, 2 * half:2 * half + 2, :], ps[:, :, :], k.vmask2, ALU.mult
                                            ).then_inc(done, 1)

                def shifted(j, u):
                    n = 4 * j + u
                    r = u % 2
                    dve.wait_ge(s_score, seen(n + 1))
                    sc = psS[r][:, :].rearrange("p (h s) -> p h s", h=HPC)
                    nc.vector.tensor_reduce(mx[:, r, :], sc, AX.X, ALU.max).then_inc(s_mx, 1)
                    dve.wait_ge(s_mx, seen(n + 1))
                    dve.wait_ge(s_prob, seen(n - 1))
                    nc.vector.tensor_tensor(sub[:, r, :, :], sc, mx[:, r, :].unsqueeze(2).to_broadcast([P, HPC, S]),
                                            ALU.subtract).then_inc(s_sub, 1)

                def sums(j, u):
                    n = 4 * j + u
                    dve.wait_ge(s_prob, seen(n + 1))
                    nc.vector.tensor_reduce(rsum[:, u, :], prob[:, u, :, :], AX.X, ALU.add).then_inc(s_rsum, 1)
                    dve.wait_ge(s_rsum, seen(n + 1))
                    dve.wait_ge(s_probn, seen(n - 3))
                    nc.vector.reciprocal(rinv[:, u, :], rsum[:, u, :]).then_inc(s_rinv, 1)

                def out_low(j):
                    dve.wait_ge(s_oThi, seen(j + 1))
                    dve.wait_ge(s_out, seen(j))
                    nc.vector.tensor_tensor(oT_lo[:, :, :], psO[:, :, :], oT_hi[:, :, :].bitcast(F32),
                                            ALU.subtract).then_inc(s_oTlo, 1)

                def residual(j):
                    dve.wait_ge(s_out, seen(j + 1))
                    nc.vector.tensor_tensor(at(k.x, 2 * j, 2), psO[:, :, :], at(k.x, 2 * j, 2), ALU.add
                                            ).then_inc(s_x1, 1)
                    dve.wait_ge(s_x1, seen(j + 1))
                    for t in range(2):
                        nc.vector.bn_stats(at(k.xstats, 2 * j + t)[:, 0, :], at(k.x, 2 * j + t)[:, 0, :])

                def weight_means():
                    dve.wait_ge(s_wsum, 1)
                    for n, count in enumerate((2 * INNER * D, D * INNER)):
                        nc.vector.tensor_scalar(k.wmean[:, n:n + 1], psT[0][:, 0, n:n + 1], 1.0 / count, 1e-5, ALU.mult,
                                                ALU.max).then_inc(s_wmean, 1)
                    dve.wait_ge(s_wmean, 2)
                    nc.vector.reciprocal(wrec[:, :], k.wmean[:, :]).then_inc(s_wrec, 1)

                def turn(i, par, one, two, three):
                    more = one and not (isinstance(i, int) and i == NP - 1)
                    if one:
                        low_parts(i, par)
                    if two:
                        shifted(i - 1, 0)
                        shifted(i - 1, 1)
                        sums(i - 1, 0)
                    if more:
                        statistics(i + 1)
                    if two:
                        shifted(i - 1, 2)
                        sums(i - 1, 1)
                        values(i - 1, 1 - par, 0)
                        values(i - 1, 1 - par, 1)
                        shifted(i - 1, 3)
                    if three:
                        out_low(i - 2)
                    if more:
                        normalised(i + 1)
                    if two:
                        sums(i - 1, 2)
                        sums(i - 1, 3)
                    if two and not three and one:
                        weight_means()
                    if three:
                        residual(i - 2)

                dve.wait_ge(k.x_loaded[0], 16)
                statistics(0)
                normalised(0)
                dve.wait_ge(k.x_loaded[1], 16)
                all_turns(dve, turn)

            @block.gpsimd
            def _(pool):
                credit(pool, s_veps, s_rstd, s_ctxpair, s_probn)
                hold = Hold(pool, b.sem("a_held_pool"))

                def context(i):
                    pool.wait_ge(s_cT, seen(i))
                    hold()
                    nc.gpsimd.tensor_copy(cpair[:, :, :], at(k.ctx, 2 * i, 2)).then_inc(s_ctxpair, 1)

                def inv_std(i):
                    pool.wait_ge(s_mv, seen(2 * i + 2))
                    pool.wait_ge(s_h, seen(2 * i))
                    hold()
                    nc.gpsimd.tensor_scalar(veps[:, :], mv[:, :, 1], EPS, None, ALU.add).then_inc(s_veps, 1)
                    pool.wait_ge(s_veps, seen(i + 1))
                    nc.gpsimd.tensor_tensor(rstd[:, :], veps[:, :], k.minus_half[:, 0:2], ALU.pow).then_inc(s_rstd, 1)

                def quotient(j, u, par):
                    n = 4 * j + u
                    pool.wait_ge(s_rinv, seen(n + 1))
                    if u == 0:
                        pool.wait_ge(s_pT, seen(4 * j - 4))
                    nc.gpsimd.tensor_tensor(probn[:, par, u, :].rearrange("p (h s) -> p h s", h=HPC),
                                            prob[:, u, :, :], rinv[:, u, :].unsqueeze(2).to_broadcast([P, HPC, S]),
                                            ALU.mult).then_inc(s_probn, 1)

                TERNARY_TURNS = (1, NP - 2, NP - 1, NP)

                def ternary(j, n):
                    part = (slice(None), slice(4 * j, 4 * j + 4), slice(None)) if n == 0 else \
                        (slice(None), slice(None), slice(2 * P * j, 2 * P * (j + 1)))
                    w, q = ((k.wg_nat, k.wgq), (k.wd_nat, k.wdq))[n]
                    w, q = w[part], q[part]
                    first = 6 * j + 3 * n
                    pool.wait_ge(s_wrec, 1)
                    nc.gpsimd.tensor_scalar(w, w, wrec[:, n:n + 1], ROUND, ALU.mult, ALU.add).then_inc(s_tern, 1)
                    pool.wait_ge(s_tern, first + 1)
                    nc.gpsimd.tensor_scalar(w, w, -ROUND, 1.0, ALU.add, ALU.mult).then_inc(s_tern, 1)
                    pool.wait_ge(s_tern, first + 2)
                    nc.gpsimd.tensor_scalar(q, w, 1.0, -1.0, ALU.min, ALU.max).then_inc(s_tern, 1)

                def turn(i, par, one, two, three):
                    if one and not (isinstance(i, int) and i == NP - 1):
                        context(i + 1)
                    if two:
                        quotient(i - 1, 0, 1 - par)
                    if one and not (isinstance(i, int) and i == NP - 1):
                        inv_std(i + 1)
                    if two:
                        for u in range(1, 4):
                            quotient(i - 1, u, 1 - par)
                    if isinstance(i, int) and i in TERNARY_TURNS:
                        for n in range(2):
                            ternary(TERNARY_TURNS.index(i), n)

                pool.wait_ge(k.ctx_loaded, 32)
                context(0)
                inv_std(0)
                all_turns(pool, turn)

            @block.scalar
            def _(act):
                nc.scalar.preload_act_table(ACT.Exp)
                credit(act, s_hThi, s_cThi, s_qsb, s_kbd, s_prob, s_pTsb, s_oThi)

                def high_parts(i, par):
                    act.wait_ge(s_hT, seen(i + 1))
                    act.wait_ge(s_q, seen(i))
                    nc.scalar.activation(hT_hi[:, :, :], R0[:, :, :], ACT.Copy).then_inc(s_hThi, 1)
                    act.wait_ge(s_cT, seen(i + 1))
                    act.wait_ge(s_v23, seen(i - 1))
                    cps = R1[0:L, 0, :].rearrange("p (b s) -> p b s", b=4)
                    for dup in range(2):
                        last = nc.scalar.activation(cT_hi[:, par, :, dup, :], cps, ACT.Copy)
                    last.then_inc(s_cThi, 1)

                def queries(i, par):
                    act.wait_ge(s_q, seen(i + 1))
                    act.wait_ge(s_score, seen(4 * i - 4))
                    nc.scalar.activation(q_sb[:, par, :, :], R2[:, :, :], ACT.Copy).then_inc(s_qsb, 1)

                def keys(i, par, first, end):
                    if first == 0:
                        act.wait_ge(s_k, seen(i + 1))
                    for hh in range(first, end):
                        last = nc.scalar.activation(kbd[:, par, :, hh, :], R0[:, :, :], ACT.Copy,
                                                    scale=k.headmask[:, hh:hh + 1])
                    if end == HPC:
                        last.then_inc(s_kbd, 1)

                def exps(j, u):
                    n = 4 * j + u
                    act.wait_ge(s_sub, seen(n + 1))
                    act.wait_ge(s_probn, seen(n - 3))
                    nc.scalar.activation(prob[:, u, :, :], sub[:, u % 2, :, :], ACT.Exp,
                                         scale=float(HD) ** -0.5).then_inc(s_prob, 1)

                def probs_out(j, u):
                    n = 4 * j + u
                    act.wait_ge(s_pT, seen(n + 1))
                    act.wait_ge(s_pv, seen(n - 1))
                    nc.scalar.activation(pT[:, u % 2, :, :], psT[u % 2][:, :, :], ACT.Copy).then_inc(s_pTsb, 1)

                def out_high(j):
                    act.wait_ge(s_pv, seen(4 * j + 4))
                    act.wait_ge(s_out, seen(j))
                    nc.scalar.activation(oT_hi[:, :, :], psO[:, :, :], ACT.Copy).then_inc(s_oThi, 1)

                def weight_sums(n):
                    act.wait_ge(k.bit_loaded, 64)
                    w, scratch = ((k.wg_nat, k.wgq), (k.wd_nat, k.wdq))[n]
                    nc.scalar.activation(scratch[:, :, :], w[:, :, :], ACT.Abs,
                                         accum_out=asum[:, n:n + 1]).then_inc(s_asum, 1)

                def turn(i, par, one, two, three):
                    if one:
                        high_parts(i, par)
                    if three:
                        probs_out(i - 2, 0)
                    if two:
                        exps(i - 1, 0)
                    if three:
                        probs_out(i - 2, 1)
                    if two:
                        exps(i - 1, 1)
                    if three:
                        probs_out(i - 2, 2)
                    if one:
                        if not two:
                            weight_sums(0)
                        queries(i, par)
                        keys(i, par, 0, HPC // 2)
                    if three:
                        probs_out(i - 2, 3)
                    if two:
                        exps(i - 1, 2)
                    if one:
                        keys(i, par, HPC // 2, 3 * HPC // 4)
                    if three:
                        out_high(i - 2)
                    if one:
                        keys(i, par, 3 * HPC // 4, HPC)
                        if not two:
                            weight_sums(1)
                    if two:
                        exps(i - 1, 3)

                all_turns(act, turn)

            @block.tensor
            def _(pe):
                credit(pe, s_hT, s_cT, s_q, s_k, s_v01, s_v23, s_score, s_pT, s_pv, s_out)
                hold = Hold(pe, b.sem("a_held_pe"))

                def three_products(out, parts):
                    for c, (lh, ll, rh, rl) in enumerate(parts):
                        nc.tensor.matmul(out, ll, rh, start=(c == 0), stop=False)
                        nc.tensor.matmul(out, lh, rl, start=False, stop=False)
                        last = nc.tensor.matmul(out, lh, rh, start=False, stop=(c == len(parts) - 1))
                    return last

                def transposes(i, par):
                    pe.wait_ge(s_kbd, seen(i))
                    for t in range(2):
                        pe.wait_ge(s_h, seen(2 * i + t + 1))
                        for c in range(DC):
                            last = nc.tensor.transpose(R0[:, c, t * P:(t + 1) * P], h[:, t, c * P:(c + 1) * P],
                                                       k.ident[:, :])
                    last.then_inc(s_hT, 1)
                    pe.wait_ge(s_vbd01, seen(i - 1))
                    pe.wait_ge(s_ctxpair, seen(i + 1))
                    hold()
                    for t in range(2):
                        last = nc.tensor.transpose(R1[0:L, 0, t * P:(t + 1) * P], cpair[:, t, :], k.ident[:, :])
                    last.then_inc(s_cT, 1)

                def queries_keys(i, par):
                    pe.wait_ge(s_hTlo, seen(i + 1))
                    pe.wait_ge(s_vbd23, seen(i - 1))
                    for m in range(DC):
                        cols = slice(m * P, (m + 1) * P)
                        last = three_products(R2[:, m, :], [(k.wqT_hi[:, c, cols], k.wqT_lo[:, c, cols],
                                                             hT_hi[:, c, :], hT_lo[:, c, :]) for c in range(DC)])
                    last.then_inc(s_q, 1)
                    pe.wait_ge(s_cTlo, seen(i + 1))
                    for m in range(DC):
                        cols = slice(m * P, (m + 1) * P)
                        last = three_products(R0[:, m, :].rearrange("p (b s) -> p b s", b=4),
                                              [(k.wkvT_hi[:, cols], k.wkvT_lo[:, cols], cT_hi[:, par, :, 0, :],
                                                cT_lo[:, par, :, 0, :])])
                    last.then_inc(s_k, 1)

                def values(j, par, half):
                    ps, ready = ((R1, s_v01), (R2, s_v23))[half]
                    for bb in range(2):
                        bt = 2 * half + bb
                        hi = cT_hi[:, par, bt, :, :].rearrange("p a s -> p (a s)")
                        lo = cT_lo[:, par, bt, :, :].rearrange("p a s -> p (a s)")
                        last = three_products(ps[:, bb, :], [(hi, lo, k.wkvT_hi[:, D:2 * D], k.wkvT_lo[:, D:2 * D])])
                    last.then_inc(ready, 1)

                def scores(j, u, par):
                    n = 4 * j + u
                    t, m = u // 2, u % 2
                    if u == 0:
                        pe.wait_ge(s_qsb, seen(j + 1))
                        pe.wait_ge(s_kbd, seen(j + 1))
                    pe.wait_ge(s_sub, seen(n - 1))
                    nc.tensor.matmul(psS[m][:, :], k.identb[:, :], k.causal[:, :, :].rearrange("p h s -> p (h s)"),
                                     start=True, stop=True, skip_group_check=True)
                    for bb in range(2):
                        tok = slice(t * P + bb * S, t * P + (bb + 1) * S)
                        last = nc.tensor.matmul(psS[m][bb * S:(bb + 1) * S, :].rearrange("p (h s) -> p h s", h=HPC),
                                                q_sb[:, par, m, tok], kbd[:, par, m, :, tok], start=False, stop=True,
                                                skip_group_check=True)
                    last.then_inc(s_score, 1)

                def probs_transposed(j, u, par):
                    n = 4 * j + u
                    pe.wait_ge(s_probn, seen(n + 1))
                    pe.wait_ge(s_pTsb, seen(n - 1))
                    for hp in range(4):
                        last = nc.tensor.transpose(psT[u % 2][:, hp, :], probn[:, par, u, hp * P:(hp + 1) * P],
                                                   k.ident[:, :])
                    last.then_inc(s_pT, 1)

                def attend(j, u, par):
                    n = 4 * j + u
                    t, m = u // 2, u % 2
                    pe.wait_ge(s_pTsb, seen(n + 1))
                    if u == 0:
                        pe.wait_ge(s_x1, seen(j))
                        pe.wait_ge(s_vbd23, seen(j + 1))
                    for hp in range(4):
                        for bb in range(2):
                            tok = slice(t * P + bb * S, t * P + (bb + 1) * S)
                            head = (m * 4 + hp) * 2 * HD
                            last = nc.tensor.matmul(psO[32 * hp:32 * hp + 32, m, tok],
                                                    vbd[:, par, 2 * t + bb, head:head + 2 * HD],
                                                    pT[:, u % 2, hp, bb * S:(bb + 1) * S], start=True, stop=True)
                    last.then_inc(s_pv, 1)

                def project(j):
                    pe.wait_ge(s_oTlo, seen(j + 1))
                    for t in range(2):
                        tok = slice(t * P, (t + 1) * P)
                        last = three_products(psO[:, t, :], [(oT_hi[:, c, tok], oT_lo[:, c, tok], k.woT_hi[:, c, :],
                                                             k.woT_lo[:, c, :]) for c in range(DC)])
                    last.then_inc(s_out, 1)

                def turn(i, par, one, two, three):
                    if one:
                        transposes(i, par)
                    if three:
                        probs_transposed(i - 2, 0, par)
                    if two:
                        scores(i - 1, 0, 1 - par)
                    if three:
                        probs_transposed(i - 2, 1, par)
                    if two:
                        scores(i - 1, 1, 1 - par)
                    if three:
                        attend(i - 2, 0, par)
                    if one:
                        queries_keys(i, par)
                    if one and two and not three:
                        pe.wait_ge(s_asum, 2)
                        nc.tensor.matmul(psT[0][:, 0, 0:2], k.ones[:, :], asum[:, :], start=True, stop=True
                                         ).then_inc(s_wsum, 1)
                    if three:
                        attend(i - 2, 1, par)
                        probs_transposed(i - 2, 2, par)
                        probs_transposed(i - 2, 3, par)
                    if two:
                        values(i - 1, 1 - par, 0)
                        scores(i - 1, 2, 1 - par)
                    if three:
                        attend(i - 2, 2, par)
                    if two:
                        if one:
                            pe.wait_ge(s_qsb, seen(i + 1))
                        values(i - 1, 1 - par, 1)
                    if three:
                        attend(i - 2, 3, par)
                    if two:
                        scores(i - 1, 3, 1 - par)
                    if three:
                        project(i - 2)
                    if two and not three and one:
                        pe.wait_ge(s_wmean, 2)

                all_turns(pe, turn)


class Steps:

    def __init__(self, eng, sem, per_turn):
        self.eng, self.sem, self.per_turn = eng, sem, per_turn

    def begin(self, turn):
        self.base, self.k = turn * self.per_turn, 0

    def done(self, ins):
        ins.then_inc(self.sem, 1)
        self.k += 1

    def wait_last(self):
        self.eng.wait_ge(self.sem, seen(self.base + self.k))

    def end(self):
        assert self.k == self.per_turn, (self.k, self.per_turn)


def quantise_stage(nc, k):
    with ExitStack() as ctx:
        b = Bufs(nc, ctx)
        mv = b.sb("mv_all", [P, NT, 2])
        norm = b.sb("norm_all", [P, NT])
        tmp = b.sb("q_tmp", [P, NT])
        top = b.sb("q_top", [P, 3, NT])
        psW = [b.ps(f"psW{n}", [P, 1024], BF16) for n in range(6)]
        s_mv, s_norm, s_pool, s_xg, s_step, s_wT = (b.sem("q_" + n) for n in ("mv", "norm", "pool", "xg", "step", "wT"))

        with nc.Block() as block:
            @block.vector
            def _(dve):
                for n in range(NT):
                    nc.vector.bn_aggr(mv[:, n, :], k.xstats[:, n, :]).then_inc(s_mv, 1)
                dve.wait_ge(s_mv, NT)
                for n in range(NT):
                    nc.vector.scalar_tensor_tensor(out=k.xg[:, n, :], in0=k.x[:, n, :], scalar=mv[:, n, 0:1],
                                                   in1=k.g_in[:, :], op0=ALU.subtract, op1=ALU.mult).then_inc(s_xg, 1)
                step = [0]

                def in_turn(ins):
                    ins.then_inc(s_step, 1)
                    step[0] += 1
                    dve.wait_ge(s_step, step[0])

                dve.wait_ge(s_xg, NT)
                in_turn(nc.vector.tensor_reduce(top[:, 0, :], k.xg[:, :, :], AX.X, ALU.max, apply_absolute_value=True))
                dve.wait_ge(s_norm, 1)
                in_turn(nc.vector.tensor_tensor(top[:, 1, :], top[:, 0, :], norm[:, :], ALU.mult))
                in_turn(nc.vector.tensor_scalar(top[:, 1, :], top[:, 1, :], 1e-5, None, ALU.max))
                nc.vector.tensor_scalar(k.dq[:, :], top[:, 1, :], k.wmean[:, 0:1], 1.0 / 127.0, ALU.mult, ALU.mult)
                in_turn(nc.vector.reciprocal(top[:, 2, :], top[:, 1, :]))
                in_turn(nc.vector.tensor_tensor(k.rscale[:, :], top[:, 2, :], norm[:, :], ALU.mult))
                in_turn(nc.vector.tensor_scalar(k.rscale[:, :], k.rscale[:, :], 127.0, None, ALU.mult))

            @block.gpsimd
            def _(pool):
                pool.wait_ge(s_mv, NT)
                var, mh = mv[:, :, 1], k.minus_half[:, 0:NT]
                nc.gpsimd.tensor_scalar(tmp[:, :], var, 1.0 + EPS, EPS * EPS, ALU.mult, ALU.add).then_inc(s_pool, 1)
                pool.wait_ge(s_pool, 1)
                nc.gpsimd.tensor_tensor(norm[:, :], tmp[:, :], mh, ALU.pow).then_inc(s_norm, 1)

            @block.scalar
            def _(act):
                for n in range(4):
                    act.wait_ge(s_wT, n + 1)
                    nc.scalar.activation(k.wgT[:, :, n * 512:(n + 1) * 512],
                                         psW[n][:, :].rearrange("p (c o) -> p c o", c=DC), ACT.Copy)
                for n in range(4, 6):
                    act.wait_ge(s_wT, n + 1)
                    nc.scalar.activation(k.wdT[:, 4 * (n - 4):4 * (n - 3), :],
                                         psW[n][:, :].rearrange("p (c d) -> p c d", c=4), ACT.Copy)

            @block.tensor
            def _(pe):
                for n in range(4):
                    for c in range(4):
                        for ic in range(DC):
                            last = nc.tensor.transpose(psW[n][:, ic * 512 + c * P:ic * 512 + (c + 1) * P],
                                                       k.wgq[:, 4 * n + c, ic * P:(ic + 1) * P], k.identb[:, :])
                    last.then_inc(s_wT, 1)
                for n in range(2):
                    for c in range(4):
                        for dc in range(DC):
                            last = nc.tensor.transpose(psW[4 + n][:, c * D + dc * P:c * D + (dc + 1) * P],
                                                       k.wdq[:, dc, (4 * n + c) * P:(4 * n + c + 1) * P],
                                                       k.identb[:, :])
                    last.then_inc(s_wT, 1)


def bitlinear_stage(nc, k):
    with ExitStack() as ctx:
        b = Bufs(nc, ctx)
        xr = b.sb("xr", [P, D])
        q = b.sb("q_in", [P, D], BF16)
        qT = b.sb("qT", [P, 2, DC, P], BF16)
        dq = b.sb("dq", [P, 2])
        gate = b.sb("gate", [P, 2, INNER])
        hid = b.sb("hid", [P, 2, INNER])
        hsq = b.sb("hsq", [P, INNER])
        ssq = b.sb("ssq", [P, 2])
        rms = b.sb("rms", [P, 2, 2])
        hg = b.sb("hg", [P, 2, INNER])
        hr = b.sb("hr", [P, INNER])
        hq = b.sb("hq", [P, 2, INNER], BF16)
        hsmall = b.sb("small_h", [P, 3])
        hscale = b.sb("hscale", [P, 2])
        dqh = b.sb("dqh", [P, 2])
        rounder = b.sb("rounder", [P, 1])
        hqT = b.sb("hqT", [P, 2, IC, P], BF16)
        psUp = b.ps("psUp", [P, 2 * INNER])
        psQ = b.ps("psQ", [P, DC, P], BF16)
        psH = b.ps("psH", [P, IC, P], BF16)
        psD = b.ps("psD", [P, D])
        (s_xr, s_q, s_qT, s_qTsb, s_dq, s_gate, s_v, s_silu, s_hid, s_ssq, s_hg, s_pool, s_small, s_hscale, s_hr, s_hq,
         s_hqT, s_hqTsb, s_down, s_x2, s_rows, s_round, s_held) = (b.sem("b_" + n) for n in (
             "xr", "q", "qT", "qTsb", "dq", "gate", "v", "silu", "hid", "ssq", "hg", "pool", "small", "hscale", "hr", "hq",
             "hqT", "hqTsb", "down", "x2", "rows", "round", "held"))

        def column(t, n):
            return t[:, n:n + 1] if isinstance(n, int) else t[:, bass.ds(n, 1)]

        def all_turns(eng, turn):
            turn(0, 0, 2, True, False, False)
            turn(1, 1, 2, True, True, False)
            with eng.Fori(0, NT // 2 - 2) as g:
                turn(2 * g + 2, 0, 2, True, True, True)
                turn(2 * g + 3, 1, 2, True, True, True)
            turn(NT - 2, 0, 1, True, True, True)
            turn(NT - 1, 1, 0, True, True, True)
            turn(NT, 0, 0, False, True, True)
            turn(NT + 1, 1, 0, False, False, True)

        with nc.Block() as block:
            @block.sync
            def _(sp):
                sp.dma_start(k.gw[:, :], k.gate_w).then_inc(k.gw_loaded, 16)
                for u in range(W_RING):
                    load_unit(sp, k, u)

            @block.vector
            def _(dve):
                credit(dve, s_xr, s_q, s_dq, s_hid, s_small, s_hscale, s_hq, s_x2)
                nc.vector.memset(rounder[:, :], ROUND).then_inc(s_round, 1)
                small = Steps(dve, s_small, 3)

                def quantise_input(n, par):
                    dve.wait_ge(s_q, seen(n))
                    nc.vector.tensor_scalar(xr[:, :], at(k.xg, n)[:, 0, :], column(k.rscale, n), ROUND, ALU.mult,
                                            ALU.add).then_inc(s_xr, 1)
                    dve.wait_ge(s_hid, seen(n - 1))
                    nc.vector.tensor_copy(dq[:, par:par + 1], column(k.dq, n)).then_inc(s_dq, 1)
                    dve.wait_ge(s_xr, seen(n + 1))
                    dve.wait_ge(s_qT, seen(n))
                    nc.vector.tensor_scalar(q[:, :], xr[:, :], -ROUND, 127.0, ALU.add, ALU.min).then_inc(s_q, 1)

                def hidden(n, par):
                    dve.wait_ge(s_silu, seen(n + 1))
                    dve.wait_ge(s_v, seen(n + 1))
                    dve.wait_ge(s_ssq, seen(n - 1))
                    dve.wait_ge(s_hg, seen(n - 1))
                    nc.vector.scalar_tensor_tensor(out=hid[:, par, :], in0=psUp[:, INNER:2 * INNER],
                                                   scalar=dq[:, par:par + 1], in1=gate[:, par, :], op0=ALU.mult,
                                                   op1=ALU.mult).then_inc(s_hid, 1)

                def hidden_scale(n, par):
                    rs = rms[:, par, 1:2]
                    small.begin(n)
                    dve.wait_ge(s_hg, seen(n + 1))
                    small.done(nc.vector.tensor_reduce(hsmall[:, 0:1], hg[:, par, :], AX.X, ALU.max,
                                                       apply_absolute_value=True))
                    small.wait_last()
                    dve.wait_ge(s_pool, seen(2 * n + 2))
                    small.done(nc.vector.tensor_scalar(hsmall[:, 1:2], hsmall[:, 0:1], rs, 1e-5, ALU.mult, ALU.max))
                    small.wait_last()
                    small.done(nc.vector.reciprocal(hsmall[:, 2:3], hsmall[:, 1:2]))
                    nc.vector.tensor_scalar(dqh[:, par:par + 1], hsmall[:, 1:2], k.wmean[:, 1:2], 1.0 / 127.0, ALU.mult,
                                            ALU.mult)
                    small.wait_last()
                    dve.wait_ge(s_hr, seen(n - 1))
                    nc.vector.tensor_scalar(hscale[:, par:par + 1], hsmall[:, 2:3], rs, 127.0, ALU.mult, ALU.mult
                                            ).then_inc(s_hscale, 1)
                    small.end()

                def quantise_hidden(n, par):
                    dve.wait_ge(s_hr, seen(n + 1))
                    dve.wait_ge(s_hqT, seen(n - 1))
                    nc.vector.tensor_scalar(hq[:, par, :], hr[:, :], -ROUND, 127.0, ALU.add, ALU.min).then_inc(s_hq, 1)

                def residual(n, par):
                    dve.wait_ge(s_down, seen(n + 1))
                    nc.vector.scalar_tensor_tensor(out=at(k.x, n)[:, 0, :], in0=psD[:, :], scalar=dqh[:, par:par + 1],
                                                   in1=at(k.x, n)[:, 0, :], op0=ALU.mult, op1=ALU.add
                                                   ).then_inc(s_x2, 1)
                    dve.wait_ge(s_x2, seen(n + 1))
                    nc.vector.bn_stats(at(k.xstats, n)[:, 0, :], at(k.x, n)[:, 0, :]).then_inc(s_rows, 1)

                def turn(n, par, ahead, one, two, three):
                    if two:
                        hidden_scale(n - 1, 1 - par)
                    if one:
                        hidden(n, par)
                    if ahead == 2:
                        quantise_input(n + 2, par)
                    if two:
                        quantise_hidden(n - 1, 1 - par)
                    if three:
                        residual(n - 2, par)

                for n in range(2):
                    quantise_input(n, n)
                all_turns(dve, turn)
                dve.wait_ge(s_rows, NT)
                for n in range(NT):
                    nc.vector.bn_aggr(k.mv[:, n, :], k.xstats[:, n, :])

            @block.gpsimd
            def _(pool):
                credit(pool, s_hg, s_pool)
                hold = Hold(pool, s_held)

                def gained(n, par):
                    pool.wait_ge(s_hid, seen(n + 1))
                    pool.wait_ge(s_hr, seen(n - 1))
                    nc.gpsimd.tensor_tensor(hg[:, par, :], hid[:, par, :], k.g_hid[:, :], ALU.mult).then_inc(s_hg, 1)

                def inv_rms(n, par):
                    pool.wait_ge(s_ssq, seen(n + 1))
                    pool.wait_ge(s_hscale, seen(n - 1))
                    hold()
                    nc.gpsimd.tensor_scalar(rms[:, par, 0:1], ssq[:, par:par + 1], 1.0 / INNER, EPS, ALU.mult,
                                            ALU.add).then_inc(s_pool, 1)
                    pool.wait_ge(s_pool, seen(2 * n + 1))
                    nc.gpsimd.tensor_tensor(rms[:, par, 1:2], rms[:, par, 0:1], k.minus_half[:, 0:1],
                                            ALU.pow).then_inc(s_pool, 1)

                def turn(n, par, ahead, one, two, three):
                    if one:
                        gained(n, par)
                        inv_rms(n, par)

                all_turns(pool, turn)

            @block.scalar
            def _(act):
                nc.scalar.preload_act_table(ACT.Silu)
                credit(act, s_qTsb, s_silu, s_ssq, s_hr, s_hqTsb)
                act.wait_ge(s_round, 1)

                def q_out(n, par):
                    act.wait_ge(s_qT, seen(n + 1))
                    act.wait_ge(s_v, seen(n - 1))
                    nc.scalar.activation(qT[:, par, :, :], psQ[:, :, :], ACT.Copy).then_inc(s_qTsb, 1)

                def silu(n, par):
                    act.wait_ge(s_gate, seen(n + 1))
                    act.wait_ge(s_dq, seen(n + 1))
                    act.wait_ge(s_hid, seen(n - 1))
                    nc.scalar.activation(gate[:, par, :], psUp[:, 0:INNER], ACT.Silu,
                                         scale=dq[:, par:par + 1]).then_inc(s_silu, 1)

                def squares(n, par):
                    act.wait_ge(s_hid, seen(n + 1))
                    act.wait_ge(s_pool, seen(2 * n - 2))
                    nc.scalar.activation(hsq[:, :], hid[:, par, :], ACT.Square,
                                         accum_out=ssq[:, par:par + 1]).then_inc(s_ssq, 1)

                def rounded(n, par):
                    act.wait_ge(s_hscale, seen(n + 1))
                    act.wait_ge(s_hq, seen(n))
                    nc.scalar.activation(hr[:, :], hg[:, par, :], ACT.Identity, scale=hscale[:, par:par + 1],
                                         bias=rounder[:, :]).then_inc(s_hr, 1)

                def hq_out(n, par):
                    act.wait_ge(s_hqT, seen(n + 1))
                    act.wait_ge(s_down, seen(n - 1))
                    nc.scalar.activation(hqT[:, par, :, :], psH[:, :, :], ACT.Copy).then_inc(s_hqTsb, 1)

                def turn(n, par, ahead, one, two, three):
                    if one:
                        silu(n, par)
                    if three:
                        hq_out(n - 2, par)
                    if two:
                        rounded(n - 1, 1 - par)
                    if ahead:
                        q_out(n + 1, 1 - par)
                    if one:
                        squares(n, par)

                q_out(0, 0)
                all_turns(act, turn)

            @block.tensor
            def _(pe):
                credit(pe, s_qT, s_gate, s_v, s_hqT, s_down)

                def q_transposed(n, par):
                    pe.wait_ge(s_q, seen(n + 1))
                    pe.wait_ge(s_qTsb, seen(n))
                    for c in range(DC):
                        last = nc.tensor.transpose(psQ[:, c, :], q[:, c * P:(c + 1) * P], k.identb[:, :])
                    last.then_inc(s_qT, 1)

                def up(n, par, half):
                    pe.wait_ge(s_qTsb, seen(n + 1))
                    free, ready = ((s_silu, s_gate), (s_hid, s_v))[half]
                    pe.wait_ge(free, seen(n))
                    for o in range(2 * half, 2 * half + 2):
                        for c in range(DC):
                            last = nc.tensor.matmul(psUp[:, o * 512:(o + 1) * 512], qT[:, par, c, :],
                                                    k.wgT[:, c, o * 512:(o + 1) * 512], start=(c == 0),
                                                    stop=(c == DC - 1))
                    last.then_inc(ready, 1)

                def h_transposed(n, par):
                    pe.wait_ge(s_hq, seen(n + 1))
                    pe.wait_ge(s_hqTsb, seen(n))
                    for c in range(IC):
                        last = nc.tensor.transpose(psH[:, c, :], hq[:, par, c * P:(c + 1) * P], k.identb[:, :])
                    last.then_inc(s_hqT, 1)

                def down(n, par):
                    pe.wait_ge(s_hqTsb, seen(n + 1))
                    pe.wait_ge(s_x2, seen(n))
                    for c in range(IC):
                        last = nc.tensor.matmul(psD[:, :], hqT[:, par, c, :], k.wdT[:, c, :], start=(c == 0),
                                                stop=(c == IC - 1))
                    last.then_inc(s_down, 1)

                def turn(n, par, ahead, one, two, three):
                    if one:
                        up(n, par, 0)
                    if three:
                        h_transposed(n - 2, par)
                    if ahead:
                        q_transposed(n + 1, 1 - par)
                    if one:
                        up(n, par, 1)
                    if three:
                        down(n - 2, par)

                q_transposed(0, 0)
                all_turns(pe, turn)


W_RING = 4
W_UNITS = [(m, j) for m in range(3) for j in range(NCH // 2)]


def unit_sources(k, u):
    m, j = W_UNITS[u]
    first, end = 2 * P * j, 2 * P * (j + 1)
    if m < 2:
        rows = k.expert_w[m].rearrange("e f d -> (e f) d")[first:end, :]
        return [(None, rows.rearrange("(c p) d -> p c d", p=P))]
    parts, col = [], first
    while col < end:
        e, f = divmod(col, FE)
        n = min(FE - f, end - col)
        parts.append((slice(col - first, col - first + n),
                      k.expert_w[2][e, :, f:f + n].rearrange("(c p) f -> p c f", p=P)))
        col += n
    return parts


def load_unit(eng, k, u):
    for cols, src in unit_sources(k, u):
        dst = k.w_stage[u % W_RING][:, :, :] if cols is None else k.w_stage[u % W_RING][:, :, cols]
        eng.dma_start(dst, src).then_inc(k.w_loaded[u % W_RING], 16)


def route_stage(nc, k):
    with ExitStack() as ctx:
        b = Bufs(nc, ctx)
        veps = b.sb("r_veps", [P, NT])
        rstd = b.sb("r_rstd", [P, NT])
        h = b.sb("r_h", [P, 2, 2, D])
        gwT_hi, gwT_lo = (b.sb(f"gwT_{p}", [P, DC, E], F32R) for p in ("hi", "lo"))
        lgT = b.sb("lgT", [E, 2 * P])
        logit = b.sb("logit", [P, NT, E])
        mx = b.sb("r_mx", [P, NT])
        ex = b.sb("r_ex", [P, NT, E])
        rsum = b.sb("r_sum", [P, NT])
        rinv = b.sb("r_inv", [P, NT])
        score = b.sb("score", [P, NT, E])
        top = b.sb("top", [P, NT, 8])
        topi = b.sb("topi", [P, NT, 8], U32)
        topf = b.sb("topf", [P, NT, 8])
        iota_i = b.sb("iota_i", [P, E], mybir.dt.int32)
        iota_f = b.sb("iota_f", [P, E])
        chosen = b.sb("chosen", [P, NT, E])
        cw = b.sb("cw", [P, NT, E])
        eq = k.x[:, 0:NT // 2, :].rearrange("p t d -> p (t d)")[:, 0:NT * E * TOPK].rearrange(
            "p (n e j) -> p n e j", n=NT, e=E)
        cwT = k.x[0:E, NT // 2:NT, :].rearrange("p t d -> p (t d)")
        four_banks = b.ps("r_ps4", [P, T])
        psH = [b.ps(f"r_psH{n}", [P, DC, 2 * P]) for n in range(2)]
        psW = [b.ps(f"r_psW{n}", [P, 2, 2 * P]) for n in range(2)]
        psC = four_banks[0:E, :]
        psG = four_banks[0:E, 0:2 * P]
        psL = [four_banks[:, n * 512:n * 512 + 2 * E].rearrange("p (t e) -> p t e", t=2) for n in (1, 2)]
        UPT = 3
        units = len(W_UNITS)
        (s_gwT, s_gwhi, s_gwlo, s_pool, s_rstd, s_h, s_hT, s_hi, s_lo, s_lgT, s_lgTsb, s_lg,
         s_lgsb, s_ex, s_step, s_cw, s_cwT, s_cwTsb, s_iota, s_stored, s_wT, s_whi, s_wlo) = (b.sem("r_" + n) for n in (
             "gwT", "gwhi", "gwlo", "pool", "rstdd", "hd", "hT", "hi", "lo", "lgTd", "lgTsb", "lg", "lgsb", "exd", "step",
             "cwd", "cwT", "cwTsb", "iota", "stored", "wT", "whi", "wlo"))
        landed, count = [], [0] * W_RING
        for u in range(units):
            count[u % W_RING] += 16 * len(unit_sources(k, u))
            landed.append(count[u % W_RING])

        def targets(u):
            m, j = W_UNITS[u]
            if m < 2:
                cols = slice(2 * P * j, 2 * P * (j + 1))
                return (k.wg_hi, k.wu_hi)[m][:, :, cols], (k.wg_lo, k.wu_lo)[m][:, :, cols]
            return k.wd_hi[:, 2 * j:2 * j + 2, :], k.wd_lo[:, 2 * j:2 * j + 2, :]

        with nc.Block() as block:
            @block.sync
            def _(sp):
                sp.dma_start(k.x2_dram, k.x[:, :, :]).then_inc(k.x2_spilled, 16)
                for u in range(W_RING, units):
                    sp.wait_ge(s_wT, u - W_RING + 1)
                    load_unit(sp, k, u)
                sp.wait_ge(k.x2_spilled, 16)
                sp.wait_ge(s_cwTsb, 1)
                sp.dma_start(k.cw_dram, cwT).then_inc(s_stored, 16)
                sp.wait_ge(s_stored, 16)

            @block.gpsimd
            def _(pool):
                nc.gpsimd.tensor_scalar(veps[:, :], k.mv[:, :, 1], EPS, None, ALU.add).then_inc(s_pool, 1)
                pool.wait_ge(s_pool, 1)
                nc.gpsimd.tensor_tensor(rstd[:, :], veps[:, :], k.minus_half[:, :], ALU.pow).then_inc(s_rstd, 1)
                pool.wait_ge(s_rstd, 1)
                nc.gpsimd.iota(iota_i[:, :], pattern=[[1, E]], base=0, channel_multiplier=0).then_inc(s_iota, 1)

            @block.scalar
            def _(act):
                def high(u):
                    act.wait_ge(s_wT, u + 1)
                    nc.scalar.activation(targets(u)[0], psW[u % 2][:, :, :], ACT.Copy).then_inc(s_whi, 1)

                nc.scalar.preload_act_table(ACT.Exp)
                act.wait_ge(s_gwT, 1)
                nc.scalar.activation(gwT_hi[:, :, :], psH[1][:, :, 0:E], ACT.Copy).then_inc(s_gwhi, 1)
                for i in range(NP + 1):
                    for n in range(UPT):
                        high(UPT * i + n)
                        if n == 0 and i < NP:
                            act.wait_ge(s_hT, i + 1)
                            nc.scalar.activation(k.h_hi[:, :, i * 2 * P:(i + 1) * 2 * P], psH[i % 2][:, :, :], ACT.Copy
                                                 ).then_inc(s_hi, 1)
                        if n == 1 and i > 0:
                            act.wait_ge(s_lgT, i)
                            if i > 1:
                                act.wait_ge(s_lg, i - 1)
                            nc.scalar.activation(lgT[:, :], psG, ACT.Copy).then_inc(s_lgTsb, 1)
                act.wait_ge(s_step, 2)
                nc.scalar.activation(ex[:, :, :], logit[:, :, :], ACT.Exp).then_inc(s_ex, 1)
                for u in range(UPT * (NP + 1), units):
                    high(u)
                act.wait_ge(s_cwT, 1)
                act.wait_ge(k.x2_spilled, 16)
                nc.scalar.activation(cwT, psC, ACT.Copy).then_inc(s_cwTsb, 1)

            @block.vector
            def _(dve):
                def low(u):
                    hi, lo = targets(u)
                    dve.wait_ge(s_whi, u + 1)
                    nc.vector.tensor_tensor(lo, psW[u % 2][:, :, :], hi.bitcast(F32), ALU.subtract).then_inc(s_wlo, 1)

                dve.wait_ge(s_gwhi, 1)
                nc.vector.tensor_tensor(gwT_lo[:, :, :], psH[1][:, :, 0:E], gwT_hi[:, :, :].bitcast(F32),
                                        ALU.subtract).then_inc(s_gwlo, 1)

                def rows(i):
                    if i > 1:
                        dve.wait_ge(s_hT, i - 1)
                    for t in range(2):
                        n = 2 * i + t
                        nc.vector.tensor_scalar(h[:, i % 2, t, :], k.x[:, n, :], k.mv[:, n, 0:1], rstd[:, n:n + 1],
                                                ALU.subtract, ALU.mult).then_inc(s_h, 1)

                dve.wait_ge(s_rstd, 1)
                rows(0)
                for i in range(NP + 1):
                    if i < NP - 1:
                        rows(i + 1)
                    for n in range(UPT):
                        low(UPT * i + n)
                        if n == 0 and i < NP:
                            cols = slice(i * 2 * P, (i + 1) * 2 * P)
                            dve.wait_ge(s_hi, i + 1)
                            nc.vector.tensor_tensor(k.h_lo[:, :, cols], psH[i % 2][:, :, :],
                                                    k.h_hi[:, :, cols].bitcast(F32), ALU.subtract).then_inc(s_lo, 1)
                    if i > 0:
                        dve.wait_ge(s_lg, i)
                        nc.vector.tensor_copy(logit[:, 2 * i - 2:2 * i, :],
                                              psL[(i - 1) % 2]).then_inc(s_lgsb, 1)
                step, unit = [0], [UPT * (NP + 1)]

                def in_turn(ins, with_unit=True):
                    ins.then_inc(s_step, 1)
                    step[0] += 1
                    if with_unit and unit[0] < units:
                        low(unit[0])
                        unit[0] += 1
                    dve.wait_ge(s_step, step[0])

                def over_experts(t2):
                    return t2[:, :].unsqueeze(2).to_broadcast([P, NT, E])

                dve.wait_ge(s_lgsb, NP)
                in_turn(nc.vector.tensor_reduce(mx[:, :], logit[:, :, :], AX.X, ALU.max), False)
                in_turn(nc.vector.tensor_tensor(logit[:, :, :], logit[:, :, :], over_experts(mx), ALU.subtract))
                dve.wait_ge(s_ex, 1)
                in_turn(nc.vector.tensor_reduce(rsum[:, :], ex[:, :, :], AX.X, ALU.add))
                in_turn(nc.vector.reciprocal(rinv[:, :], rsum[:, :]))
                in_turn(nc.vector.tensor_tensor(score[:, :, :], ex[:, :, :], over_experts(rinv), ALU.mult))
                for n in range(NT):
                    last = nc.vector.max(top[:, n, :], score[:, n, :])
                in_turn(last)
                for n in range(NT):
                    last = nc.vector.max_index(topi[:, n, :], top[:, n, :], score[:, n, :])
                in_turn(last)
                in_turn(nc.vector.tensor_copy(topf[:, :, :], topi[:, :, :]))
                dve.wait_ge(s_iota, 1)
                in_turn(nc.vector.tensor_copy(iota_f[:, :], iota_i[:, :]))
                dve.wait_ge(k.x2_spilled, 16)
                in_turn(nc.vector.tensor_tensor(eq, topf[:, :, 0:TOPK].unsqueeze(2).to_broadcast([P, NT, E, TOPK]),
                                                iota_f[:, :].unsqueeze(1).unsqueeze(3).to_broadcast([P, NT, E, TOPK]),
                                                ALU.is_equal))
                in_turn(nc.vector.tensor_reduce(chosen[:, :, :], eq, AX.X, ALU.max))
                nc.vector.tensor_tensor(cw[:, :, :], score[:, :, :], chosen[:, :, :], ALU.mult).then_inc(s_cw, 1)
                assert unit[0] == units

            @block.tensor
            def _(pe):
                def unit(u):
                    m, j = W_UNITS[u]
                    pe.wait_ge(k.w_loaded[u % W_RING], landed[u])
                    if u >= 2:
                        pe.wait_ge(s_wlo, u - 1)
                    for ch in range(2):
                        for c in range(DC):
                            if m < 2:
                                out, src = psW[u % 2][:, c, ch * P:(ch + 1) * P], \
                                    k.w_stage[u % W_RING][:, ch, c * P:(c + 1) * P]
                            else:
                                out, src = psW[u % 2][:, ch, c * P:(c + 1) * P], \
                                    k.w_stage[u % W_RING][:, c, ch * P:(ch + 1) * P]
                            last = nc.tensor.transpose(out, src, k.ident[:, :])
                    last.then_inc(s_wT, 1)

                def rows(i):
                    pe.wait_ge(s_h, 2 * i + 2)
                    if i >= 2:
                        pe.wait_ge(s_lo, i - 1)
                    if i == 1:
                        pe.wait_ge(s_gwlo, 1)
                    for t in range(2):
                        for c in range(DC):
                            last = nc.tensor.transpose(psH[i % 2][:, c, t * P:(t + 1) * P],
                                                       h[:, i % 2, t, c * P:(c + 1) * P], k.ident[:, :])
                    last.then_inc(s_hT, 1)

                def logits(i):
                    pe.wait_ge(s_gwlo, 1)
                    pe.wait_ge(s_lo, i + 1)
                    if i:
                        pe.wait_ge(s_lgTsb, i)
                    cols = slice(i * 2 * P, (i + 1) * 2 * P)
                    for c in range(DC):
                        nc.tensor.matmul(psG, gwT_lo[:, c, :], k.h_hi[:, c, cols], start=(c == 0), stop=False)
                        nc.tensor.matmul(psG, gwT_hi[:, c, :], k.h_lo[:, c, cols], start=False, stop=False)
                        last = nc.tensor.matmul(psG, gwT_hi[:, c, :], k.h_hi[:, c, cols], start=False,
                                                stop=(c == DC - 1))
                    last.then_inc(s_lgT, 1)

                def logits_out(i):
                    pe.wait_ge(s_lgTsb, i + 1)
                    if i >= 2:
                        pe.wait_ge(s_lgsb, i - 1)
                    for t in range(2):
                        last = nc.tensor.transpose(psL[i % 2][:, t, :], lgT[:, t * P:(t + 1) * P], k.ident[0:E, 0:E])
                    last.then_inc(s_lg, 1)

                pe.wait_ge(k.gw_loaded, 16)
                for c in range(DC):
                    last = nc.tensor.transpose(psH[1][:, c, 0:E], k.gw[:, c * P:(c + 1) * P], k.ident[0:E, 0:E])
                last.then_inc(s_gwT, 1)
                for i in range(NP + 1):
                    unit(UPT * i)
                    if i < NP:
                        rows(i)
                    if i > 0:
                        logits(i - 1)
                    unit(UPT * i + 1)
                    unit(UPT * i + 2)
                    if i > 0:
                        logits_out(i - 1)
                for u in range(UPT * (NP + 1), units):
                    unit(u)
                pe.wait_ge(s_cw, 1)
                for n in range(NT):
                    last = nc.tensor.transpose(psC[:, n * P:(n + 1) * P], cw[:, n, :], k.ident[:, :])
                last.then_inc(s_cwT, 1)


def experts_stage(nc, k):
    with ExitStack() as ctx:
        b = Bufs(nc, ctx)
        tiles = GT // P
        a = [k.x[:, 2 * n:2 * n + 2, :].rearrange("p t d -> p (t d)") for n in range(2)]
        yT = k.x[:, 4:8, :].rearrange("p (c t) d -> p c (t d)", c=DC)
        res = k.x[:, 8:8 + tiles, :]
        a_hi = [b.sb(f"act_hi{n}", [P, GT], F32R) for n in range(2)]
        a_lo = [b.sb(f"act_lo{n}", [P, GT], F32R) for n in range(2)]
        psG = [b.ps(f"psG{n}", [P, GT]) for n in range(2)]
        psU = [b.ps(f"psU{n}", [P, GT]) for n in range(2)]
        cw = [b.sb(f"cw_rows{n}", [P, GT]) for n in range(2)]
        psY = b.ps("psY", [P, DC, GT])
        psT = b.ps("psT", [P, 2, D])
        s_cw = [b.sem(f"e_cw{n}") for n in range(2)]
        (s_gate, s_up, s_silu, s_t, s_a, s_hi, s_lo, s_down, s_ysb, s_T, s_out, s_res) = (
            b.sem("e_" + n) for n in ("gate", "up", "silu", "t", "a", "hi", "lo", "down", "ysb", "T", "out",
                                      "res"))
        LAST = NCH - 1

        with nc.Block() as block:
            @block.sync
            def _(sp):
                def expert_weights(g, s):
                    n = g * NCH + s
                    if not (isinstance(n, int) and n < 2):
                        sp.wait_ge(s_a, seen(n - 1))
                    tok = slice(g * GT, (g + 1) * GT) if isinstance(g, int) else bass.ds(g * GT, GT)
                    e, row = divmod(s * P, FE)
                    cut = FE - row if FE - row < P else P // 2
                    for rows, ex in ((slice(0, cut), e), (slice(cut, P), (s * P + cut) // FE)):
                        sp.dma_start(cw[s % 2][rows, :], k.cw_dram[ex:ex + 1, tok].to_broadcast(
                            [rows.stop - rows.start, GT])).then_inc(s_cw[s % 2], 16)

                for s in range(NCH):
                    expert_weights(0, s)
                with sp.Fori(1, NG) as g:
                    for s in range(NCH):
                        expert_weights(g, s)

            @block.gpsimd
            def _(pool):
                x2_v, out_v, tiles = k.x2_dram, k.out_v, GT // P
                pool.dma_start(res[:, :, :], x2_v[:, 0:tiles, :]).then_inc(s_res, 16)
                with pool.Fori(0, NG - 1) as g:
                    pool.wait_ge(s_out, seen(2 * g + 2))
                    pool.dma_start(out_v[:, bass.ds(tiles * g, tiles), :], res[:, :, :]).then_inc(k.stored, 16)
                    pool.wait_ge(k.stored, 16 * g + 16)
                    pool.dma_start(res[:, :, :], x2_v[:, bass.ds(tiles * g + tiles, tiles), :]).then_inc(s_res, 16)
                pool.wait_ge(s_out, seen(2 * NG))
                pool.dma_start(out_v[:, NT - tiles:NT, :], res[:, :, :]).then_inc(k.stored, 16)
                pool.wait_ge(k.stored, 16 * NG)

            @block.tensor
            def _(pe):
                credit(pe, s_gate)

                def tokens(t, c, g):
                    return t[:, c, g * GT:(g + 1) * GT] if isinstance(g, int) else t[:, c, bass.ds(g * GT, GT)]

                def front(g, s):
                    n = g * NCH + s
                    rows = slice(s * P, (s + 1) * P)
                    first = isinstance(n, int) and n < 2
                    for w_hi, w_lo, ps, free, ready in ((k.wg_hi, k.wg_lo, psG, s_silu, s_gate),
                                                        (k.wu_hi, k.wu_lo, psU, s_t, s_up)):
                        if not first:
                            pe.wait_ge(free, seen(n - 1))
                        for c in range(DC):
                            hh, hl = tokens(k.h_hi, c, g), tokens(k.h_lo, c, g)
                            nc.tensor.matmul(ps[s % 2][:, :], w_lo[:, c, rows], hh, start=(c == 0), stop=False)
                            nc.tensor.matmul(ps[s % 2][:, :], w_hi[:, c, rows], hl, start=False, stop=False)
                            last = nc.tensor.matmul(ps[s % 2][:, :], w_hi[:, c, rows], hh, start=False,
                                                    stop=(c == DC - 1))
                        last.then_inc(ready, 1)

                def back(n, s, g):
                    pe.wait_ge(s_lo, seen(n + 1))
                    if s == 0:
                        pe.wait_ge(s_ysb, seen(g))
                    for m in range(DC):
                        cols = slice(m * P, (m + 1) * P)
                        nc.tensor.matmul(psY[:, m, :], k.wd_lo[:, s, cols], a_hi[s % 2][:, :], start=(s == 0),
                                         stop=False)
                        nc.tensor.matmul(psY[:, m, :], k.wd_hi[:, s, cols], a_lo[s % 2][:, :], start=False, stop=False)
                        last = nc.tensor.matmul(psY[:, m, :], k.wd_hi[:, s, cols], a_hi[s % 2][:, :], start=False,
                                                stop=(s == LAST))
                    last.then_inc(s_down, 1)

                def transposed(g, half):
                    pe.wait_ge(s_ysb, seen(g + 1))
                    pe.wait_ge(s_out, seen(2 * g + half))
                    for t in range(2):
                        for m in range(DC):
                            tok = (2 * half + t) * P
                            last = nc.tensor.transpose(psT[:, t, m * P:(m + 1) * P], yT[:, m, tok:tok + P],
                                                       k.ident[:, :])
                    last.then_inc(s_T, 1)

                def turn(g, before):
                    for s in range(NCH):
                        front(g, s)
                        if s > 0:
                            back(g * NCH + s - 1, s - 1, g)
                        elif before:
                            back(g * NCH - 1, LAST, g)
                        if before and s in (1, 2):
                            transposed(g - 1, s - 1)

                turn(0, False)
                with pe.Fori(1, NG) as g:
                    turn(g, True)
                back(NG * NCH - 1, LAST, NG - 1)
                for half in range(2):
                    transposed(NG - 1, half)

            @block.scalar
            def _(act):
                nc.scalar.preload_act_table(ACT.Silu)
                credit(act, s_silu, s_ysb)

                def silu(n, s):
                    act.wait_ge(s_gate, seen(n + 1))
                    if not (isinstance(n, int) and n < 2):
                        act.wait_ge(s_lo, seen(n - 1))
                    nc.scalar.activation(a[s % 2][:, :], psG[s % 2][:, :], ACT.Silu).then_inc(s_silu, 1)

                def high(n, s):
                    act.wait_ge(s_a, seen(n + 1))
                    if not (isinstance(n, int) and n < 2):
                        act.wait_ge(s_down, n - 1)
                    nc.scalar.activation(a_hi[s % 2][:, :], a[s % 2][:, :], ACT.Copy).then_inc(s_hi, 1)

                def sums_out(g):
                    act.wait_ge(s_down, (g + 1) * NCH)
                    if not isinstance(g, int) or g > 0:
                        act.wait_ge(s_T, 2 * g)
                    nc.scalar.activation(yT[:, :, :], psY[:, :, :], ACT.Copy).then_inc(s_ysb, 1)

                def turn(g, before):
                    for s in range(NCH):
                        n = g * NCH + s
                        silu(n, s)
                        if before and s == 0:
                            sums_out(g - 1)
                        high(n, s)

                turn(0, False)
                with act.Fori(1, NG) as g:
                    turn(g, True)
                sums_out(NG - 1)

            @block.vector
            def _(dve):
                credit(dve, s_t, s_a, s_lo, s_out)

                def middle(g, s):
                    n = g * NCH + s
                    dve.wait_ge(s_silu, seen(n + 1))
                    dve.wait_ge(s_up, n + 1)
                    nc.vector.tensor_tensor(a[s % 2][:, :], psU[s % 2][:, :], a[s % 2][:, :], ALU.mult).then_inc(s_t, 1)
                    dve.wait_ge(s_t, seen(n + 1))
                    dve.wait_ge(s_cw[s % 2], 32 * (g * (NCH // 2) + s // 2 + 1))
                    nc.vector.tensor_tensor(a[s % 2][:, :], cw[s % 2][:, :], a[s % 2][:, :], ALU.mult).then_inc(s_a, 1)
                    dve.wait_ge(s_hi, n + 1)
                    nc.vector.tensor_tensor(a_lo[s % 2][:, :], a[s % 2][:, :], a_hi[s % 2][:, :].bitcast(F32),
                                            ALU.subtract).then_inc(s_lo, 1)

                def output(g, half):
                    dve.wait_ge(s_T, 2 * g + half + 1)
                    dve.wait_ge(s_res, 16 * g + 16)
                    rows = res[:, 2 * half:2 * half + 2, :]
                    nc.vector.tensor_tensor(rows, psT[:, :, :], rows, ALU.add).then_inc(s_out, 1)

                def turn(g, before):
                    for s in range(NCH):
                        middle(g, s)
                        if before and s in (1, 2):
                            output(g - 1, s - 1)

                turn(0, False)
                with dve.Fori(1, NG) as g:
                    turn(g, True)
                for half in range(2):
                    output(NG - 1, half)


class Kept:
    pass


def build(nc, x, ctx_in, Wq, Wkv, Wout, w_gate, g_gate, w_down, g_down, gate_w, e_gate, e_up, e_down, out):
    k = Kept()
    with ExitStack() as ctx:
        b = Bufs(nc, ctx)
        k.ident = b.sb("ident", [P, P])
        k.x = b.sb("x_tok", [P, NT, D])
        k.w_stage = [b.sb(f"w_stage{n}", [P, 2, 2 * P]) for n in range(W_RING)]
        k.w_loaded = [b.sem(f"w_loaded{n}") for n in range(W_RING)]
        k.gw = b.sb("gw", [E, D])
        k.gw_loaded = b.sem("gw_loaded")
        k.gate_w, k.expert_w = gate_w, (e_gate, e_up, e_down)
        k.mv = b.sb("x_mv", [P, NT, 2])
        k.minus_half = b.sb("minus_half", [P, NT])
        k.x_loaded = [b.sem(f"x_loaded{n}") for n in range(2)]
        k.ctx_loaded = b.sem("ctx_loaded")
        k.bit_loaded = b.sem("bit_loaded")
        k.x2_spilled = b.sem("x2_spilled")
        k.stored = b.sem("stored")
        with ExitStack() as xctx:
            xb = Bufs(nc, xctx)
            k.identb = xb.sb("identb", [P, P], BF16)
            k.xstats = xb.sb("x_stats", [P, NT, 6])
            k.ones = xb.sb("ones", [P, P])
            k.wg_nat = xb.sb("wg_nat", [P, 2 * INNER // P, D])
            k.wd_nat = xb.sb("wd_nat", [P, DC, INNER])
            k.g_in = xb.sb("g_in", [P, D])
            k.g_hid = xb.sb("g_hid", [P, INNER])
            k.bit_weights = (w_gate, w_down, g_gate, g_down)
            k.wgq = xb.sb("wgq", [P, 2 * INNER // P, D], BF16)
            k.wdq = xb.sb("wdq", [P, DC, INNER], BF16)
            k.wmean = xb.sb("wmean", [P, 2])
            with ExitStack() as actx:
                a = Bufs(nc, actx)
                k.ctx = a.sb("ctx_tok", [P, NT, L])
                k.causal = a.sb("causal", [P, HPC, S], BF16)
                k.headmask = a.sb("headmask", [P, HPC])
                k.vmask = a.sb("vmask", [P, NH // 2, 2, HD])
                k.vmask2 = k.vmask[:, :, :, :].rearrange("p a b c -> p (a b c)").unsqueeze(1).to_broadcast([P, 2, D])
                k.wqT_hi, k.wqT_lo = (a.sb(f"wqT_{p}", [P, DC, D], F32R) for p in ("hi", "lo"))
                k.woT_hi, k.woT_lo = (a.sb(f"woT_{p}", [P, DC, D], F32R) for p in ("hi", "lo"))
                k.wkvT_hi, k.wkvT_lo = (a.sb(f"wkvT_{p}", [L, 2 * D], F32R) for p in ("hi", "lo"))
                setup_stage(nc, k, Wq, Wkv, Wout, x, ctx_in)
                attention_stage(nc, k)
            with ExitStack() as bctx:
                a = Bufs(nc, bctx)
                k.wgT = a.sb("wgT", [P, DC, 2 * INNER], BF16)
                k.wdT = a.sb("wdT", [P, IC, D], BF16)
                k.xg = a.sb("xg_all", [P, NT, D])
                k.dq = a.sb("dq_all", [P, NT])
                k.rscale = a.sb("rscale_all", [P, NT])
                quantise_stage(nc, k)
                bitlinear_stage(nc, k)
        k.out_v = out.rearrange("b s d -> (b s) d").rearrange("(n p) d -> p n d", p=P)
        k.x2_dram = nc.dram_tensor("x2_spill", [P, NT, D], F32, kind="Internal").ap()
        k.h_hi, k.h_lo = (b.sb(f"h3T_{p}", [P, DC, T], F32R) for p in ("hi", "lo"))
        k.wg_hi, k.wg_lo, k.wu_hi, k.wu_lo = (b.sb(n, [P, DC, E * FE], F32R) for n in (
            "wg_hi", "wg_lo", "wu_hi", "wu_lo"))
        k.wd_hi, k.wd_lo = (b.sb(n, [P, NCH, D], F32R) for n in ("wd_hi", "wd_lo"))
        k.cw_dram = nc.dram_tensor("cw_spill", [E, T], F32, kind="Internal").ap()
        route_stage(nc, k)
        experts_stage(nc, k)


_INS = ["x", "ctx_512", "L0_xattn_Wq", "L0_xattn_Wkv_expand", "L0_xattn_Wout", "L0_attn_w_gate", "L0_attn_g_gate",
        "L0_attn_w_down", "L0_attn_g_down", "L0_ffn_gate_w", "L0_ffn_w_gate", "L0_ffn_w_up", "L0_ffn_w_down"]


def kernel(**inputs):
    import numpy as _np
    import concourse.bacc as _bacc
    from concourse import mybir as _mybir
    from concourse.bass_utils import run_bass_kernel_spmd as _run

    nc = _bacc.Bacc("TRN2", target_bir_lowering=False, num_devices=1)
    arrays, args = {}, []
    for name in _INS:
        a = _np.ascontiguousarray(inputs[name])
        arrays[f"in_{name}_dram"] = a
        args.append(nc.dram_tensor(f"in_{name}_dram", a.shape, _mybir.dt.from_np(a.dtype), kind="ExternalInput").ap())
    args.append(nc.dram_tensor("out_0_dram", (B, S, D), _mybir.dt.float32, kind="ExternalOutput").ap())
    build(nc, *args)
    r = _run(nc, [arrays], core_ids=[0])
    return r.results[0]["out_0_dram"]
```

```python
from contextlib import ExitStack

import numpy as np

import concourse.bass as bass
from concourse import mybir

P = 128
F32 = mybir.dt.float32
F32R = mybir.dt.float32r
BF16 = mybir.dt.bfloat16
ALU = mybir.AluOpType
ACT = mybir.ActivationFunctionType
AX = mybir.AxisListType

B, S, D = 32, 64, 256
SKV, L = 1601, 64
NH = 16
HD = D // NH
INNER = 1024
E, FE, TOPK = 16, 176, 6
T = B * S
NT = T // P
NP = NT // 2
DC = D // P
EPS = 1e-5
ROUND = 1.5 * 2.0 ** 23
MASKED = -1.0e30

HPC = P // HD
NCH = E * FE // P
GT = 512
NG = T // GT
IC = INNER // P


def seen(n):
    return max(n, 0) + 1 if isinstance(n, int) else n + 1


class Bufs:

    def __init__(self, nc, ctx):
        self.nc, self.ctx = nc, ctx

    def sb(self, name, shape, dt=F32):
        return self.ctx.enter_context(self.nc.sbuf_tensor(name, shape, dt))

    def ps(self, name, shape, dt=F32):
        return self.ctx.enter_context(self.nc.psum_tensor(name, shape, dt))

    def sem(self, name):
        return self.ctx.enter_context(self.nc.semaphore(name))


class Hold:

    def __init__(self, eng, sem):
        self.eng, self.sem = eng, sem

    def __call__(self):
        self.eng.nop().then_inc(self.sem, 1)


def credit(eng, *sems):
    for s in sems:
        eng.nop().then_inc(s, 1)


ROW_PARTS = ((0, 2), (2, 4), (4, NT))


def row_statistics(nc, k, dve, part):
    first, end = ROW_PARTS[part]
    dve.wait_ge(k.x_loaded[min(part, 1)], 16)
    for n in range(first, end):
        nc.vector.bn_stats(k.xstats[:, n, :], k.x[:, n, :]).then_inc(k.row_stats_ready, 1)
    dve.wait_ge(k.row_stats_ready, end)
    for n in range(first, end):
        nc.vector.bn_aggr(k.row_mv[:, n, :], k.xstats[:, n, :]).then_inc(k.row_mv_ready, 1)


def row_inv_std(nc, k, pool, part):
    first, end = ROW_PARTS[part]
    pool.wait_ge(k.row_mv_ready, end)
    nc.gpsimd.tensor_scalar(k.row_veps[:, first:end], k.row_mv[:, first:end, 1], EPS, None, ALU.add
                            ).then_inc(k.row_veps_ready, 1)
    pool.wait_ge(k.row_veps_ready, part + 1)
    nc.gpsimd.tensor_tensor(k.row_rstd[:, first:end], k.row_veps[:, first:end], k.minus_half[:, first:end], ALU.pow
                            ).then_inc(k.row_rstd_ready, 1)


def setup_stage(nc, k, Wq, Wkv, Wout, x, ctx_in):
    with ExitStack() as ctx:
        b = Bufs(nc, ctx)
        wq = b.sb("wq_nat", [P, DC, D])
        wkv = b.sb("wkv_nat", [P, 2 * D // P, L])
        wo = b.sb("wo_nat", [P, DC, D])
        psQ = b.ps("psWq", [P, DC, D])
        psO = b.ps("psWo", [P, DC, D])
        psKV = b.ps("psWkv", [L, 2 * D])
        zeroed = b.sem("zeroed")
        ident_ready = b.sem("ident_ready")
        minus_half_ready = b.sem("minus_half_ready")
        w_loaded = [b.sem(f"w_loaded_{name}") for name in ("q", "o", "kv")]
        wT_ready = b.sem("wT_ready")
        wT_hi_ready = b.sem("wT_hi_ready")

        with nc.Block() as block:
            @block.sync
            def _(sp):
                x_v = x.rearrange("b s d -> (b s) d").rearrange("(n p) d -> p n d", p=P)
                sp.dma_start(wq[:, :, :], Wq.rearrange("(c p) i -> p c i", p=P)).then_inc(w_loaded[0], 16)
                sp.dma_start(wo[:, :, :], Wout.rearrange("(c p) i -> p c i", p=P)).then_inc(w_loaded[1], 16)
                sp.dma_start(wkv[:, :, :], Wkv.rearrange("(c p) i -> p c i", p=P)).then_inc(w_loaded[2], 16)
                sp.dma_start(k.x[:, 0:2, :], x_v[:, 0:2, :]).then_inc(k.x_loaded[0], 16)
                sp.dma_start(k.x[:, 2:NT, :], x_v[:, 2:NT, :]).then_inc(k.x_loaded[1], 16)
                w_gate, w_down, g_gate, g_down = k.bit_weights
                sp.dma_start(k.wg_nat[:, :, :], w_gate.rearrange("(c p) i -> p c i", p=P)).then_inc(k.bit_loaded, 16)
                sp.dma_start(k.wd_nat[:, :, :], w_down.rearrange("(c p) i -> p c i", p=P)).then_inc(k.bit_loaded, 16)
                sp.dma_start(k.g_in[:, :], g_gate.unsqueeze(0).to_broadcast([P, D])).then_inc(k.bit_loaded, 16)
                sp.dma_start(k.g_hid[:, :], g_down.unsqueeze(0).to_broadcast([P, INNER])).then_inc(k.bit_loaded, 16)

            @block.gpsimd
            def _(pool):
                step = [0]

                def in_turn(ins):
                    ins.then_inc(zeroed, 1)
                    step[0] += 1
                    pool.wait_ge(zeroed, step[0])

                in_turn(nc.gpsimd.memset(k.ident[:, :], 0.0))
                nc.gpsimd.affine_select(out=k.ident[:, :], in_=k.ident[:, :], compare_op=ALU.not_equal, fill=1.0,
                                        base=0, pattern=[[-1, P]], channel_multiplier=1).then_inc(ident_ready, 1)
                pool.wait_ge(ident_ready, 1)
                in_turn(nc.gpsimd.memset(k.causal[:, :, :], 0.0))
                for half in range(2):
                    rows = k.causal[half * S:(half + 1) * S, :, :]
                    in_turn(nc.gpsimd.affine_select(out=rows, in_=rows, compare_op=ALU.is_ge, fill=MASKED, base=0,
                                                    pattern=[[0, HPC], [-1, S]], channel_multiplier=1))
                in_turn(nc.gpsimd.memset(k.headmask[:, :], 1.0))
                in_turn(nc.gpsimd.affine_select(out=k.headmask[:, :], in_=k.headmask[:, :], compare_op=ALU.is_ge,
                                                fill=0.0, base=0, pattern=[[-HD, HPC]], channel_multiplier=1))
                in_turn(nc.gpsimd.affine_select(out=k.headmask[:, :], in_=k.headmask[:, :], compare_op=ALU.is_ge,
                                                fill=0.0, base=HD - 1, pattern=[[HD, HPC]], channel_multiplier=-1))
                pool.wait_ge(minus_half_ready, 1)
                row_inv_std(nc, k, pool, 0)

            @block.scalar
            def _(act):
                ctx_v = ctx_in.rearrange("(n b) s l -> b s n l", b=2)
                nc.scalar.preload_act_table(ACT.Exp)
                for half in range(2):
                    act.dma_start(k.ctx[half * S:(half + 1) * S, :, :], ctx_v[half, 0:S, :, :]
                                  ).then_inc(k.ctx_loaded, 16)
                act.wait_ge(wT_ready, 1)
                nc.scalar.activation(k.wqT_hi[:, :, :], psQ[:, :, :], ACT.Copy).then_inc(wT_hi_ready, 1)
                act.wait_ge(wT_ready, 2)
                nc.scalar.activation(k.woT_hi[:, :, :], psO[:, :, :], ACT.Copy).then_inc(wT_hi_ready, 1)
                act.wait_ge(wT_ready, 3)
                nc.scalar.activation(k.wkvT_hi[:, :], psKV[:, :], ACT.Copy).then_inc(wT_hi_ready, 1)

            @block.vector
            def _(dve):
                for half in range(2):
                    nc.vector.memset(k.vmask[half * S:(half + 1) * S, :, half, :], 1.0)
                    nc.vector.memset(k.vmask[half * S:(half + 1) * S, :, 1 - half, :], 0.0)
                nc.vector.memset(k.minus_half[:, :], -0.5).then_inc(minus_half_ready, 1)
                nc.vector.memset(k.ones[:, :], 1.0)
                dve.wait_ge(ident_ready, 1)
                nc.vector.tensor_copy(k.identb[:, :], k.ident[:, :])
                for n, (lo, ps, hi) in enumerate(((k.wqT_lo[:, :, :], psQ[:, :, :], k.wqT_hi[:, :, :]),
                                                  (k.woT_lo[:, :, :], psO[:, :, :], k.woT_hi[:, :, :]),
                                                  (k.wkvT_lo[:, :], psKV[:, :], k.wkvT_hi[:, :]))):
                    dve.wait_ge(wT_hi_ready, n + 1)
                    nc.vector.tensor_tensor(lo, ps, hi.bitcast(F32), ALU.subtract)
                    if n == 1:
                        row_statistics(nc, k, dve, 0)

            @block.tensor
            def _(pe):
                pe.wait_ge(ident_ready, 1)
                for w, ps, loaded in ((wq, psQ, w_loaded[0]), (wo, psO, w_loaded[1])):
                    pe.wait_ge(loaded, 16)
                    for oc in range(DC):
                        for ic in range(DC):
                            last = nc.tensor.transpose(ps[:, ic, oc * P:(oc + 1) * P], w[:, oc, ic * P:(ic + 1) * P],
                                                       k.ident[:, :])
                    last.then_inc(wT_ready, 1)
                pe.wait_ge(w_loaded[2], 16)
                for oc in range(2 * D // P):
                    last = nc.tensor.transpose(psKV[:, oc * P:(oc + 1) * P], wkv[:, oc, :], k.ident[:, :])
                last.then_inc(wT_ready, 1)


def at(t3, n, count=1):
    return t3[:, n:n + count, :] if isinstance(n, int) else t3[:, bass.ds(n, count), :]


def attention_stage(nc, k):
    with ExitStack() as ctx:
        b = Bufs(nc, ctx)
        W2 = 2 * P
        h = b.sb("h", [P, 2, D])
        cpair = b.sb("cpair", [P, 2, L])
        hT_hi = b.sb("hT_hi", [P, DC, W2], F32R)
        hT_lo = b.sb("hT_lo", [P, DC, W2], F32R)
        cT_hi = b.sb("cT_hi", [L, 2, 4, 2, S], F32R)
        cT_lo = b.sb("cT_lo", [L, 2, 4, 2, S], F32R)
        q_sb = b.sb("q_sb", [P, 2, DC, W2])
        kbd = b.sb("kbd", [P, 2, DC, HPC, W2])
        vbd = b.sb("vbd", [P, 2, 4, D])
        sub = b.sb("sub", [P, 2, HPC, S])
        mx = b.sb("mx", [P, 2, HPC])
        prob = b.sb("prob", [P, 4, HPC, S])
        rsum = b.sb("rsum", [P, 4, HPC])
        rinv = b.sb("rinv", [P, 4, HPC])
        probn = b.sb("probn", [P, 2, 4, HPC * S])
        pT = b.sb("pT", [P, 2, 4, P])
        oT_hi = b.sb("oT_hi", [P, DC, W2], F32R)
        oT_lo = b.sb("oT_lo", [P, DC, W2], F32R)

        R0 = b.ps("R0", [P, 2, 256])
        R1 = b.ps("R1", [P, 2, 256])
        R2 = b.ps("R2", [P, 2, 256])
        psS = [b.ps(f"psS{u}", [P, 512]) for u in range(2)]
        psT = [b.ps(f"psT{u}", [P, 4, P]) for u in range(2)]
        psO = b.ps("psO", [P, DC, W2])

        s_h = b.sem("a_h")
        s_hT, s_cT, s_hThi, s_cThi, s_hTlo, s_cTlo = (b.sem(n) for n in (
            "a_hT", "a_cT", "a_hThi", "a_cThi", "a_hTlo", "a_cTlo"))
        s_ctxpair = b.sem("a_ctxpair")
        s_q, s_k, s_v01, s_v23 = (b.sem(n) for n in ("a_q", "a_k", "a_v01", "a_v23"))
        s_qsb, s_kbd, s_vbd01, s_vbd23 = (b.sem(n) for n in ("a_qsb", "a_kbd", "a_vbd01", "a_vbd23"))
        s_score, s_mx, s_sub, s_prob, s_rsum, s_rinv, s_probn = (b.sem(n) for n in (
            "a_score", "a_mx", "a_sub", "a_prob", "a_rsum", "a_rinv", "a_probn"))
        s_pT, s_pTsb, s_pv = (b.sem(n) for n in ("a_pT", "a_pTsb", "a_pv"))
        s_oThi, s_oTlo, s_out, s_x1 = (b.sem(n) for n in ("a_oThi", "a_oTlo", "a_out", "a_x1"))

        def all_turns(eng, turn):
            turn(0, 0, True, False, False)
            turn(1, 1, True, True, False)
            with eng.Fori(0, NP // 2 - 2) as g:
                turn(2 * g + 2, 0, True, True, True)
                turn(2 * g + 3, 1, True, True, True)
            turn(NP - 2, 0, True, True, True)
            turn(NP - 1, 1, True, True, True)
            turn(NP, 0, False, True, True)
            turn(NP + 1, 1, False, False, True)

        asum = b.sb("asum", [P, 2])
        wrec = b.sb("wrec", [P, 2])
        s_asum, s_wsum, s_wmean, s_wrec, s_tern, s_tern3 = (
            b.sem("a_" + n) for n in ("asum", "wsum", "wmean", "wrec", "tern", "tern3"))

        def ternary(ops, eng, steps, j, n):
            part = (slice(None), slice(4 * j, 4 * j + 4), slice(None)) if n == 0 else \
                (slice(None), slice(None), slice(2 * P * j, 2 * P * (j + 1)))
            w, q = ((k.wg_nat, k.wgq), (k.wd_nat, k.wdq))[n]
            w, q = w[part], q[part]
            first = 3 * n + (6 * j if steps is s_tern else 0)
            eng.wait_ge(s_wrec, 1)
            ops.tensor_scalar(w, w, wrec[:, n:n + 1], ROUND, ALU.mult, ALU.add).then_inc(steps, 1)
            eng.wait_ge(steps, first + 1)
            ops.tensor_scalar(w, w, -ROUND, 1.0, ALU.add, ALU.mult).then_inc(steps, 1)
            eng.wait_ge(steps, first + 2)
            ops.tensor_scalar(q, w, 1.0, -1.0, ALU.min, ALU.max).then_inc(steps, 1)

        with nc.Block() as block:
            @block.vector
            def _(dve):
                credit(dve, s_h, s_hTlo, s_cTlo, s_vbd01, s_vbd23, s_mx, s_sub, s_rsum, s_rinv,
                       s_oTlo, s_x1)

                def normalised(i):
                    dve.wait_ge(s_hT, seen(i))
                    for t in range(2):
                        n = 2 * i + t
                        rstd = k.row_rstd[:, n:n + 1] if isinstance(n, int) else k.row_rstd[:, bass.ds(n, 1)]
                        nc.vector.tensor_scalar(h[:, t:t + 1, :], at(k.x, n), at(k.row_mv, n)[:, 0, 0:1], rstd,
                                                ALU.subtract, ALU.mult).then_inc(s_h, 1)

                def low_parts(i, par):
                    dve.wait_ge(s_hThi, seen(i + 1))
                    dve.wait_ge(s_q, seen(i))
                    nc.vector.tensor_tensor(hT_lo[:, :, :], R0[:, :, :], hT_hi[:, :, :].bitcast(F32),
                                            ALU.subtract).then_inc(s_hTlo, 1)
                    dve.wait_ge(s_cThi, seen(i + 1))
                    dve.wait_ge(s_v23, seen(i - 1))
                    cps = R1[0:L, 0, :].rearrange("p (b s) -> p b s", b=4)
                    for dup in range(2):
                        last = nc.vector.tensor_tensor(cT_lo[:, par, :, dup, :], cps,
                                                       cT_hi[:, par, :, dup, :].bitcast(F32), ALU.subtract)
                    last.then_inc(s_cTlo, 1)

                def values(j, par, half):
                    ps, ready, done = ((R1, s_v01, s_vbd01), (R2, s_v23, s_vbd23))[half]
                    dve.wait_ge(ready, seen(j + 1))
                    dve.wait_ge(s_pv, seen(4 * j - 4))
                    nc.vector.tensor_tensor(vbd[:, par, 2 * half:2 * half + 2, :], ps[:, :, :], k.vmask2, ALU.mult
                                            ).then_inc(done, 1)

                def shifted(j, u):
                    n = 4 * j + u
                    r = u % 2
                    dve.wait_ge(s_score, seen(n + 1))
                    sc = psS[r][:, :].rearrange("p (h s) -> p h s", h=HPC)
                    nc.vector.tensor_reduce(mx[:, r, :], sc, AX.X, ALU.max).then_inc(s_mx, 1)
                    dve.wait_ge(s_mx, seen(n + 1))
                    dve.wait_ge(s_prob, seen(n - 1))
                    nc.vector.tensor_tensor(sub[:, r, :, :], sc, mx[:, r, :].unsqueeze(2).to_broadcast([P, HPC, S]),
                                            ALU.subtract).then_inc(s_sub, 1)

                def sums(j, u):
                    n = 4 * j + u
                    dve.wait_ge(s_prob, seen(n + 1))
                    nc.vector.tensor_reduce(rsum[:, u, :], prob[:, u, :, :], AX.X, ALU.add).then_inc(s_rsum, 1)
                    dve.wait_ge(s_rsum, seen(n + 1))
                    dve.wait_ge(s_probn, seen(n - 3))
                    nc.vector.reciprocal(rinv[:, u, :], rsum[:, u, :]).then_inc(s_rinv, 1)

                def out_low(j):
                    dve.wait_ge(s_oThi, seen(j + 1))
                    dve.wait_ge(s_out, seen(j))
                    nc.vector.tensor_tensor(oT_lo[:, :, :], psO[:, :, :], oT_hi[:, :, :].bitcast(F32),
                                            ALU.subtract).then_inc(s_oTlo, 1)

                def residual(j):
                    dve.wait_ge(s_out, seen(j + 1))
                    nc.vector.tensor_tensor(at(k.x, 2 * j, 2), psO[:, :, :], at(k.x, 2 * j, 2), ALU.add
                                            ).then_inc(s_x1, 1)
                    dve.wait_ge(s_x1, seen(j + 1))
                    for t in range(2):
                        nc.vector.bn_stats(at(k.xstats, 2 * j + t)[:, 0, :], at(k.x, 2 * j + t)[:, 0, :])

                def weight_means():
                    dve.wait_ge(s_wsum, 1)
                    for n, count in enumerate((2 * INNER * D, D * INNER)):
                        nc.vector.tensor_scalar(k.wmean[:, n:n + 1], psT[0][:, 0, n:n + 1], 1.0 / count, 1e-5, ALU.mult,
                                                ALU.max).then_inc(s_wmean, 1)
                    dve.wait_ge(s_wmean, 2)
                    nc.vector.reciprocal(wrec[:, :], k.wmean[:, :]).then_inc(s_wrec, 1)

                def turn(i, par, one, two, three):
                    if not two and not one:
                        for n in range(2):
                            ternary(nc.vector, dve, s_tern3, 3, n)
                    more = one and not (isinstance(i, int) and i == NP - 1)
                    if one:
                        low_parts(i, par)
                    if one and not two:
                        row_statistics(nc, k, dve, 1)
                    if two:
                        shifted(i - 1, 0)
                        shifted(i - 1, 1)
                        sums(i - 1, 0)
                    if two:
                        shifted(i - 1, 2)
                        sums(i - 1, 1)
                        values(i - 1, 1 - par, 0)
                        shifted(i - 1, 3)
                        values(i - 1, 1 - par, 1)
                    if three:
                        out_low(i - 2)
                    if more:
                        if one and not three:
                            dve.wait_ge(k.row_rstd_ready, 3 if two else 2)
                        normalised(i + 1)
                    if one and not two:
                        row_statistics(nc, k, dve, 2)
                    if two:
                        sums(i - 1, 2)
                        sums(i - 1, 3)
                    if two and not three and one:
                        weight_means()
                    if three:
                        residual(i - 2)

                normalised(0)
                all_turns(dve, turn)

            @block.gpsimd
            def _(pool):
                credit(pool, s_ctxpair, s_probn)
                hold = Hold(pool, b.sem("a_held_pool"))

                def context(i):
                    pool.wait_ge(s_cT, seen(i))
                    hold()
                    nc.gpsimd.tensor_copy(cpair[:, :, :], at(k.ctx, 2 * i, 2)).then_inc(s_ctxpair, 1)

                def quotient(j, u, par):
                    n = 4 * j + u
                    pool.wait_ge(s_rinv, seen(n + 1))
                    if u == 0:
                        pool.wait_ge(s_pT, seen(4 * j - 4))
                    nc.gpsimd.tensor_tensor(probn[:, par, u, :].rearrange("p (h s) -> p h s", h=HPC),
                                            prob[:, u, :, :], rinv[:, u, :].unsqueeze(2).to_broadcast([P, HPC, S]),
                                            ALU.mult).then_inc(s_probn, 1)

                TERNARY_TURNS = (1, NP - 2, NP - 1)

                def turn(i, par, one, two, three):
                    if one and not (isinstance(i, int) and i == NP - 1):
                        context(i + 1)
                    if two:
                        quotient(i - 1, 0, 1 - par)
                    if one and not two:
                        row_inv_std(nc, k, pool, 1)
                        row_inv_std(nc, k, pool, 2)
                    if two:
                        for u in range(1, 4):
                            quotient(i - 1, u, 1 - par)
                    if isinstance(i, int) and i in TERNARY_TURNS:
                        for n in range(2):
                            ternary(nc.gpsimd, pool, s_tern, TERNARY_TURNS.index(i), n)

                pool.wait_ge(k.ctx_loaded, 32)
                context(0)
                all_turns(pool, turn)

            @block.scalar
            def _(act):
                nc.scalar.preload_act_table(ACT.Exp)
                credit(act, s_hThi, s_cThi, s_qsb, s_kbd, s_prob, s_pTsb, s_oThi)

                def high_parts(i, par):
                    act.wait_ge(s_hT, seen(i + 1))
                    act.wait_ge(s_q, seen(i))
                    nc.scalar.activation(hT_hi[:, :, :], R0[:, :, :], ACT.Copy).then_inc(s_hThi, 1)
                    act.wait_ge(s_cT, seen(i + 1))
                    act.wait_ge(s_v23, seen(i - 1))
                    cps = R1[0:L, 0, :].rearrange("p (b s) -> p b s", b=4)
                    for dup in range(2):
                        last = nc.scalar.activation(cT_hi[:, par, :, dup, :], cps, ACT.Copy)
                    last.then_inc(s_cThi, 1)

                def queries(i, par):
                    act.wait_ge(s_q, seen(i + 1))
                    act.wait_ge(s_score, seen(4 * i - 4))
                    nc.scalar.activation(q_sb[:, par, :, :], R2[:, :, :], ACT.Copy).then_inc(s_qsb, 1)

                def keys(i, par, first, end):
                    if first == 0:
                        act.wait_ge(s_k, seen(i + 1))
                    for hh in range(first, end):
                        last = nc.scalar.activation(kbd[:, par, :, hh, :], R0[:, :, :], ACT.Copy,
                                                    scale=k.headmask[:, hh:hh + 1])
                    if end == HPC:
                        last.then_inc(s_kbd, 1)

                def exps(j, u):
                    n = 4 * j + u
                    act.wait_ge(s_sub, seen(n + 1))
                    act.wait_ge(s_probn, seen(n - 3))
                    nc.scalar.activation(prob[:, u, :, :], sub[:, u % 2, :, :], ACT.Exp,
                                         scale=float(HD) ** -0.5).then_inc(s_prob, 1)

                def probs_out(j, u):
                    n = 4 * j + u
                    act.wait_ge(s_pT, seen(n + 1))
                    act.wait_ge(s_pv, seen(n - 1))
                    nc.scalar.activation(pT[:, u % 2, :, :], psT[u % 2][:, :, :], ACT.Copy).then_inc(s_pTsb, 1)

                def out_high(j):
                    act.wait_ge(s_pv, seen(4 * j + 4))
                    act.wait_ge(s_out, seen(j))
                    nc.scalar.activation(oT_hi[:, :, :], psO[:, :, :], ACT.Copy).then_inc(s_oThi, 1)

                def weight_sums(n):
                    act.wait_ge(k.bit_loaded, 64)
                    w, scratch = ((k.wg_nat, k.wgq), (k.wd_nat, k.wdq))[n]
                    nc.scalar.activation(scratch[:, :, :], w[:, :, :], ACT.Abs,
                                         accum_out=asum[:, n:n + 1]).then_inc(s_asum, 1)

                def turn(i, par, one, two, three):
                    if one:
                        high_parts(i, par)
                    if one and two and not three:
                        weight_sums(0)
                    if three:
                        probs_out(i - 2, 0)
                    if two:
                        exps(i - 1, 0)
                    if three:
                        probs_out(i - 2, 1)
                    if two:
                        exps(i - 1, 1)
                    if one:
                        queries(i, par)
                        keys(i, par, 0, 3)
                    if three:
                        probs_out(i - 2, 2)
                    if two:
                        exps(i - 1, 2)
                    if three:
                        probs_out(i - 2, 3)
                    if one:
                        keys(i, par, 3, 6)
                    if three:
                        out_high(i - 2)
                    if one:
                        keys(i, par, 6, HPC)
                    if two:
                        exps(i - 1, 3)
                    if one and two and not three:
                        weight_sums(1)

                all_turns(act, turn)

            @block.tensor
            def _(pe):
                credit(pe, s_hT, s_cT, s_q, s_k, s_v01, s_v23, s_score, s_pT, s_pv, s_out)
                hold = Hold(pe, b.sem("a_held_pe"))

                def three_products(out, parts):
                    for c, (lh, ll, rh, rl) in enumerate(parts):
                        nc.tensor.matmul(out, ll, rh, start=(c == 0), stop=False)
                        nc.tensor.matmul(out, lh, rl, start=False, stop=False)
                        last = nc.tensor.matmul(out, lh, rh, start=False, stop=(c == len(parts) - 1))
                    return last

                def transposes(i, par):
                    pe.wait_ge(s_kbd, seen(i))
                    for t in range(2):
                        pe.wait_ge(s_h, seen(2 * i + t + 1))
                        for c in range(DC):
                            last = nc.tensor.transpose(R0[:, c, t * P:(t + 1) * P], h[:, t, c * P:(c + 1) * P],
                                                       k.ident[:, :])
                    last.then_inc(s_hT, 1)
                    pe.wait_ge(s_vbd01, seen(i - 1))
                    pe.wait_ge(s_ctxpair, seen(i + 1))
                    hold()
                    for t in range(2):
                        last = nc.tensor.transpose(R1[0:L, 0, t * P:(t + 1) * P], cpair[:, t, :], k.ident[:, :])
                    last.then_inc(s_cT, 1)

                def queries_keys(i, par):
                    pe.wait_ge(s_hTlo, seen(i + 1))
                    pe.wait_ge(s_vbd23, seen(i - 1))
                    for m in range(DC):
                        cols = slice(m * P, (m + 1) * P)
                        last = three_products(R2[:, m, :], [(k.wqT_hi[:, c, cols], k.wqT_lo[:, c, cols],
                                                             hT_hi[:, c, :], hT_lo[:, c, :]) for c in range(DC)])
                    last.then_inc(s_q, 1)
                    pe.wait_ge(s_cTlo, seen(i + 1))
                    for m in range(DC):
                        cols = slice(m * P, (m + 1) * P)
                        last = three_products(R0[:, m, :].rearrange("p (b s) -> p b s", b=4),
                                              [(k.wkvT_hi[:, cols], k.wkvT_lo[:, cols], cT_hi[:, par, :, 0, :],
                                                cT_lo[:, par, :, 0, :])])
                    last.then_inc(s_k, 1)

                def values(j, par, half):
                    ps, ready = ((R1, s_v01), (R2, s_v23))[half]
                    for bb in range(2):
                        bt = 2 * half + bb
                        hi = cT_hi[:, par, bt, :, :].rearrange("p a s -> p (a s)")
                        lo = cT_lo[:, par, bt, :, :].rearrange("p a s -> p (a s)")
                        last = three_products(ps[:, bb, :], [(hi, lo, k.wkvT_hi[:, D:2 * D], k.wkvT_lo[:, D:2 * D])])
                    last.then_inc(ready, 1)

                def scores(j, u, par):
                    n = 4 * j + u
                    t, m = u // 2, u % 2
                    if u == 0:
                        pe.wait_ge(s_qsb, seen(j + 1))
                        pe.wait_ge(s_kbd, seen(j + 1))
                    pe.wait_ge(s_sub, seen(n - 1))
                    nc.tensor.matmul(psS[m][:, :], k.identb[:, :], k.causal[:, :, :].rearrange("p h s -> p (h s)"),
                                     start=True, stop=True, skip_group_check=True)
                    for bb in range(2):
                        tok = slice(t * P + bb * S, t * P + (bb + 1) * S)
                        last = nc.tensor.matmul(psS[m][bb * S:(bb + 1) * S, :].rearrange("p (h s) -> p h s", h=HPC),
                                                q_sb[:, par, m, tok], kbd[:, par, m, :, tok], start=False, stop=True,
                                                skip_group_check=True)
                    last.then_inc(s_score, 1)

                def probs_transposed(j, u, par):
                    n = 4 * j + u
                    pe.wait_ge(s_probn, seen(n + 1))
                    pe.wait_ge(s_pTsb, seen(n - 1))
                    for hp in range(4):
                        last = nc.tensor.transpose(psT[u % 2][:, hp, :], probn[:, par, u, hp * P:(hp + 1) * P],
                                                   k.ident[:, :])
                    last.then_inc(s_pT, 1)

                def attend(j, u, par):
                    n = 4 * j + u
                    t, m = u // 2, u % 2
                    pe.wait_ge(s_pTsb, seen(n + 1))
                    if u == 0:
                        pe.wait_ge(s_x1, seen(j))
                        pe.wait_ge(s_vbd23, seen(j + 1))
                    for hp in range(4):
                        for bb in range(2):
                            tok = slice(t * P + bb * S, t * P + (bb + 1) * S)
                            head = (m * 4 + hp) * 2 * HD
                            last = nc.tensor.matmul(psO[32 * hp:32 * hp + 32, m, tok],
                                                    vbd[:, par, 2 * t + bb, head:head + 2 * HD],
                                                    pT[:, u % 2, hp, bb * S:(bb + 1) * S], start=True, stop=True)
                    last.then_inc(s_pv, 1)

                def project(j):
                    pe.wait_ge(s_oTlo, seen(j + 1))
                    for t in range(2):
                        tok = slice(t * P, (t + 1) * P)
                        last = three_products(psO[:, t, :], [(oT_hi[:, c, tok], oT_lo[:, c, tok], k.woT_hi[:, c, :],
                                                             k.woT_lo[:, c, :]) for c in range(DC)])
                    last.then_inc(s_out, 1)

                def turn(i, par, one, two, three):
                    if one:
                        transposes(i, par)
                    if three:
                        probs_transposed(i - 2, 0, par)
                    if two:
                        scores(i - 1, 0, 1 - par)
                    if three:
                        probs_transposed(i - 2, 1, par)
                    if two:
                        scores(i - 1, 1, 1 - par)
                    if three:
                        attend(i - 2, 0, par)
                    if one:
                        queries_keys(i, par)
                    if two:
                        scores(i - 1, 2, 1 - par)
                    if three:
                        attend(i - 2, 1, par)
                        probs_transposed(i - 2, 2, par)
                        probs_transposed(i - 2, 3, par)
                    if two:
                        values(i - 1, 1 - par, 0)
                        scores(i - 1, 3, 1 - par)
                    if three:
                        attend(i - 2, 2, par)
                    if two:
                        if one:
                            pe.wait_ge(s_qsb, seen(i + 1))
                        values(i - 1, 1 - par, 1)
                    if three:
                        attend(i - 2, 3, par)
                        project(i - 2)
                    if one and two and not three:
                        pe.wait_ge(s_asum, 2)
                        nc.tensor.matmul(psT[0][:, 0, 0:2], k.ones[:, :], asum[:, :], start=True, stop=True
                                         ).then_inc(s_wsum, 1)
                        pe.wait_ge(s_wmean, 2)

                all_turns(pe, turn)


class Steps:

    def __init__(self, eng, sem, per_turn):
        self.eng, self.sem, self.per_turn = eng, sem, per_turn

    def begin(self, turn):
        self.base, self.k = turn * self.per_turn, 0

    def done(self, ins):
        ins.then_inc(self.sem, 1)
        self.k += 1

    def wait_last(self):
        self.eng.wait_ge(self.sem, seen(self.base + self.k))

    def end(self):
        assert self.k == self.per_turn, (self.k, self.per_turn)


INPUT_PARTS = ((0, 2), (2, NT // 2), (NT // 2, NT))


def input_scales(nc, k, dve, part):
    first, end = INPUT_PARTS[part]
    cols = slice(first, end)
    top, clipped, inverse = (k.top[:, n, cols] for n in range(3))
    step = [7 * part]

    def in_turn(ins):
        ins.then_inc(k.scale_step, 1)
        step[0] += 1
        dve.wait_ge(k.scale_step, step[0])

    if part < 2:
        for n in range(first, end):
            nc.vector.scalar_tensor_tensor(out=k.xg[:, n, :], in0=k.x[:, n, :], scalar=k.in_mv[:, n, 0:1],
                                           in1=k.g_in[:, :], op0=ALU.subtract, op1=ALU.mult).then_inc(k.xg_ready, 1)
        dve.wait_ge(k.xg_ready, end)
    else:
        dve.wait_ge(k.late_xg_ready, end - first)
    in_turn(nc.vector.tensor_reduce(top, k.xg[:, cols, :], AX.X, ALU.max, apply_absolute_value=True))
    in_turn(nc.vector.tensor_tensor(top, top, k.in_norm[:, cols], ALU.mult))
    in_turn(nc.vector.tensor_scalar(clipped, top, 1e-5, None, ALU.max))
    in_turn(nc.vector.tensor_scalar(k.dq[:, cols], clipped, k.wmean[:, 0:1], 1.0 / 127.0, ALU.mult, ALU.mult))
    in_turn(nc.vector.reciprocal(inverse, clipped))
    in_turn(nc.vector.tensor_tensor(k.rscale[:, cols], inverse, k.in_norm[:, cols], ALU.mult))
    in_turn(nc.vector.tensor_scalar(k.rscale[:, cols], k.rscale[:, cols], 127.0, None, ALU.mult))


def quantise_stage(nc, k):
    with ExitStack() as ctx:
        b = Bufs(nc, ctx)
        mv, norm = k.in_mv, k.in_norm
        tmp = b.sb("q_tmp", [P, NT])
        psW = [b.ps(f"psW{n}", [P, 1024], BF16) for n in range(6)]
        s_mv, s_norm, s_pool, s_wT = (b.sem("q_" + n) for n in ("mv", "norm", "pool", "wT"))

        with nc.Block() as block:
            @block.vector
            def _(dve):
                for n in range(NT):
                    nc.vector.bn_aggr(mv[:, n, :], k.xstats[:, n, :]).then_inc(s_mv, 1)
                dve.wait_ge(s_mv, NT)
                dve.wait_ge(s_norm, 1)
                input_scales(nc, k, dve, 0)
                for n in range(2):
                    dve.wait_ge(s_wT, 5 + n)
                    nc.vector.tensor_copy(k.wdT[:, 4 * n:4 * n + 4, :],
                                          psW[4 + n][:, :].rearrange("p (c d) -> p c d", c=4))

            @block.gpsimd
            def _(pool):
                for part, (first, end) in enumerate(((0, 2), (2, NT))):
                    cols = slice(first, end)
                    pool.wait_ge(s_mv, end)
                    nc.gpsimd.tensor_scalar(tmp[:, cols], mv[:, cols, 1], 1.0 + EPS, EPS * EPS, ALU.mult, ALU.add
                                            ).then_inc(s_pool, 1)
                    pool.wait_ge(s_pool, part + 1)
                    nc.gpsimd.tensor_tensor(norm[:, cols], tmp[:, cols], k.minus_half[:, cols], ALU.pow
                                            ).then_inc(s_norm, 1)

            @block.scalar
            def _(act):
                for n in range(4):
                    act.wait_ge(s_wT, n + 1)
                    nc.scalar.activation(k.wgT[:, :, n * 512:(n + 1) * 512],
                                         psW[n][:, :].rearrange("p (c o) -> p c o", c=DC), ACT.Copy)

            @block.tensor
            def _(pe):
                for n in range(4):
                    for c in range(4):
                        for ic in range(DC):
                            last = nc.tensor.transpose(psW[n][:, ic * 512 + c * P:ic * 512 + (c + 1) * P],
                                                       k.wgq[:, 4 * n + c, ic * P:(ic + 1) * P], k.identb[:, :])
                    last.then_inc(s_wT, 1)
                for n in range(2):
                    for c in range(4):
                        for dc in range(DC):
                            last = nc.tensor.transpose(psW[4 + n][:, c * D + dc * P:c * D + (dc + 1) * P],
                                                       k.wdq[:, dc, (4 * n + c) * P:(4 * n + c + 1) * P],
                                                       k.identb[:, :])
                    last.then_inc(s_wT, 1)


def bitlinear_stage(nc, k):
    with ExitStack() as ctx:
        b = Bufs(nc, ctx)
        xr = b.sb("xr", [P, D])
        q = b.sb("q_in", [P, D], BF16)
        qT = b.sb("qT", [P, 2, DC, P], BF16)
        dq = b.sb("dq", [P, 2])
        gate = b.sb("gate", [P, 2, INNER])
        hid = b.sb("hid", [P, 2, INNER])
        hsq = b.sb("hsq", [P, INNER])
        ssq = b.sb("ssq", [P, 2])
        rms = b.sb("rms", [P, 2, 2])
        hg = b.sb("hg", [P, 2, INNER])
        hr = b.sb("hr", [P, INNER])
        hq = b.sb("hq", [P, 2, INNER], BF16)
        hsmall = b.sb("small_h", [P, 3])
        hscale = b.sb("hscale", [P, 2])
        dqh = b.sb("dqh", [P, 2])
        rounder = b.sb("rounder", [P, 1])
        less = b.sb("less_mean", [P, NT - INPUT_PARTS[-1][0]])
        s_less = b.sem("b_less")
        hqT = b.sb("hqT", [P, 2, IC, P], BF16)
        psUp = b.ps("psUp", [P, 2 * INNER])
        psQ = b.ps("psQ", [P, DC, P], BF16)
        psH = b.ps("psH", [P, IC, P], BF16)
        psD = b.ps("psD", [P, D])
        (s_xr, s_q, s_qT, s_qTsb, s_dq, s_gate, s_v, s_silu, s_hid, s_ssq, s_hg, s_pool) = (b.sem("b_" + n) for n in (
            "xr", "q", "qT", "qTsb", "dq", "gate", "v", "silu", "hid", "ssq", "hg", "pool"))
        (s_small, s_hscale, s_hr, s_hq, s_hqT, s_hqTsb, s_down, s_x2, s_rows, s_round, s_centred, s_held) = (
            b.sem("b_" + n) for n in (
                "small", "hscale", "hr", "hq", "hqT", "hqTsb", "down", "x2", "rows", "round", "centred", "held"))

        def column(t, n):
            return t[:, n:n + 1] if isinstance(n, int) else t[:, bass.ds(n, 1)]

        def all_turns(eng, turn):
            turn(0, 0, 2, True, False, False)
            turn(1, 1, 2, True, True, False)
            with eng.Fori(0, NT // 2 - 2) as g:
                turn(2 * g + 2, 0, 2, True, True, True)
                turn(2 * g + 3, 1, 2, True, True, True)
            turn(NT - 2, 0, 1, True, True, True)
            turn(NT - 1, 1, 0, True, True, True)
            turn(NT, 0, 0, False, True, True)
            turn(NT + 1, 1, 0, False, False, True)

        with nc.Block() as block:
            @block.sync
            def _(sp):
                sp.dma_start(k.gw[:, :], k.gate_w).then_inc(k.gw_loaded, 16)
                for u in range(W_RING):
                    load_unit(sp, k, u)

            @block.vector
            def _(dve):
                credit(dve, s_xr, s_q, s_dq, s_hid, s_small, s_hscale, s_hq, s_x2)
                nc.vector.memset(rounder[:, :], ROUND).then_inc(s_round, 1)
                small = Steps(dve, s_small, 3)

                def round_input(n, par):
                    dve.wait_ge(s_q, seen(n))
                    nc.vector.tensor_scalar(xr[:, :], at(k.xg, n)[:, 0, :], column(k.rscale, n), ROUND, ALU.mult,
                                            ALU.add).then_inc(s_xr, 1)

                def quantise_input(n, par):
                    dve.wait_ge(s_hid, seen(n - 1))
                    nc.vector.tensor_copy(dq[:, par:par + 1], column(k.dq, n)).then_inc(s_dq, 1)
                    dve.wait_ge(s_xr, seen(n + 1))
                    dve.wait_ge(s_qT, seen(n))
                    nc.vector.tensor_scalar(q[:, :], xr[:, :], -ROUND, 127.0, ALU.add, ALU.min).then_inc(s_q, 1)

                def hidden(n, par):
                    dve.wait_ge(s_silu, seen(n + 1))
                    dve.wait_ge(s_v, seen(n + 1))
                    dve.wait_ge(s_ssq, seen(n - 1))
                    dve.wait_ge(s_hg, seen(n - 1))
                    nc.vector.scalar_tensor_tensor(out=hid[:, par, :], in0=psUp[:, INNER:2 * INNER],
                                                   scalar=dq[:, par:par + 1], in1=gate[:, par, :], op0=ALU.mult,
                                                   op1=ALU.mult).then_inc(s_hid, 1)

                def largest(n, par):
                    small.begin(n)
                    dve.wait_ge(s_hg, seen(n + 1))
                    small.done(nc.vector.tensor_reduce(hsmall[:, 0:1], hg[:, par, :], AX.X, ALU.max,
                                                       apply_absolute_value=True))

                def hidden_scale(n, par):
                    rs = rms[:, par, 1:2]
                    small.wait_last()
                    dve.wait_ge(s_pool, seen(2 * n + 2))
                    small.done(nc.vector.tensor_scalar(hsmall[:, 1:2], hsmall[:, 0:1], rs, 1e-5, ALU.mult, ALU.max))
                    small.wait_last()
                    small.done(nc.vector.reciprocal(hsmall[:, 2:3], hsmall[:, 1:2]))
                    nc.vector.tensor_scalar(dqh[:, par:par + 1], hsmall[:, 1:2], k.wmean[:, 1:2], 1.0 / 127.0, ALU.mult,
                                            ALU.mult)
                    small.wait_last()
                    dve.wait_ge(s_hr, seen(n - 1))
                    nc.vector.tensor_scalar(hscale[:, par:par + 1], hsmall[:, 2:3], rs, 127.0, ALU.mult, ALU.mult
                                            ).then_inc(s_hscale, 1)
                    small.end()

                def quantise_hidden(n, par):
                    dve.wait_ge(s_hr, seen(n + 1))
                    dve.wait_ge(s_hqT, seen(n - 1))
                    nc.vector.tensor_scalar(hq[:, par, :], hr[:, :], -ROUND, 127.0, ALU.add, ALU.min).then_inc(s_hq, 1)

                def residual(n, par):
                    dve.wait_ge(s_down, seen(n + 1))
                    nc.vector.scalar_tensor_tensor(out=at(k.x, n)[:, 0, :], in0=psD[:, :], scalar=dqh[:, par:par + 1],
                                                   in1=at(k.x, n)[:, 0, :], op0=ALU.mult, op1=ALU.add
                                                   ).then_inc(s_x2, 1)

                def statistics(n):
                    dve.wait_ge(s_x2, seen(n + 1))
                    nc.vector.bn_stats(at(k.xstats, n)[:, 0, :], at(k.x, n)[:, 0, :]).then_inc(s_rows, 1)

                def turn(n, par, ahead, one, two, three):
                    if one:
                        hidden(n, par)
                    if two:
                        largest(n - 1, 1 - par)
                    elif one:
                        input_scales(nc, k, dve, 2)
                    if ahead == 2:
                        round_input(n + 2, par)
                        quantise_input(n + 2, par)
                    if two:
                        hidden_scale(n - 1, 1 - par)
                    if three:
                        residual(n - 2, par)
                        statistics(n - 2)
                    if two:
                        quantise_hidden(n - 1, 1 - par)

                for n in range(2):
                    round_input(n, n)
                    quantise_input(n, n)
                input_scales(nc, k, dve, 1)
                all_turns(dve, turn)
                dve.wait_ge(s_rows, NT)
                for n in range(NT):
                    nc.vector.bn_aggr(k.mv[:, n, :], k.xstats[:, n, :])

            @block.gpsimd
            def _(pool):
                credit(pool, s_hg, s_pool)
                hold = Hold(pool, s_held)
                first, end = INPUT_PARTS[-1]
                nc.gpsimd.tensor_scalar(less[:, :], k.in_mv[:, first:end, 0], -1.0, 0.0, ALU.mult, ALU.add
                                        ).then_inc(s_less, 1)
                pool.wait_ge(s_less, 1)
                for n in range(first, end):
                    nc.gpsimd.tensor_scalar(k.xg[:, n, :], k.x[:, n, :], less[:, n - first:n - first + 1], 1.0, ALU.add,
                                            ALU.mult).then_inc(s_centred, 1)
                    if n > first:
                        pool.wait_ge(s_centred, n - first)
                        nc.gpsimd.tensor_tensor(k.xg[:, n - 1, :], k.xg[:, n - 1, :], k.g_in[:, :], ALU.mult
                                                ).then_inc(k.late_xg_ready, 1)
                pool.wait_ge(s_centred, end - first)
                nc.gpsimd.tensor_tensor(k.xg[:, end - 1, :], k.xg[:, end - 1, :], k.g_in[:, :], ALU.mult
                                        ).then_inc(k.late_xg_ready, 1)

                def gained(n, par):
                    pool.wait_ge(s_hid, seen(n + 1))
                    pool.wait_ge(s_hr, seen(n - 1))
                    nc.gpsimd.tensor_tensor(hg[:, par, :], hid[:, par, :], k.g_hid[:, :], ALU.mult).then_inc(s_hg, 1)

                def inv_rms(n, par):
                    pool.wait_ge(s_ssq, seen(n + 1))
                    pool.wait_ge(s_hscale, seen(n - 1))
                    hold()
                    nc.gpsimd.tensor_scalar(rms[:, par, 0:1], ssq[:, par:par + 1], 1.0 / INNER, EPS, ALU.mult,
                                            ALU.add).then_inc(s_pool, 1)
                    pool.wait_ge(s_pool, seen(2 * n + 1))
                    nc.gpsimd.tensor_tensor(rms[:, par, 1:2], rms[:, par, 0:1], k.minus_half[:, 0:1],
                                            ALU.pow).then_inc(s_pool, 1)

                def turn(n, par, ahead, one, two, three):
                    if one:
                        gained(n, par)
                        inv_rms(n, par)

                all_turns(pool, turn)

            @block.scalar
            def _(act):
                nc.scalar.preload_act_table(ACT.Silu)
                credit(act, s_qTsb, s_silu, s_ssq, s_hr, s_hqTsb)
                act.wait_ge(s_round, 1)

                def q_out(n, par):
                    act.wait_ge(s_qT, seen(n + 1))
                    act.wait_ge(s_v, seen(n - 1))
                    nc.scalar.activation(qT[:, par, :, :], psQ[:, :, :], ACT.Copy).then_inc(s_qTsb, 1)

                def silu(n, par):
                    act.wait_ge(s_gate, seen(n + 1))
                    act.wait_ge(s_dq, seen(n + 1))
                    act.wait_ge(s_hid, seen(n - 1))
                    nc.scalar.activation(gate[:, par, :], psUp[:, 0:INNER], ACT.Silu,
                                         scale=dq[:, par:par + 1]).then_inc(s_silu, 1)

                def squares(n, par):
                    act.wait_ge(s_hid, seen(n + 1))
                    act.wait_ge(s_pool, seen(2 * n - 2))
                    nc.scalar.activation(hsq[:, :], hid[:, par, :], ACT.Square,
                                         accum_out=ssq[:, par:par + 1]).then_inc(s_ssq, 1)

                def rounded(n, par):
                    act.wait_ge(s_hscale, seen(n + 1))
                    act.wait_ge(s_hq, seen(n))
                    nc.scalar.activation(hr[:, :], hg[:, par, :], ACT.Identity, scale=hscale[:, par:par + 1],
                                         bias=rounder[:, :]).then_inc(s_hr, 1)

                def hq_out(n, par):
                    act.wait_ge(s_hqT, seen(n + 1))
                    act.wait_ge(s_down, seen(n - 1))
                    nc.scalar.activation(hqT[:, par, :, :], psH[:, :, :], ACT.Copy).then_inc(s_hqTsb, 1)

                def turn(n, par, ahead, one, two, three):
                    if ahead:
                        silu(n + 1, 1 - par)
                    if three:
                        hq_out(n - 2, par)
                    if one:
                        squares(n, par)
                    if ahead == 2:
                        q_out(n + 2, par)
                    if two:
                        rounded(n - 1, 1 - par)

                for n in range(2):
                    q_out(n, n)
                silu(0, 0)
                all_turns(act, turn)

            @block.tensor
            def _(pe):
                credit(pe, s_qT, s_gate, s_v, s_hqT, s_down)

                def q_transposed(n, par):
                    pe.wait_ge(s_q, seen(n + 1))
                    pe.wait_ge(s_qTsb, seen(n))
                    for c in range(DC):
                        last = nc.tensor.transpose(psQ[:, c, :], q[:, c * P:(c + 1) * P], k.identb[:, :])
                    last.then_inc(s_qT, 1)

                def up(n, par, half):
                    pe.wait_ge(s_qTsb, seen(n + 1))
                    free, ready = ((s_silu, s_gate), (s_hid, s_v))[half]
                    pe.wait_ge(free, seen(n))
                    for o in range(2 * half, 2 * half + 2):
                        for c in range(DC):
                            last = nc.tensor.matmul(psUp[:, o * 512:(o + 1) * 512], qT[:, par, c, :],
                                                    k.wgT[:, c, o * 512:(o + 1) * 512], start=(c == 0),
                                                    stop=(c == DC - 1))
                    last.then_inc(ready, 1)

                def h_transposed(n, par):
                    pe.wait_ge(s_hq, seen(n + 1))
                    pe.wait_ge(s_hqTsb, seen(n))
                    for c in range(IC):
                        last = nc.tensor.transpose(psH[:, c, :], hq[:, par, c * P:(c + 1) * P], k.identb[:, :])
                    last.then_inc(s_hqT, 1)

                def down(n, par):
                    pe.wait_ge(s_hqTsb, seen(n + 1))
                    pe.wait_ge(s_x2, seen(n))
                    for c in range(IC):
                        last = nc.tensor.matmul(psD[:, :], hqT[:, par, c, :], k.wdT[:, c, :], start=(c == 0),
                                                stop=(c == IC - 1))
                    last.then_inc(s_down, 1)

                def turn(n, par, ahead, one, two, three):
                    if ahead:
                        up(n + 1, 1 - par, 0)
                    if three:
                        h_transposed(n - 2, par)
                    if ahead:
                        up(n + 1, 1 - par, 1)
                    if three:
                        down(n - 2, par)
                    if ahead == 2:
                        q_transposed(n + 2, par)

                for n in range(2):
                    q_transposed(n, n)
                for half in range(2):
                    up(0, 0, half)
                all_turns(pe, turn)


W_RING = 4
W_UNITS = [(m, j) for m in range(3) for j in range(NCH // 2)]


def unit_sources(k, u):
    m, j = W_UNITS[u]
    first, end = 2 * P * j, 2 * P * (j + 1)
    if m < 2:
        rows = k.expert_w[m].rearrange("e f d -> (e f) d")[first:end, :]
        return [(None, rows.rearrange("(c p) d -> p c d", p=P))]
    parts, col = [], first
    while col < end:
        e, f = divmod(col, FE)
        n = min(FE - f, end - col)
        parts.append((slice(col - first, col - first + n),
                      k.expert_w[2][e, :, f:f + n].rearrange("(c p) f -> p c f", p=P)))
        col += n
    return parts


def load_unit(eng, k, u):
    for cols, src in unit_sources(k, u):
        dst = k.w_stage[u % W_RING][:, :, :] if cols is None else k.w_stage[u % W_RING][:, :, cols]
        eng.dma_start(dst, src).then_inc(k.w_loaded[u % W_RING], 16)


def route_stage(nc, k):
    with ExitStack() as ctx:
        b = Bufs(nc, ctx)
        veps = b.sb("r_veps", [P, NT])
        rstd = b.sb("r_rstd", [P, NT])
        h = b.sb("r_h", [P, 2, 2, D])
        gwT_hi, gwT_lo = (b.sb(f"gwT_{p}", [P, DC, E], F32R) for p in ("hi", "lo"))
        lgT = b.sb("lgT", [E, 2 * P])
        logit = b.sb("logit", [P, NT, E])
        mx = b.sb("r_mx", [P, NT])
        ex = b.sb("r_ex", [P, NT, E])
        rsum = b.sb("r_sum", [P, NT])
        rinv = b.sb("r_inv", [P, NT])
        score = b.sb("score", [P, NT, 8 + E - TOPK])
        rest = b.sb("rest", [P, NT, 8 + E - TOPK])
        top = b.sb("top", [P, NT, 8])
        cw = b.sb("cw", [P, NT, E])
        cwT = k.x[0:E, NT // 2:NT, :].rearrange("p t d -> p (t d)")
        four_banks = b.ps("r_ps4", [P, T])
        psH = [b.ps(f"r_psH{n}", [P, DC, 2 * P]) for n in range(2)]
        psW = [b.ps(f"r_psW{n}", [P, 2, 2 * P]) for n in range(2)]
        psW.append(four_banks[:, 3 * 512:].rearrange("p (c r) -> p c r", c=2))
        psC = four_banks[0:E, :]
        psG = four_banks[0:E, 0:2 * P]
        psL = [four_banks[:, n * 512:n * 512 + 2 * E].rearrange("p (t e) -> p t e", t=2) for n in (1, 2)]
        UPT = 3
        units = len(W_UNITS)
        (s_gwT, s_gwhi, s_gwlo, s_pool, s_rstd, s_h0, s_h1, s_hT, s_hi, s_lo) = (b.sem("r_" + n) for n in (
            "gwT", "gwhi", "gwlo", "pool", "rstdd", "h0", "h1", "hT", "hi", "lo"))
        (s_lgT, s_lgTsb, s_lg, s_lgsb, s_ex, s_step, s_cw, s_cwT, s_wT, s_whi, s_wlo) = (b.sem("r_" + n) for n in (
            "lgTd", "lgTsb", "lg", "lgsb", "exd", "step", "cwd", "cwT", "wT", "whi", "wlo"))
        s_cwTsb = [b.sem(f"r_cwTsb{half}") for half in range(2)]
        landed, count = [], [0] * W_RING
        for u in range(units):
            count[u % W_RING] += 16 * len(unit_sources(k, u))
            landed.append(count[u % W_RING])

        def targets(u):
            m, j = W_UNITS[u]
            if m < 2:
                cols = slice(2 * P * j, 2 * P * (j + 1))
                return (k.wg_hi, k.wu_hi)[m][:, :, cols], (k.wg_lo, k.wu_lo)[m][:, :, cols]
            return k.wd_hi[:, 2 * j:2 * j + 2, :], k.wd_lo[:, 2 * j:2 * j + 2, :]

        with nc.Block() as block:
            @block.sync
            def _(sp):
                sp.dma_start(k.x2_dram, k.x[:, :, :]).then_inc(k.x2_spilled, 16)
                for u in range(W_RING, units):
                    sp.wait_ge(s_wT, u - W_RING + 1)
                    load_unit(sp, k, u)
                sp.wait_ge(k.x2_spilled, 16)
                for half, ready in enumerate(s_cwTsb):
                    cols = slice(half * T // 2, (half + 1) * T // 2)
                    sp.wait_ge(ready, 1)
                    sp.dma_start(k.cw_dram[:, cols], cwT[:, cols]).then_inc(k.cw_stored[half], 16)

            @block.gpsimd
            def _(pool):
                def row(i):
                    if i > 1:
                        pool.wait_ge(s_hT, i - 1)
                    n = 2 * i
                    nc.gpsimd.tensor_scalar(h[:, i % 2, 0, :], k.x[:, n, :], k.mv[:, n, 0:1], rstd[:, n:n + 1],
                                            ALU.subtract, ALU.mult).then_inc(s_h0, 1)

                for part, cols in enumerate((slice(0, 2), slice(2, NT))):
                    nc.gpsimd.tensor_scalar(veps[:, cols], k.mv[:, cols, 1], EPS, None, ALU.add).then_inc(s_pool, 1)
                    pool.wait_ge(s_pool, part + 1)
                    nc.gpsimd.tensor_tensor(rstd[:, cols], veps[:, cols], k.minus_half[:, cols], ALU.pow
                                            ).then_inc(s_rstd, 1)
                    pool.wait_ge(s_rstd, part + 1)
                    if part == 0:
                        row(0)
                for i in range(1, NP):
                    row(i)

            @block.scalar
            def _(act):
                def high(u):
                    act.wait_ge(s_wT, u + 1)
                    nc.scalar.activation(targets(u)[0], psW[u % 3][:, :, :], ACT.Copy).then_inc(s_whi, 1)

                nc.scalar.preload_act_table(ACT.Exp)
                act.wait_ge(s_gwT, 1)
                nc.scalar.activation(gwT_hi[:, :, :], psH[1][:, :, 0:E], ACT.Copy).then_inc(s_gwhi, 1)
                for i in range(NP + 1):
                    for n in range(UPT):
                        high(UPT * i + n)
                        if n == 0 and i < NP:
                            act.wait_ge(s_hT, i + 1)
                            nc.scalar.activation(k.h_hi[:, :, i * 2 * P:(i + 1) * 2 * P], psH[i % 2][:, :, :], ACT.Copy
                                                 ).then_inc(s_hi, 1)
                        if n == 1 and i > 0:
                            act.wait_ge(s_lgT, i)
                            if i > 1:
                                act.wait_ge(s_lg, i - 1)
                            nc.scalar.activation(lgT[:, :], psG, ACT.Copy).then_inc(s_lgTsb, 1)
                act.wait_ge(s_step, 2)
                nc.scalar.activation(ex[:, :, :], logit[:, :, :], ACT.Exp).then_inc(s_ex, 1)
                for u in range(UPT * (NP + 1), units):
                    high(u)
                act.wait_ge(s_cwT, 1)
                act.wait_ge(k.x2_spilled, 16)
                nc.scalar.activation(cwT[:, 0:T // 2], psC[:, 0:T // 2], ACT.Copy).then_inc(s_cwTsb[0], 1)

            @block.vector
            def _(dve):
                def low(u):
                    hi, lo = targets(u)
                    dve.wait_ge(s_whi, u + 1)
                    nc.vector.tensor_tensor(lo, psW[u % 3][:, :, :], hi.bitcast(F32), ALU.subtract).then_inc(s_wlo, 1)

                nc.vector.memset(score[:, :, E:], -1.0)
                dve.wait_ge(s_gwhi, 1)
                nc.vector.tensor_tensor(gwT_lo[:, :, :], psH[1][:, :, 0:E], gwT_hi[:, :, :].bitcast(F32),
                                        ALU.subtract).then_inc(s_gwlo, 1)

                def row(i):
                    if i > 1:
                        dve.wait_ge(s_hT, i - 1)
                    n = 2 * i + 1
                    dve.wait_ge(s_rstd, 1 if i == 0 else 2)
                    nc.vector.tensor_scalar(h[:, i % 2, 1, :], k.x[:, n, :], k.mv[:, n, 0:1], rstd[:, n:n + 1],
                                            ALU.subtract, ALU.mult).then_inc(s_h1, 1)

                row(0)
                for i in range(NP + 1):
                    for n in range(UPT):
                        low(UPT * i + n)
                        if n == 0 and i < NP - 1:
                            row(i + 1)
                        if n == 0 and i < NP:
                            cols = slice(i * 2 * P, (i + 1) * 2 * P)
                            dve.wait_ge(s_hi, i + 1)
                            nc.vector.tensor_tensor(k.h_lo[:, :, cols], psH[i % 2][:, :, :],
                                                    k.h_hi[:, :, cols].bitcast(F32), ALU.subtract).then_inc(s_lo, 1)
                    if i > 0:
                        dve.wait_ge(s_lg, i)
                        nc.vector.tensor_copy(logit[:, 2 * i - 2:2 * i, :],
                                              psL[(i - 1) % 2]).then_inc(s_lgsb, 1)
                step, unit = [0], [UPT * (NP + 1)]

                def in_turn(ins, with_unit=True):
                    ins.then_inc(s_step, 1)
                    step[0] += 1
                    if with_unit and unit[0] < units:
                        low(unit[0])
                        unit[0] += 1
                    dve.wait_ge(s_step, step[0])

                def over_experts(t2):
                    return t2[:, :].unsqueeze(2).to_broadcast([P, NT, E])

                dve.wait_ge(s_lgsb, NP)
                in_turn(nc.vector.tensor_reduce(mx[:, :], logit[:, :, :], AX.X, ALU.max), False)
                in_turn(nc.vector.tensor_tensor(logit[:, :, :], logit[:, :, :], over_experts(mx), ALU.subtract))
                dve.wait_ge(s_ex, 1)
                in_turn(nc.vector.tensor_reduce(rsum[:, :], ex[:, :, :], AX.X, ALU.add))
                in_turn(nc.vector.reciprocal(rinv[:, :], rsum[:, :]))
                in_turn(nc.vector.tensor_tensor(score[:, :, 0:E], ex[:, :, :], over_experts(rinv), ALU.mult))
                for n in range(NT):
                    last = nc.vector.max(top[:, n, :], score[:, n, 0:E])
                in_turn(last)
                in_turn(nc.vector.memset(top[:, :, TOPK:8], -1.0))
                for n in range(NT):
                    last = nc.vector.match_replace(rest[:, n, :], top[:, n, :], score[:, n, :], 0.0)
                in_turn(last)
                while unit[0] < units:
                    low(unit[0])
                    unit[0] += 1
                nc.vector.tensor_tensor(cw[:, :, :], score[:, :, 0:E], rest[:, :, 0:E], ALU.subtract).then_inc(s_cw, 1)
                dve.wait_ge(s_cwT, 2)
                dve.wait_ge(k.x2_spilled, 16)
                nc.vector.tensor_copy(cwT[:, T // 2:], psC[:, T // 2:]).then_inc(s_cwTsb[1], 1)
                assert unit[0] == units

            @block.tensor
            def _(pe):
                def unit(u):
                    m, j = W_UNITS[u]
                    pe.wait_ge(k.w_loaded[u % W_RING], landed[u])
                    if u >= 3:
                        pe.wait_ge(s_wlo, u - 2)
                    for ch in range(2):
                        for c in range(DC):
                            if m < 2:
                                out, src = psW[u % 3][:, c, ch * P:(ch + 1) * P], \
                                    k.w_stage[u % W_RING][:, ch, c * P:(c + 1) * P]
                            else:
                                out, src = psW[u % 3][:, ch, c * P:(c + 1) * P], \
                                    k.w_stage[u % W_RING][:, c, ch * P:(ch + 1) * P]
                            last = nc.tensor.transpose(out, src, k.ident[:, :])
                    last.then_inc(s_wT, 1)

                def rows(i):
                    pe.wait_ge(s_h0, i + 1)
                    pe.wait_ge(s_h1, i + 1)
                    if i >= 2:
                        pe.wait_ge(s_lo, i - 1)
                    if i == 1:
                        pe.wait_ge(s_gwlo, 1)
                    for t in range(2):
                        for c in range(DC):
                            last = nc.tensor.transpose(psH[i % 2][:, c, t * P:(t + 1) * P],
                                                       h[:, i % 2, t, c * P:(c + 1) * P], k.ident[:, :])
                    last.then_inc(s_hT, 1)

                def logits(i):
                    pe.wait_ge(s_gwlo, 1)
                    pe.wait_ge(s_lo, i + 1)
                    if i:
                        pe.wait_ge(s_lgTsb, i)
                    cols = slice(i * 2 * P, (i + 1) * 2 * P)
                    for c in range(DC):
                        nc.tensor.matmul(psG, gwT_lo[:, c, :], k.h_hi[:, c, cols], start=(c == 0), stop=False)
                        nc.tensor.matmul(psG, gwT_hi[:, c, :], k.h_lo[:, c, cols], start=False, stop=False)
                        last = nc.tensor.matmul(psG, gwT_hi[:, c, :], k.h_hi[:, c, cols], start=False,
                                                stop=(c == DC - 1))
                    last.then_inc(s_lgT, 1)

                def logits_out(i):
                    pe.wait_ge(s_lgTsb, i + 1)
                    if i >= 2:
                        pe.wait_ge(s_lgsb, i - 1)
                    for t in range(2):
                        last = nc.tensor.transpose(psL[i % 2][:, t, :], lgT[:, t * P:(t + 1) * P], k.ident[0:E, 0:E])
                    last.then_inc(s_lg, 1)

                pe.wait_ge(k.gw_loaded, 16)
                for c in range(DC):
                    last = nc.tensor.transpose(psH[1][:, c, 0:E], k.gw[:, c * P:(c + 1) * P], k.ident[0:E, 0:E])
                last.then_inc(s_gwT, 1)
                for i in range(NP + 1):
                    unit(UPT * i)
                    if i < NP:
                        rows(i)
                    if i > 0:
                        logits(i - 1)
                    unit(UPT * i + 1)
                    unit(UPT * i + 2)
                    if i > 0:
                        logits_out(i - 1)
                for u in range(UPT * (NP + 1), units):
                    unit(u)
                pe.wait_ge(s_cw, 1)
                for n in range(NT):
                    last = nc.tensor.transpose(psC[:, n * P:(n + 1) * P], cw[:, n, :], k.ident[:, :])
                    if n % (NT // 2) == NT // 2 - 1:
                        last.then_inc(s_cwT, 1)


def experts_stage(nc, k):
    with ExitStack() as ctx:
        b = Bufs(nc, ctx)
        tiles = GT // P
        a = [k.x[:, 2 * n:2 * n + 2, :].rearrange("p t d -> p (t d)") for n in range(2)]
        yT = k.x[:, 4:8, :].rearrange("p (c t) d -> p c (t d)", c=DC)
        res = k.x[:, 8:8 + tiles, :]
        a_hi = [b.sb(f"act_hi{n}", [P, GT], F32R) for n in range(2)]
        a_lo = [b.sb(f"act_lo{n}", [P, GT], F32R) for n in range(2)]
        psG = [b.ps(f"psG{n}", [P, GT]) for n in range(2)]
        psU = [b.ps(f"psU{n}", [P, GT]) for n in range(2)]
        cw = [b.sb(f"cw_rows{n}", [P, GT]) for n in range(2)]
        psY = b.ps("psY", [P, DC, GT])
        psT = b.ps("psT", [P, 2, D])
        s_cw = [b.sem(f"e_cw{n}") for n in range(2)]
        (s_gate, s_up, s_silu, s_t, s_a, s_hi, s_lo, s_down, s_ysb, s_T, s_out, s_res) = (
            b.sem("e_" + n) for n in ("gate", "up", "silu", "t", "a", "hi", "lo", "down", "ysb", "T", "out",
                                      "res"))
        LAST = NCH - 1

        with nc.Block() as block:
            @block.sync
            def _(sp):
                def expert_weights(g, s):
                    n = g * NCH + s
                    if not (isinstance(n, int) and n < 2):
                        sp.wait_ge(s_a, seen(n - 1))
                    tok = slice(g * GT, (g + 1) * GT) if isinstance(g, int) else bass.ds(g * GT, GT)
                    e, row = divmod(s * P, FE)
                    cut = FE - row if FE - row < P else P // 2
                    for rows, ex in ((slice(0, cut), e), (slice(cut, P), (s * P + cut) // FE)):
                        sp.dma_start(cw[s % 2][rows, :], k.cw_dram[ex:ex + 1, tok].to_broadcast(
                            [rows.stop - rows.start, GT])).then_inc(s_cw[s % 2], 16)

                sp.wait_ge(k.cw_stored[0], 16)
                for s in range(NCH):
                    expert_weights(0, s)
                sp.wait_ge(k.cw_stored[1], 16)
                with sp.Fori(1, NG) as g:
                    for s in range(NCH):
                        expert_weights(g, s)
                for half in range(2):
                    first = NT - GT // P + 2 * half
                    sp.wait_ge(s_out, seen(2 * NG - 1 + half))
                    sp.dma_start(k.out_v[:, first:first + 2, :], res[:, 2 * half:2 * half + 2, :]
                                 ).then_inc(k.last_stored, 16)
                sp.wait_ge(k.last_stored, 32)

            @block.gpsimd
            def _(pool):
                x2_v, out_v, tiles = k.x2_dram, k.out_v, GT // P
                for half in range(2):
                    pool.wait_ge(k.cw_stored[half], 16)
                pool.dma_start(res[:, :, :], x2_v[:, 0:tiles, :]).then_inc(s_res, 16)
                with pool.Fori(0, NG - 1) as g:
                    pool.wait_ge(s_out, seen(2 * g + 2))
                    pool.dma_start(out_v[:, bass.ds(tiles * g, tiles), :], res[:, :, :]).then_inc(k.stored, 16)
                    pool.wait_ge(k.stored, 16 * g + 16)
                    pool.dma_start(res[:, :, :], x2_v[:, bass.ds(tiles * g + tiles, tiles), :]).then_inc(s_res, 16)

            @block.tensor
            def _(pe):
                credit(pe, s_gate)

                def tokens(t, c, g):
                    return t[:, c, g * GT:(g + 1) * GT] if isinstance(g, int) else t[:, c, bass.ds(g * GT, GT)]

                def front(g, s):
                    n = g * NCH + s
                    rows = slice(s * P, (s + 1) * P)
                    first = isinstance(n, int) and n < 2
                    for w_hi, w_lo, ps, free, ready in ((k.wg_hi, k.wg_lo, psG, s_silu, s_gate),
                                                        (k.wu_hi, k.wu_lo, psU, s_t, s_up)):
                        if not first:
                            pe.wait_ge(free, seen(n - 1))
                        for c in range(DC):
                            hh, hl = tokens(k.h_hi, c, g), tokens(k.h_lo, c, g)
                            nc.tensor.matmul(ps[s % 2][:, :], w_lo[:, c, rows], hh, start=(c == 0), stop=False)
                            nc.tensor.matmul(ps[s % 2][:, :], w_hi[:, c, rows], hl, start=False, stop=False)
                            last = nc.tensor.matmul(ps[s % 2][:, :], w_hi[:, c, rows], hh, start=False,
                                                    stop=(c == DC - 1))
                        last.then_inc(ready, 1)

                def back(n, s, g):
                    pe.wait_ge(s_lo, seen(n + 1))
                    if s == 0:
                        pe.wait_ge(s_ysb, seen(g))
                    for m in range(DC):
                        cols = slice(m * P, (m + 1) * P)
                        nc.tensor.matmul(psY[:, m, :], k.wd_lo[:, s, cols], a_hi[s % 2][:, :], start=(s == 0),
                                         stop=False)
                        nc.tensor.matmul(psY[:, m, :], k.wd_hi[:, s, cols], a_lo[s % 2][:, :], start=False, stop=False)
                        last = nc.tensor.matmul(psY[:, m, :], k.wd_hi[:, s, cols], a_hi[s % 2][:, :], start=False,
                                                stop=(s == LAST))
                    last.then_inc(s_down, 1)

                def transposed(g, half):
                    pe.wait_ge(s_ysb, seen(g + 1))
                    pe.wait_ge(s_out, seen(2 * g + half))
                    for t in range(2):
                        for m in range(DC):
                            tok = (2 * half + t) * P
                            last = nc.tensor.transpose(psT[:, t, m * P:(m + 1) * P], yT[:, m, tok:tok + P],
                                                       k.ident[:, :])
                    last.then_inc(s_T, 1)

                def turn(g, before):
                    for s in range(NCH):
                        front(g, s)
                        if s > 0:
                            back(g * NCH + s - 1, s - 1, g)
                        elif before:
                            back(g * NCH - 1, LAST, g)
                        if before and s in (1, 2):
                            transposed(g - 1, s - 1)

                turn(0, False)
                with pe.Fori(1, NG) as g:
                    turn(g, True)
                back(NG * NCH - 1, LAST, NG - 1)
                for half in range(2):
                    transposed(NG - 1, half)

            @block.scalar
            def _(act):
                nc.scalar.preload_act_table(ACT.Silu)
                credit(act, s_silu, s_ysb)

                def silu(n, s):
                    act.wait_ge(s_gate, seen(n + 1))
                    if not (isinstance(n, int) and n < 2):
                        act.wait_ge(s_lo, seen(n - 1))
                    nc.scalar.activation(a[s % 2][:, :], psG[s % 2][:, :], ACT.Silu).then_inc(s_silu, 1)

                def high(n, s):
                    act.wait_ge(s_a, seen(n + 1))
                    if not (isinstance(n, int) and n < 2):
                        act.wait_ge(s_down, n - 1)
                    nc.scalar.activation(a_hi[s % 2][:, :], a[s % 2][:, :], ACT.Copy).then_inc(s_hi, 1)

                def sums_out(g):
                    act.wait_ge(s_down, (g + 1) * NCH)
                    if not isinstance(g, int) or g > 0:
                        act.wait_ge(s_T, 2 * g)
                    nc.scalar.activation(yT[:, :, :], psY[:, :, :], ACT.Copy).then_inc(s_ysb, 1)

                def turn(g, before):
                    for s in range(NCH):
                        n = g * NCH + s
                        silu(n, s)
                        if before and s == 0:
                            sums_out(g - 1)
                        high(n, s)

                turn(0, False)
                with act.Fori(1, NG) as g:
                    turn(g, True)
                sums_out(NG - 1)

            @block.vector
            def _(dve):
                credit(dve, s_t, s_a, s_lo, s_out)

                def middle(g, s):
                    n = g * NCH + s
                    dve.wait_ge(s_silu, seen(n + 1))
                    dve.wait_ge(s_up, n + 1)
                    nc.vector.tensor_tensor(a[s % 2][:, :], psU[s % 2][:, :], a[s % 2][:, :], ALU.mult).then_inc(s_t, 1)
                    dve.wait_ge(s_t, seen(n + 1))
                    dve.wait_ge(s_cw[s % 2], 32 * (g * (NCH // 2) + s // 2 + 1))
                    nc.vector.tensor_tensor(a[s % 2][:, :], cw[s % 2][:, :], a[s % 2][:, :], ALU.mult).then_inc(s_a, 1)
                    dve.wait_ge(s_hi, n + 1)
                    nc.vector.tensor_tensor(a_lo[s % 2][:, :], a[s % 2][:, :], a_hi[s % 2][:, :].bitcast(F32),
                                            ALU.subtract).then_inc(s_lo, 1)

                def output(g, half):
                    dve.wait_ge(s_T, 2 * g + half + 1)
                    dve.wait_ge(s_res, 16 * g + 16)
                    rows = res[:, 2 * half:2 * half + 2, :]
                    nc.vector.tensor_tensor(rows, psT[:, :, :], rows, ALU.add).then_inc(s_out, 1)

                def turn(g, before):
                    for s in range(NCH):
                        middle(g, s)
                        if before and s in (1, 2):
                            output(g - 1, s - 1)

                turn(0, False)
                with dve.Fori(1, NG) as g:
                    turn(g, True)
                for half in range(2):
                    output(NG - 1, half)


class Kept:
    pass


def build(nc, x, ctx_in, Wq, Wkv, Wout, w_gate, g_gate, w_down, g_down, gate_w, e_gate, e_up, e_down, out):
    k = Kept()
    with ExitStack() as ctx:
        b = Bufs(nc, ctx)
        k.ident = b.sb("ident", [P, P])
        k.x = b.sb("x_tok", [P, NT, D])
        k.w_stage = [b.sb(f"w_stage{n}", [P, 2, 2 * P]) for n in range(W_RING)]
        k.w_loaded = [b.sem(f"w_loaded{n}") for n in range(W_RING)]
        k.gw = b.sb("gw", [E, D])
        k.gw_loaded = b.sem("gw_loaded")
        k.gate_w, k.expert_w = gate_w, (e_gate, e_up, e_down)
        k.mv = b.sb("x_mv", [P, NT, 2])
        k.minus_half = b.sb("minus_half", [P, NT])
        k.x_loaded = [b.sem(f"x_loaded{n}") for n in range(2)]
        k.ctx_loaded = b.sem("ctx_loaded")
        k.bit_loaded = b.sem("bit_loaded")
        k.x2_spilled = b.sem("x2_spilled")
        k.stored = b.sem("stored")
        k.last_stored = b.sem("last_stored")
        with ExitStack() as xctx:
            xb = Bufs(nc, xctx)
            k.identb = xb.sb("identb", [P, P], BF16)
            k.xstats = xb.sb("x_stats", [P, NT, 6])
            k.ones = xb.sb("ones", [P, P])
            k.wg_nat = xb.sb("wg_nat", [P, 2 * INNER // P, D])
            k.wd_nat = xb.sb("wd_nat", [P, DC, INNER])
            k.g_in = xb.sb("g_in", [P, D])
            k.g_hid = xb.sb("g_hid", [P, INNER])
            k.bit_weights = (w_gate, w_down, g_gate, g_down)
            k.wgq = xb.sb("wgq", [P, 2 * INNER // P, D], BF16)
            k.wdq = xb.sb("wdq", [P, DC, INNER], BF16)
            k.wmean = xb.sb("wmean", [P, 2])
            with ExitStack() as actx:
                a = Bufs(nc, actx)
                k.ctx = a.sb("ctx_tok", [P, NT, L])
                k.causal = a.sb("causal", [P, HPC, S], BF16)
                k.headmask = a.sb("headmask", [P, HPC])
                k.row_mv = a.sb("row_mv", [P, NT, 2])
                k.row_veps = a.sb("row_veps", [P, NT])
                k.row_rstd = a.sb("row_rstd", [P, NT])
                k.row_stats_ready, k.row_mv_ready, k.row_veps_ready, k.row_rstd_ready = (
                    a.sem("row_" + n) for n in ("statd", "mvd", "vepsd", "rstdd"))
                k.vmask = a.sb("vmask", [P, NH // 2, 2, HD])
                k.vmask2 = k.vmask[:, :, :, :].rearrange("p a b c -> p (a b c)").unsqueeze(1).to_broadcast([P, 2, D])
                k.wqT_hi, k.wqT_lo = (a.sb(f"wqT_{p}", [P, DC, D], F32R) for p in ("hi", "lo"))
                k.woT_hi, k.woT_lo = (a.sb(f"woT_{p}", [P, DC, D], F32R) for p in ("hi", "lo"))
                k.wkvT_hi, k.wkvT_lo = (a.sb(f"wkvT_{p}", [L, 2 * D], F32R) for p in ("hi", "lo"))
                setup_stage(nc, k, Wq, Wkv, Wout, x, ctx_in)
                attention_stage(nc, k)
            with ExitStack() as bctx:
                a = Bufs(nc, bctx)
                k.wgT = a.sb("wgT", [P, DC, 2 * INNER], BF16)
                k.wdT = a.sb("wdT", [P, IC, D], BF16)
                k.xg = a.sb("xg_all", [P, NT, D])
                k.dq = a.sb("dq_all", [P, NT])
                k.rscale = a.sb("rscale_all", [P, NT])
                k.in_mv = a.sb("in_mv", [P, NT, 2])
                k.in_norm = a.sb("in_norm", [P, NT])
                k.top = a.sb("in_top", [P, 3, NT])
                k.scale_step = a.sem("scale_step")
                k.xg_ready = a.sem("xg_ready")
                k.late_xg_ready = a.sem("late_xg_ready")
                quantise_stage(nc, k)
                bitlinear_stage(nc, k)
        k.out_v = out.rearrange("b s d -> (b s) d").rearrange("(n p) d -> p n d", p=P)
        k.x2_dram = nc.dram_tensor("x2_spill", [P, NT, D], F32, kind="Internal").ap()
        k.h_hi, k.h_lo = (b.sb(f"h3T_{p}", [P, DC, T], F32R) for p in ("hi", "lo"))
        k.wg_hi, k.wg_lo, k.wu_hi, k.wu_lo = (b.sb(n, [P, DC, E * FE], F32R) for n in (
            "wg_hi", "wg_lo", "wu_hi", "wu_lo"))
        k.wd_hi, k.wd_lo = (b.sb(n, [P, NCH, D], F32R) for n in ("wd_hi", "wd_lo"))
        k.cw_stored = [b.sem(f"cw_stored{half}") for half in range(2)]
        k.cw_dram = nc.dram_tensor("cw_spill", [E, T], F32, kind="Internal").ap()
        route_stage(nc, k)
        experts_stage(nc, k)


_INS = ["x", "ctx_512", "L0_xattn_Wq", "L0_xattn_Wkv_expand", "L0_xattn_Wout", "L0_attn_w_gate", "L0_attn_g_gate",
        "L0_attn_w_down", "L0_attn_g_down", "L0_ffn_gate_w", "L0_ffn_w_gate", "L0_ffn_w_up", "L0_ffn_w_down"]


def kernel(**inputs):
    import numpy as _np
    import concourse.bacc as _bacc
    from concourse import mybir as _mybir
    from concourse.bass_utils import run_bass_kernel_spmd as _run

    nc = _bacc.Bacc("TRN2", target_bir_lowering=False, num_devices=1)
    arrays, args = {}, []
    for name in _INS:
        a = _np.ascontiguousarray(inputs[name])
        arrays[f"in_{name}_dram"] = a
        args.append(nc.dram_tensor(f"in_{name}_dram", a.shape, _mybir.dt.from_np(a.dtype), kind="ExternalInput").ap())
    args.append(nc.dram_tensor("out_0_dram", (B, S, D), _mybir.dt.float32, kind="ExternalOutput").ap())
    build(nc, *args)
    r = _run(nc, [arrays], core_ids=[0])
    return r.results[0]["out_0_dram"]
```
